# Optimizing a Trainium2 kernel written in Bass

```python
import numpy as np
import jax
import jax.numpy as jnp

def _softmax(x, axis=-1):
    return jax.nn.softmax(x, axis=axis)

def _gelu(x):
    return jax.nn.gelu(x, approximate=True)

def _silu(x):
    return jax.nn.silu(x)

def _sigmoid(x):
    return jax.nn.sigmoid(x)

def _layernorm(x, axis=-1, eps=1e-05):
    m = jnp.mean(x, axis=axis, keepdims=True)
    v = jnp.var(x, axis=axis, keepdims=True)
    return (x - m) / jnp.sqrt(v + eps)

def _scatter_add(tgt, idx, src, axis=0):
    return tgt.at[idx].add(src)

def _segment_sum(src, seg, n):
    return jax.ops.segment_sum(src, seg, n)
kernel_name = 'mk_seq_preln_d2_jaxref_r8_5ddeb3'

def setup_inputs(seed: int=0):
    np.random.seed(seed)
    _w = jnp.asarray

    def _L0_attn_setup():
        import jax, jax.numpy as jnp
        import numpy as np
        CHUNK = 32

        def l2norm(x):
            return x * jax.lax.rsqrt(jnp.sum(x * x, -1, keepdims=True) + 1e-06)

        def causal_dwconv(x, w):
            k = w.shape[-1]
            xt = jnp.transpose(x, (0, 2, 1))
            xt = jnp.pad(xt, ((0, 0), (0, 0), (k - 1, 0)))
            y = jax.lax.conv_general_dilated(xt, w, (1,), 'VALID', dimension_numbers=('NCH', 'OIH', 'NCH'), feature_group_count=xt.shape[1])
            return jnp.transpose(y, (0, 2, 1))

        def delta_rule_chunkwise(q, k, v, beta):
            b, h, L, dk = q.shape
            dv = v.shape[-1]
            n = L // CHUNK
            q = l2norm(q)
            k = l2norm(k)
            v = v * beta[..., None]
            kb = k * beta[..., None]
            resh = lambda t: t.reshape(b, h, n, CHUNK, t.shape[-1])
            q, k, v, kb = (resh(t) for t in (q, k, v, kb))
            strict = jnp.tril(jnp.ones((CHUNK, CHUNK), bool), -1)
            A = jnp.where(strict, -(kb @ jnp.swapaxes(k, -1, -2)), 0.0)
            eye = jnp.eye(CHUNK, dtype=A.dtype)
            T = jax.scipy.linalg.solve_triangular(eye - A, jnp.broadcast_to(eye, A.shape), lower=True)
            u = T @ v
            w = T @ kb
            incl = jnp.tril(jnp.ones((CHUNK, CHUNK), bool))

            def step(S, xs):
                q_i, k_i, u_i, w_i = xs
                attn = jnp.where(incl, q_i @ jnp.swapaxes(k_i, -1, -2), 0.0)
                u_hat = u_i - w_i @ S
                o_i = q_i @ S + attn @ u_hat
                return (S + jnp.swapaxes(k_i, -1, -2) @ u_hat, o_i)
            xs = tuple((jnp.moveaxis(t, 2, 0) for t in (q, k, u, w)))
            S0 = jnp.zeros((b, h, dk, dv), q.dtype)
            S, o = jax.lax.scan(step, S0, xs)
            o = jnp.moveaxis(o, 0, 2).reshape(b, h, L, dv)
            return (o, S)

        def branch_stats(x):
            m = jnp.mean(x, -1, keepdims=True)
            s = jnp.std(x, -1, keepdims=True, ddof=1)
            a = jnp.mean(jnp.abs(x), -1, keepdims=True)
            l = jnp.sqrt(jnp.sum(x * x, -1, keepdims=True))
            return jnp.concatenate([m, s, a, l], -1)
        key = jax.random.key(seed)
        B, L, D, H = (2, 256, 128, 4)
        dk = dv = D // H
        S = 6
        ks = iter(jax.random.split(key, 32))
        nrm = lambda shape, s=0.02: jax.random.normal(next(ks), shape, jnp.float32) * s

        def fir(kw):
            base = jnp.zeros((H * dv, 1, kw), jnp.float32).at[:, 0, -1].set(1.0)
            return base + nrm((H * dv, 1, kw))
        gate_in_dim = D + S * 4 * H
        hgd = D * 2 // 2
        b2 = np.zeros(H * S, np.float32)
        for h in range(H):
            b2[h * S + S - 1] = 2.0
        return {'hidden_states': jax.random.normal(next(ks), (B, L, D), jnp.float32), 'q_w': nrm((D, D)), 'k_w': nrm((D, D)), 'v_w': nrm((D, D)), 'b_w': nrm((D, H)), 'qc_w': nrm((D, 1, 4), 0.3), 'kc_w': nrm((D, 1, 4), 0.3), 'vc_w': nrm((D, 1, 4), 0.3), 'fir_w1': fir(1), 'fir_w3': fir(3), 'fir_w7': fir(7), 'fir_w31': fir(31), 'mlp_w1': nrm((gate_in_dim, hgd)), 'mlp_b1': jnp.zeros((hgd,), jnp.float32), 'mlp_w2': nrm((hgd, H * S)), 'mlp_b2': jnp.asarray(b2), 'gate_log_temp': jnp.zeros((H,), jnp.float32), 'onorm_w': jnp.ones((dv,), jnp.float32), 'o_w': nrm((D, D))}
    _L0_attn_in = _L0_attn_setup()

    def _L0_ffn_setup():
        import jax, jax.numpy as jnp
        import numpy as np
        TOP_K = 2
        NUM_EXPERTS = 8
        B, T, H, F = (4, 256, 128, 512)
        key = jax.random.key(seed)
        ks = jax.random.split(key, 6)
        s_in = 1.0 / np.sqrt(H)
        s_ff = 1.0 / np.sqrt(F)
        return {'x': jax.random.normal(ks[0], (B, T, H), dtype=jnp.float32), 'router_w': jax.random.normal(ks[1], (NUM_EXPERTS, H), dtype=jnp.float32) * s_in, 'router_b': jax.random.normal(ks[2], (NUM_EXPERTS,), dtype=jnp.float32) * 0.01, 'gate_w': jax.random.normal(ks[3], (NUM_EXPERTS, F, H), dtype=jnp.float32) * s_in, 'up_w': jax.random.normal(ks[4], (NUM_EXPERTS, F, H), dtype=jnp.float32) * s_in, 'down_w': jax.random.normal(ks[5], (NUM_EXPERTS, H, F), dtype=jnp.float32) * s_ff}
    _L0_ffn_in = _L0_ffn_setup()

    def _L1_attn_setup():
        import jax, jax.numpy as jnp
        import numpy as np
        B, L, E, H = (2, 256, 128, 16)
        HD = E // H
        THETA = 10000.0

        def _rope_tables(seq_len, dim, dtype):
            inv_freq = 1.0 / THETA ** (jnp.arange(0, dim, 2, dtype=jnp.float32) / dim)
            freqs = jnp.arange(seq_len, dtype=jnp.float32)[:, None] * inv_freq[None, :]
            freqs = jnp.repeat(freqs, 2, axis=-1)
            return (jnp.cos(freqs).astype(dtype), jnp.sin(freqs).astype(dtype))

        def _rotate_half(x):
            x2 = x.reshape(*x.shape[:-1], -1, 2)
            x2 = jnp.stack([-x2[..., 1], x2[..., 0]], axis=-1)
            return x2.reshape(x.shape)

        def _apply_rope(x, cos, sin):
            return x * cos[None, None] + _rotate_half(x) * sin[None, None]
        key = jax.random.key(seed)
        ks = jax.random.split(key, 9)
        s = 1.0 / np.sqrt(E)
        return {'x': jax.random.normal(ks[0], (B, L, E), jnp.float32), 'Wq': jax.random.normal(ks[1], (E, E), jnp.float32) * s, 'bq': jax.random.normal(ks[2], (E,), jnp.float32) * 0.01, 'Wk': jax.random.normal(ks[3], (E, E), jnp.float32) * s, 'bk': jax.random.normal(ks[4], (E,), jnp.float32) * 0.01, 'Wv': jax.random.normal(ks[5], (E, E), jnp.float32) * s, 'bv': jax.random.normal(ks[6], (E,), jnp.float32) * 0.01, 'Wo': jax.random.normal(ks[7], (E, E), jnp.float32) * s, 'bo': jax.random.normal(ks[8], (E,), jnp.float32) * 0.01}
    _L1_attn_in = _L1_attn_setup()

    def _L1_ffn_setup():
        import jax, jax.numpy as jnp
        import numpy as np
        LN_EPS = 1e-12
        key = jax.random.key(seed)
        ks = jax.random.split(key, 8)
        B, S, H, I, E = (4, 256, 128, 512, 8)
        sH = 1.0 / np.sqrt(H)
        sI = 1.0 / np.sqrt(I)
        return {'hidden_states': jax.random.normal(ks[0], (B, S, H), dtype=jnp.float32), 'Wr': jax.random.uniform(ks[1], (E, H), jnp.float32, -sH, sH), 'W1': jax.random.uniform(ks[2], (E, H, I), jnp.float32, -sH, sH), 'b1': jax.random.uniform(ks[3], (E, I), jnp.float32, -sH, sH), 'Wo': jax.random.uniform(ks[4], (I, H), jnp.float32, -sI, sI), 'bo': jax.random.uniform(ks[5], (H,), jnp.float32, -sI, sI), 'gamma': jnp.ones((H,), jnp.float32), 'beta': jnp.zeros((H,), jnp.float32)}
    _L1_ffn_in = _L1_ffn_setup()
    _d = {'L0_attn_hidden_states': _L0_attn_in['hidden_states'], 'L0_attn_q_w': _L0_attn_in['q_w'], 'L0_attn_k_w': _L0_attn_in['k_w'], 'L0_attn_v_w': _L0_attn_in['v_w'], 'L0_attn_b_w': _L0_attn_in['b_w'], 'L0_attn_qc_w': _L0_attn_in['qc_w'], 'L0_attn_kc_w': _L0_attn_in['kc_w'], 'L0_attn_vc_w': _L0_attn_in['vc_w'], 'L0_attn_fir_w1': _L0_attn_in['fir_w1'], 'L0_attn_fir_w3': _L0_attn_in['fir_w3'], 'L0_attn_fir_w7': _L0_attn_in['fir_w7'], 'L0_attn_fir_w31': _L0_attn_in['fir_w31'], 'L0_attn_mlp_w1': _L0_attn_in['mlp_w1'], 'L0_attn_mlp_b1': _L0_attn_in['mlp_b1'], 'L0_attn_mlp_w2': _L0_attn_in['mlp_w2'], 'L0_attn_mlp_b2': _L0_attn_in['mlp_b2'], 'L0_attn_gate_log_temp': _L0_attn_in['gate_log_temp'], 'L0_attn_onorm_w': _L0_attn_in['onorm_w'], 'L0_attn_o_w': _L0_attn_in['o_w'], 'L0_ffn_router_w': _L0_ffn_in['router_w'], 'L0_ffn_router_b': _L0_ffn_in['router_b'], 'L0_ffn_gate_w': _L0_ffn_in['gate_w'], 'L0_ffn_up_w': _L0_ffn_in['up_w'], 'L0_ffn_down_w': _L0_ffn_in['down_w'], 'L1_attn_Wq': _L1_attn_in['Wq'], 'L1_attn_bq': _L1_attn_in['bq'], 'L1_attn_Wk': _L1_attn_in['Wk'], 'L1_attn_bk': _L1_attn_in['bk'], 'L1_attn_Wv': _L1_attn_in['Wv'], 'L1_attn_bv': _L1_attn_in['bv'], 'L1_attn_Wo': _L1_attn_in['Wo'], 'L1_attn_bo': _L1_attn_in['bo'], 'L1_ffn_Wr': _L1_ffn_in['Wr'], 'L1_ffn_W1': _L1_ffn_in['W1'], 'L1_ffn_b1': _L1_ffn_in['b1'], 'L1_ffn_Wo': _L1_ffn_in['Wo'], 'L1_ffn_bo': _L1_ffn_in['bo'], 'L1_ffn_gamma': _L1_ffn_in['gamma'], 'L1_ffn_beta': _L1_ffn_in['beta']}
    _x0 = _d['L0_attn_hidden_states']
    _d['L0_attn_hidden_states'] = jax.random.normal(jax.random.fold_in(jax.random.key(seed), 1), (2, 1024, 128), dtype=_x0.dtype)
    del _x0
    return _d

def reference(L0_attn_hidden_states, L0_attn_q_w, L0_attn_k_w, L0_attn_v_w, L0_attn_b_w, L0_attn_qc_w, L0_attn_kc_w, L0_attn_vc_w, L0_attn_fir_w1, L0_attn_fir_w3, L0_attn_fir_w7, L0_attn_fir_w31, L0_attn_mlp_w1, L0_attn_mlp_b1, L0_attn_mlp_w2, L0_attn_mlp_b2, L0_attn_gate_log_temp, L0_attn_onorm_w, L0_attn_o_w, L0_ffn_router_w, L0_ffn_router_b, L0_ffn_gate_w, L0_ffn_up_w, L0_ffn_down_w, L1_attn_Wq, L1_attn_bq, L1_attn_Wk, L1_attn_bk, L1_attn_Wv, L1_attn_bv, L1_attn_Wo, L1_attn_bo, L1_ffn_Wr, L1_ffn_W1, L1_ffn_b1, L1_ffn_Wo, L1_ffn_bo, L1_ffn_gamma, L1_ffn_beta):

    def _L0_attn_ref(hidden_states, q_w, k_w, v_w, b_w, qc_w, kc_w, vc_w, fir_w1, fir_w3, fir_w7, fir_w31, mlp_w1, mlp_b1, mlp_w2, mlp_b2, gate_log_temp, onorm_w, o_w):
        import jax, jax.numpy as jnp
        import numpy as np
        CHUNK = 32

        def l2norm(x):
            return x * jax.lax.rsqrt(jnp.sum(x * x, -1, keepdims=True) + 1e-06)

        def causal_dwconv(x, w):
            k = w.shape[-1]
            xt = jnp.transpose(x, (0, 2, 1))
            xt = jnp.pad(xt, ((0, 0), (0, 0), (k - 1, 0)))
            y = jax.lax.conv_general_dilated(xt, w, (1,), 'VALID', dimension_numbers=('NCH', 'OIH', 'NCH'), feature_group_count=xt.shape[1])
            return jnp.transpose(y, (0, 2, 1))

        def delta_rule_chunkwise(q, k, v, beta):
            b, h, L, dk = q.shape
            dv = v.shape[-1]
            n = L // CHUNK
            q = l2norm(q)
            k = l2norm(k)
            v = v * beta[..., None]
            kb = k * beta[..., None]
            resh = lambda t: t.reshape(b, h, n, CHUNK, t.shape[-1])
            q, k, v, kb = (resh(t) for t in (q, k, v, kb))
            strict = jnp.tril(jnp.ones((CHUNK, CHUNK), bool), -1)
            A = jnp.where(strict, -(kb @ jnp.swapaxes(k, -1, -2)), 0.0)
            eye = jnp.eye(CHUNK, dtype=A.dtype)
            T = jax.scipy.linalg.solve_triangular(eye - A, jnp.broadcast_to(eye, A.shape), lower=True)
            u = T @ v
            w = T @ kb
            incl = jnp.tril(jnp.ones((CHUNK, CHUNK), bool))

            def step(S, xs):
                q_i, k_i, u_i, w_i = xs
                attn = jnp.where(incl, q_i @ jnp.swapaxes(k_i, -1, -2), 0.0)
                u_hat = u_i - w_i @ S
                o_i = q_i @ S + attn @ u_hat
                return (S + jnp.swapaxes(k_i, -1, -2) @ u_hat, o_i)
            xs = tuple((jnp.moveaxis(t, 2, 0) for t in (q, k, u, w)))
            S0 = jnp.zeros((b, h, dk, dv), q.dtype)
            S, o = jax.lax.scan(step, S0, xs)
            o = jnp.moveaxis(o, 0, 2).reshape(b, h, L, dv)
            return (o, S)

        def branch_stats(x):
            m = jnp.mean(x, -1, keepdims=True)
            s = jnp.std(x, -1, keepdims=True, ddof=1)
            a = jnp.mean(jnp.abs(x), -1, keepdims=True)
            l = jnp.sqrt(jnp.sum(x * x, -1, keepdims=True))
            return jnp.concatenate([m, s, a, l], -1)
        B, L, D = hidden_states.shape
        H = gate_log_temp.shape[0]
        dk = q_w.shape[1] // H
        dv = v_w.shape[1] // H
        q = jax.nn.silu(causal_dwconv(hidden_states @ q_w, qc_w))
        k = jax.nn.silu(causal_dwconv(hidden_states @ k_w, kc_w))
        v = jax.nn.silu(causal_dwconv(hidden_states @ v_w, vc_w))
        q = q.reshape(B, L, H, dk)
        k = k.reshape(B, L, H, dk)
        v_direct = v.reshape(B, L, H, dv)
        beta = jax.nn.sigmoid(hidden_states @ b_w)
        delta_out, _ = delta_rule_chunkwise(jnp.transpose(q, (0, 2, 1, 3)), jnp.transpose(k, (0, 2, 1, 3)), jnp.transpose(v_direct, (0, 2, 1, 3)), jnp.transpose(beta, (0, 2, 1)))
        delta_out = jnp.transpose(delta_out, (0, 2, 1, 3))
        v_flat = v_direct.reshape(B, L, H * dv)
        firs = [causal_dwconv(v_flat, w).reshape(B, L, H, dv) for w in (fir_w1, fir_w3, fir_w7, fir_w31)]
        branches = firs + [delta_out, v_direct]
        S = len(branches)
        stats = jnp.concatenate([branch_stats(x) for x in branches], -1)
        gate_in = jnp.concatenate([hidden_states, stats.reshape(B, L, H * S * 4)], -1)
        hgate = jax.nn.gelu(gate_in @ mlp_w1 + mlp_b1, approximate=False)
        logits = (hgate @ mlp_w2 + mlp_b2).reshape(B, L, H, S)
        temp = jax.nn.softplus(gate_log_temp) + 0.5
        weights = jax.nn.softmax(logits / temp[None, None, :, None], axis=-1)
        fused = sum((weights[..., i, None] * br for i, br in enumerate(branches)))
        fused = fused * jax.lax.rsqrt(jnp.mean(fused * fused, -1, keepdims=True) + 1e-05) * onorm_w
        return fused.reshape(B, L, H * dv) @ o_w

    def _L0_ffn_ref(x, router_w, router_b, gate_w, up_w, down_w):
        import jax, jax.numpy as jnp
        import numpy as np
        TOP_K = 2
        NUM_EXPERTS = 8
        B, T, H, F = (4, 256, 128, 512)
        logits = jnp.einsum('bth,eh->bte', x, router_w) + router_b
        topv, topi = jax.lax.top_k(logits, TOP_K)
        gates = jax.nn.softmax(topv, axis=-1)

        def body(acc, inputs):
            e, gw, uw, dw = inputs
            w = jnp.sum(gates * (topi == e), axis=-1)
            h = jax.nn.silu(jnp.einsum('bth,fh->btf', x, gw)) * jnp.einsum('bth,fh->btf', x, uw)
            y = jnp.einsum('btf,hf->bth', h, dw)
            return (acc + y * w[..., None], None)
        init = jnp.zeros_like(x)
        xs = (jnp.arange(NUM_EXPERTS), gate_w, up_w, down_w)
        out, _ = jax.lax.scan(body, init, xs)
        return out

    def _L1_attn_ref(x, Wq, bq, Wk, bk, Wv, bv, Wo, bo):
        import jax, jax.numpy as jnp
        import numpy as np
        B, L, E, H = (2, 256, 128, 16)
        HD = E // H
        THETA = 10000.0

        def _rope_tables(seq_len, dim, dtype):
            inv_freq = 1.0 / THETA ** (jnp.arange(0, dim, 2, dtype=jnp.float32) / dim)
            freqs = jnp.arange(seq_len, dtype=jnp.float32)[:, None] * inv_freq[None, :]
            freqs = jnp.repeat(freqs, 2, axis=-1)
            return (jnp.cos(freqs).astype(dtype), jnp.sin(freqs).astype(dtype))

        def _rotate_half(x):
            x2 = x.reshape(*x.shape[:-1], -1, 2)
            x2 = jnp.stack([-x2[..., 1], x2[..., 0]], axis=-1)
            return x2.reshape(x.shape)

        def _apply_rope(x, cos, sin):
            return x * cos[None, None] + _rotate_half(x) * sin[None, None]
        b, l, e = x.shape
        q = (x @ Wq.T + bq).reshape(b, l, H, HD).transpose(0, 2, 1, 3)
        k = (x @ Wk.T + bk).reshape(b, l, H, HD).transpose(0, 2, 1, 3)
        v = (x @ Wv.T + bv).reshape(b, l, H, HD).transpose(0, 2, 1, 3)
        cos, sin = _rope_tables(l, HD, x.dtype)
        q = _apply_rope(q, cos, sin)
        k = _apply_rope(k, cos, sin)
        scale = 1.0 / np.sqrt(HD)
        scores = jnp.einsum('bhsd,bhed->bhse', q, k) * scale
        attn = jax.nn.softmax(scores, axis=-1)
        out = jnp.einsum('bhse,bhed->bhsd', attn, v)
        out = out.transpose(0, 2, 1, 3).reshape(b, l, e)
        return out @ Wo.T + bo

    def _L1_ffn_ref(hidden_states, Wr, W1, b1, Wo, bo, gamma, beta):
        import jax, jax.numpy as jnp
        import numpy as np
        LN_EPS = 1e-12
        B, S, H = hidden_states.shape
        E = Wr.shape[0]
        x = hidden_states.reshape(-1, H)
        router_logits = x @ Wr.T
        expert_idx = jnp.argmax(jax.nn.softmax(router_logits, axis=-1), axis=-1)
        inter = jnp.zeros((x.shape[0], W1.shape[2]), dtype=x.dtype)
        for e in range(E):
            mask = (expert_idx == e)[:, None].astype(x.dtype)
            inter = inter + mask * jax.nn.gelu(x @ W1[e] + b1[e], approximate=False)
        y = inter @ Wo + bo + x
        mu = jnp.mean(y, axis=-1, keepdims=True)
        var = jnp.mean(jnp.square(y - mu), axis=-1, keepdims=True)
        out = (y - mu) * jax.lax.rsqrt(var + LN_EPS) * gamma + beta
        return out.reshape(B, S, H)
    x = L0_attn_hidden_states
    x = x + _L0_attn_ref(_layernorm(x, axis=-1), L0_attn_q_w, L0_attn_k_w, L0_attn_v_w, L0_attn_b_w, L0_attn_qc_w, L0_attn_kc_w, L0_attn_vc_w, L0_attn_fir_w1, L0_attn_fir_w3, L0_attn_fir_w7, L0_attn_fir_w31, L0_attn_mlp_w1, L0_attn_mlp_b1, L0_attn_mlp_w2, L0_attn_mlp_b2, L0_attn_gate_log_temp, L0_attn_onorm_w, L0_attn_o_w)
    x = x + _L0_ffn_ref(_layernorm(x, axis=-1), L0_ffn_router_w, L0_ffn_router_b, L0_ffn_gate_w, L0_ffn_up_w, L0_ffn_down_w)
    x = x + _L1_attn_ref(_layernorm(x, axis=-1), L1_attn_Wq, L1_attn_bq, L1_attn_Wk, L1_attn_bk, L1_attn_Wv, L1_attn_bv, L1_attn_Wo, L1_attn_bo)
    x = x + _L1_ffn_ref(_layernorm(x, axis=-1), L1_ffn_Wr, L1_ffn_W1, L1_ffn_b1, L1_ffn_Wo, L1_ffn_bo, L1_ffn_gamma, L1_ffn_beta)
    return x

_drawn_inputs = setup_inputs


def setup_inputs(seed=0):
    import zlib

    import numpy as np

    out = dict(_drawn_inputs(seed))
    spreads = {'L0_attn_mlp_b1': (0.0, 0.8),
     'L0_attn_gate_log_temp': (0.0, 0.8),
     'L0_attn_onorm_w': (1.0, 0.2),
     'L1_ffn_gamma': (1.0, 0.2),
     'L1_ffn_beta': (0.0, 0.1)}
    factors = {'L0_attn_b_w': 4.828,
     'L0_attn_fir_w1': 42.233,
     'L0_attn_fir_w3': 33.153,
     'L0_attn_mlp_w1': 8.0,
     'L0_attn_mlp_w2': 8.0,
     'L0_attn_mlp_b2': 2.895,
     'L1_attn_bq': 43.405,
     'L1_attn_bk': 53.44,
     'L1_attn_bv': 4.794,
     'L1_attn_bo': 4.434,
     'L1_ffn_b1': 6.638,
     'L1_ffn_bo': 4.239,
     'L0_attn_fir_w7': 3.235}
    for name, (base, spread) in spreads.items():
        noise = np.random.default_rng([zlib.crc32(name.encode()), seed]).standard_normal(out[name].shape)
        drawn = base * np.exp(spread * noise) if base else spread * noise
        out[name] = jnp.asarray(drawn.astype(out[name].dtype))
    for name, factor in factors.items():
        out[name] = (out[name] * factor).astype(out[name].dtype)
    return out
```

```python
import numpy as np
import concourse.bass as bass
import concourse.mybir as mybir
from concourse.alu_op_type import AluOpType as ALU

F32 = mybir.dt.float32
BF16 = mybir.dt.bfloat16
ACT = mybir.ActivationFunctionType
X = mybir.AxisListType.X

P = 128
B, L, D = 2, 1024, 128
T = B * L
NT = T // P
NTB = L // P
BLK = 512
NB = T // BLK
TPB = BLK // P


class Progress:

    def __init__(self, nc, name):
        self.sem = nc.alloc_semaphore(name)
        self.n = 0

    def done(self, instruction, by=1):
        instruction.then_inc(self.sem, by)
        self.n += by
        return (self, self.n)


class Events:

    def __init__(self, nc, name, engine, credit=0, by=1):
        self.sem, self.credit, self.by = nc.alloc_semaphore(name), credit, by
        if credit:
            engine.sem_inc(self.sem, credit * by)

    def fire(self, instruction):
        return instruction.then_inc(self.sem, self.by)

    def wait(self, engine, k, alone=False):
        engine.wait_ge(self.sem, (k + (1 + self.credit)) * self.by)
        if alone:
            engine.sem_inc(self.unread, 1)


def wait(engine, *marks):
    for mark in marks:
        if mark is not None:
            engine.wait_ge(mark[0].sem, mark[1])


class Arena:

    def __init__(self, nc, words):
        self.t, self.words, self.top = nc.alloc_sbuf_tensor("arena", [P, words], F32), words, 0

    def reset(self):
        self.top = 0

    def take(self, shape, dtype=F32):
        n = int(np.prod(shape[1:]))
        words = n if dtype == F32 else (n + 1) // 2
        ap = self.t[0:shape[0], self.top:self.top + words]
        self.top += words
        assert self.top <= self.words, (self.top, self.words)
        if dtype != F32:
            ap = ap.bitcast(dtype)
        names = "abcde"[:len(shape) - 1]
        if len(names) > 1:
            ap = ap.rearrange("p (" + " ".join(names) + ") -> p " + " ".join(names), **dict(zip(names, shape[1:])))
        return ap


class Core:

    def keep(self, name, shape, dtype=F32):
        self.mem[name] = self.nc.alloc_sbuf_tensor(name, shape, dtype)

    def sb(self, name, shape, dtype=F32):
        self.mem[name] = self.arena.take(shape, dtype)
        return self.mem[name]

    def load(self, name, source, shape, dtype=F32):
        self.loads.done(self.sp.dma_start(self.sb(name, shape, dtype)[:], source), 16)

    def loaded(self, *engines):
        for engine in engines:
            engine.wait_ge(self.loads.sem, self.loads.n)

    def __init__(self, nc):
        self.mem = {}
        Events.unread = nc.alloc_semaphore("s_unread")
        self.loads = Progress(nc, "s_loads")
        self.nc = nc
        self.pe, self.dve, self.act, self.pool, self.sp = nc.tensor, nc.vector, nc.scalar, nc.gpsimd, nc.sync
        self.PE, self.DVE, self.ACT, self.POOL = (Progress(nc, "s_" + n) for n in ("pe", "dve", "act", "pool"))
        self.psum = nc.alloc_psum_tensor("psum", [P, 8, BLK], F32)

    def dve_step(self, instruction):
        m = self.DVE.done(instruction)
        wait(self.dve, m)
        return m

    def act_step(self, instruction):
        m = self.ACT.done(instruction)
        wait(self.act, m)
        return m


def layer_norm(c, x, xn, eps, lead, xnT=None, banks=(6, 7), out_at=None):
    bn, mv, rs, ident = c.mem["bn"], c.mem["mv"], c.mem["rs"], c.mem["ident"]
    wait(c.dve, *lead)
    for t in range(NT):
        last = c.DVE.done(c.dve.bn_stats(bn[:, t, :], x[:, t, :]))
    wait(c.dve, last)
    for t in range(NT):
        last = c.DVE.done(c.dve.bn_aggr(mv[:, t, :], bn[:, t, :]))
    wait(c.dve, last)
    ve = c.DVE.done(c.dve.tensor_scalar(rs[:], mv[:, :, 1], eps, None, ALU.add))
    wait(c.act, ve)
    root = c.ACT.done(c.act.activation(rs[:], rs[:], ACT.Sqrt))
    wait(c.dve, root)
    c.dve_step(c.dve.reciprocal(rs[:], rs[:]))
    marks = []
    for t in range(NT):
        m = c.DVE.done(c.dve.tensor_scalar(xn[:, t, :], x[:, t, :], mv[:, t, 0:1], rs[:, t:t + 1],
                                           ALU.subtract, ALU.mult))
        marks.append(m)
    if xnT is None:
        return marks
    outs = []
    for b in range(NB):
        bank = banks[b % len(banks)]
        wait(c.pe, marks[TPB * b + TPB - 1], outs[b - len(banks)] if b >= len(banks) else None)
        for j in range(TPB):
            m = c.pe.transpose(c.psum[:, bank, j * P:(j + 1) * P], xn[:, TPB * b + j, :], ident[:])
        m = c.PE.done(m)
        wait(c.act, m)
        outs.append(c.ACT.done(c.act.copy(out_at(b), c.psum[:, bank, :])))
    return outs


def ffn0(c, w, x, lead):
    nc, ps = c.nc, c.psum
    NE, F = 8, 512
    FC = F // P
    m = c.mem
    xn, xnT, h, sg, wbuf = m["xn"], m["xnT"], m["f0_h"], m["f0_sg"], m["f0_w"]
    landed = [Events(nc, f"s_f0_landed{k}", c.sp, by=16) for k in range(2)]
    for k in range(2):
        landed[k].fire(c.sp.dma_start(wbuf[:, k, :], w["f0_w"][k]))
    outs = layer_norm(c, x, xn, 1e-5, lead, xnT, out_at=lambda b: xnT[:, b * BLK:(b + 1) * BLK])
    c.loaded(c.pe, c.dve, c.act, c.pool)
    wait(c.pe, *outs)
    lg = ps[:, 2, 0:NT * NE]
    for t in range(NT):
        mm = c.pe.matmul(lg[:, t * NE:(t + 1) * NE], xnT[:, t * P:(t + 1) * P], m["f0_rw"][:], start=True, stop=True)
    gates = route(c, lg, m["f0_rb"], c.PE.done(mm), 2, m["gate"])
    acc = xn
    z = c.DVE.done(c.dve.memset(acc[:], 0.0))
    wait(c.dve, z)
    wait(c.pe, z)
    wait(c.act, z)
    gateup = Events(nc, "s_f0_gateup", c.pe)
    silu = Events(nc, "s_f0_silu", c.act, credit=2)
    prod = Events(nc, "s_f0_prod", c.dve, credit=2)
    down = Events(nc, "s_f0_down", c.pe, credit=2)
    summed = Events(nc, "s_f0_summed", c.dve, credit=2 * TPB)
    trips = NE // 2
    with nc.Fori(0, trips) as i:
        for k in range(2):
            landed[k].wait(c.pe, i)
            for b in range(NB):
                xs = xnT[:, b * BLK:(b + 1) * BLK]
                blk = i * (2 * NB) + (k * NB + b)
                par = b % 2
                for f in range(FC):
                    n = i * (2 * NB * FC) + ((k * NB + b) * FC + f)
                    g, u = ps[:, f % 2, :], ps[:, 2 + f % 2, :]
                    silu.wait(c.pe, n - 2)
                    prod.wait(c.pe, n - 2)
                    c.pe.matmul(g, wbuf[:, k, f * P:(f + 1) * P], xs, start=True, stop=True)
                    gateup.fire(c.pe.matmul(u, wbuf[:, k, F + f * P:F + (f + 1) * P], xs, start=True, stop=True))
                    gateup.wait(c.act, n)
                    prod.wait(c.act, n - 2)
                    silu.fire(c.act.activation(sg[:, f % 2, :], g, ACT.Silu))
                    silu.wait(c.dve, n)
                    if f == 0:
                        down.wait(c.dve, blk - 2)
                    prod.fire(c.dve.tensor_tensor(h[:, par, f, :], sg[:, f % 2, :], u, ALU.mult))
                y = ps[:, 4 + par, :]
                prod.wait(c.pe, n)
                summed.wait(c.pe, blk * TPB - (TPB + 1))
                for j in range(TPB):
                    for f in range(FC):
                        mm = c.pe.matmul(y[:, j * P:(j + 1) * P], h[:, par, f, j * P:(j + 1) * P],
                                         wbuf[:, k, 2 * F + f * P:2 * F + (f + 1) * P], start=f == 0, stop=f == FC - 1)
                down.fire(mm)
                down.wait(c.dve, blk)
                for j in range(TPB):
                    t = b * TPB + j
                    gate = gates[:, t, bass.ds(i * 2 + k, 1)]
                    summed.fire(c.dve.scalar_tensor_tensor(acc[:, t, :], y[:, j * P:(j + 1) * P], gate,
                                                             acc[:, t, :], ALU.mult, ALU.add))
            down.wait(c.sp, i * (2 * NB) + (k * NB + NB - 1))
            nxt = w["f0_w"][bass.ds(i * 2 + 2 + k, 1)].rearrange("o p f -> (o p) f")
            landed[k].fire(c.sp.dma_start(wbuf[:, k, :], nxt))
    summed.wait(c.dve, NE * NT - 1)
    for k in range(2):
        landed[k].wait(c.sp, trips)
    return c.DVE.done(c.dve.tensor_tensor(x[:], x[:], acc[:], ALU.add))


def route(c, lg, bias, ready, top, out):
    s, dve = c.mem, c.dve
    NE = 8
    lo, cmp, eq, rank = s["lo"], s["cmp"], s["eq"], s["rank"]
    wait(dve, ready)
    lgv = lg.rearrange("p (t e) -> p t e", e=NE)
    if bias is not None:
        c.dve_step(dve.tensor_tensor(lo[:], lgv, bias[:].unsqueeze(1).broadcast_to([P, NT, NE]), ALU.add))
    else:
        c.dve_step(dve.tensor_copy(lo[:], lgv))
    mine = lo[:].unsqueeze(3).broadcast_to([P, NT, NE, NE])
    other = lo[:].unsqueeze(2).broadcast_to([P, NT, NE, NE])
    c.DVE.done(dve.tensor_tensor(cmp[:], other, mine, ALU.is_gt))
    c.dve_step(dve.tensor_tensor(eq[:], other, mine, ALU.is_equal))
    lower = s["lower"][:].unsqueeze(1).broadcast_to([P, NT, NE * NE])
    eqf = eq[:].rearrange("p t a b -> p t (a b)")
    c.dve_step(dve.tensor_tensor(eqf, eqf, lower, ALU.mult))
    c.dve_step(dve.tensor_tensor(cmp[:], cmp[:], eq[:], ALU.add))
    c.dve_step(dve.tensor_reduce(rank[:], cmp[:], X, ALU.add))
    if top == 1:
        c.dve_step(dve.tensor_scalar(out[:], rank[:], 0.0, None, ALU.is_equal))
        return out
    first, second, l1, l2, g1, g2 = (s[n] for n in ("first", "second", "l1", "l2", "g1", "g2"))
    c.DVE.done(dve.tensor_scalar(first[:], rank[:], 0.0, None, ALU.is_equal))
    c.dve_step(dve.tensor_scalar(second[:], rank[:], 1.0, None, ALU.is_equal))
    c.DVE.done(dve.tensor_tensor(out[:], second[:], lo[:], ALU.mult))
    c.dve_step(dve.tensor_reduce(l1[:], lo[:], X, ALU.max))
    c.dve_step(dve.tensor_reduce(l2[:], out[:], X, ALU.add))
    d = c.dve_step(dve.tensor_tensor(l2[:], l2[:], l1[:], ALU.subtract))
    wait(c.act, d)
    m = c.ACT.done(c.act.activation(l2[:], l2[:], ACT.Exp))
    wait(dve, m)
    c.dve_step(dve.tensor_scalar(g1[:], l2[:], 1.0, None, ALU.add))
    c.dve_step(dve.reciprocal(g1[:], g1[:]))
    c.dve_step(dve.tensor_tensor(g2[:], g1[:], l2[:], ALU.mult))
    c.DVE.done(dve.tensor_tensor(first[:], first[:], g1[:].unsqueeze(2).broadcast_to([P, NT, NE]), ALU.mult))
    c.dve_step(dve.tensor_tensor(second[:], second[:], g2[:].unsqueeze(2).broadcast_to([P, NT, NE]), ALU.mult))
    c.dve_step(dve.tensor_tensor(out[:], first[:], second[:], ALU.add))
    return out


def common_memory(c, w):
    for n, shape in (("x", [P, NT, D]), ("xn", [P, NT, D]), ("xnT", [P, T + 8]), ("bn", [P, NT, 6]),
                     ("mv", [P, NT, 2]), ("rs", [P, NT]), ("ident", [P, P])):
        c.keep(n, shape)
    c.loads.done(c.sp.dma_start(c.mem["ident"][:], w["ident"]), 16)
    c.arena = Arena(c.nc, 46000)


def route_memory(c, w):
    c.load("lower", w["lower"].partition_broadcast(P), [P, 64])
    for n, shape in (("lo", [P, NT, 8]), ("cmp", [P, NT, 8, 8]), ("eq", [P, NT, 8, 8]), ("rank", [P, NT, 8]),
                     ("first", [P, NT, 8]), ("second", [P, NT, 8]), ("gate", [P, NT, 8]),
                     ("l1", [P, NT]), ("l2", [P, NT]), ("g1", [P, NT]), ("g2", [P, NT])):
        c.sb(n, shape)


def ffn0_memory(c, w):
    route_memory(c, w)
    c.load("f0_rw", w["f0_rw"], [D, 8])
    c.load("f0_rb", w["f0_rb"].partition_broadcast(P), [P, 8])
    c.sb("f0_h", [P, 2, 4, BLK]); c.sb("f0_sg", [P, 2, BLK]); c.sb("f0_w", [P, 2, 1536])


def layout(inputs):
    a = {k: np.asarray(v) for k, v in inputs.items()}
    out = {"ident": np.eye(P, dtype=np.float32)}
    out["lower"] = np.tril(np.ones((8, 8), np.float32), -1).reshape(64)
    gw = a["L0_ffn_gate_w"].transpose(0, 2, 1)
    uw = a["L0_ffn_up_w"].transpose(0, 2, 1)
    dw = a["L0_ffn_down_w"].transpose(0, 2, 1).reshape(8, 4, P, D).transpose(0, 2, 1, 3).reshape(8, P, 512)
    f0 = np.concatenate([gw, uw, dw], axis=2)
    out["f0_w"] = np.concatenate([f0, f0[:2]], axis=0)
    out["f0_rw"] = a["L0_ffn_router_w"].T
    out["f0_rb"] = a["L0_ffn_router_b"]
    attn1_layout(a, out)
    attn0_layout(a, out)
    ffn1_layout(a, out)
    return {k: np.ascontiguousarray(v) for k, v in out.items()}


NH, HD = 16, 8
NG = 4
HG = NH // NG
KR = 9 * HD
KA = KR + 3
QH = L // BLK


def attn1_memory(c, w):
    for n in ("wq", "wqs", "wk", "wks", "wv", "wo"):
        c.load("a1_" + n, w["a1_" + n], [D, D])
    c.load("a1_bcol", w["a1_bcol"], [D, 4])
    c.load("a1_bv", w["a1_bv"].partition_broadcast(P), [P, D])
    c.load("a1_bo", w["a1_bo"].partition_broadcast(P), [P, D])
    c.load("a1_cos", w["a1_cos"], [D, L]); c.load("a1_sin", w["a1_sin"], [D, L])
    c.sb("identb", [P, P], BF16)
    c.sb("a1_t", [P, 2, 2, BLK])
    c.sb("a1_part", [P, 2, 3, BLK], BF16)
    c.sb("a1_v", [P, NT, D])
    c.sb("a1_q", [P, NG, HG, L], BF16); c.sb("a1_k", [P, NG, HG, L], BF16)
    c.sb("a1_va", [P, NTB, NH, 32])
    c.sb("a1_p", [P, 2 * HG, BLK])
    c.sb("a1_o", [P, B * NG * QH, BLK])
    c.sb("a1_mx", [P, 2, HG * 4]); c.sb("a1_mr", [P, HG * 4]); c.sb("a1_ms", [P, 3, HG * 4], BF16)
    c.sb("a1_mt", [3 * HG * 4, P], BF16)
    c.sb("a1_rd", [P, 2, 4, HG])


def attn1(c, w, x, lead):
    nc, ps, m = c.nc, c.psum, c.mem
    pe, dve, act, pool, sp = c.pe, c.dve, c.act, c.pool, c.sp
    xn, xnT = m["xn"], m["xnT"]
    scr_q = nc.dram_tensor("scr_q", [NH, 9, HD, T], BF16, kind="Internal").ap()
    scr_k = nc.dram_tensor("scr_k", [NH, 9, HD, T], BF16, kind="Internal").ap()
    scr_m = nc.dram_tensor("scr_m", [2, 3, HG, 4, P], BF16, kind="Internal").ap()
    outs = layer_norm(c, x, xn, 1e-5, lead, xnT, out_at=lambda b: xnT[:, b * BLK:(b + 1) * BLK])
    c.loaded(c.pe, c.dve, c.act, c.pool)
    va, v = m["a1_va"], m["a1_v"]
    c.POOL.done(pool.memset(va[:], 0.0))
    wait(pool, (c.POOL, c.POOL.n))
    ones_v = c.POOL.done(pool.memset(va[:, :, :, HD:HD + 1], 1.0))
    ones_k = c.DVE.done(dve.memset(m["a1_k"][64:96, :, :, :], 1.0))
    idb = c.DVE.done(dve.tensor_copy(m["identb"][:], m["ident"][:]))
    stored = {}
    s_st = [Progress(nc, f"s_a1_st{k}") for k in range(2)]
    used = {}
    n = 0
    for b in range(NB):
        xs = xnT[:, b * BLK:(b + 1) * BLK]
        lpos = (b * BLK) % L
        wait(pe, outs[b])
        for what, (w1, w2, b1, scr) in enumerate((("a1_wq", "a1_wqs", 0, scr_q), ("a1_wk", "a1_wks", 2, scr_k))):
            k = n % 2
            bank = 2 * k
            wait(pe, used.get(n - 2, {}).get("t"))
            pe.matmul(ps[:, bank, :], m[w1][:], xs, start=True, stop=True)
            mp = c.PE.done(pe.matmul(ps[:, bank + 1, :], m[w2][:], xs, start=True, stop=True))
            t, part = m["a1_t"][:, k], m["a1_part"][:, k]
            wait(dve, mp, used.get(n - 2, {}).get("split"))
            c.DVE.done(dve.scalar_tensor_tensor(t[:, 0, :], ps[:, bank, :], m["a1_bcol"][:, b1:b1 + 1],
                                                m["a1_cos"][:, lpos:lpos + BLK], ALU.add, ALU.mult))
            tt = c.dve_step(dve.scalar_tensor_tensor(t[:, 1, :], ps[:, bank + 1, :], m["a1_bcol"][:, b1 + 1:b1 + 2],
                                                     m["a1_sin"][:, lpos:lpos + BLK], ALU.add, ALU.mult))
            r0 = c.DVE.done(dve.tensor_tensor(t[:, 0, :], t[:, 0, :], t[:, 1, :], ALU.add))
            wait(act, r0, used.get(n - 2, {}).get("stored"))
            h0 = c.ACT.done(act.copy(part[:, 0, :], t[:, 0, :]))
            wait(pool, h0)
            r1 = c.POOL.done(pool.tensor_tensor(t[:, 1, :], t[:, 0, :], part[:, 0, :], ALU.subtract))
            wait(act, r1)
            h1 = c.ACT.done(act.copy(part[:, 1, :], t[:, 1, :]))
            wait(pool, h1)
            r2 = c.POOL.done(pool.tensor_tensor(part[:, 2, :], t[:, 1, :], part[:, 1, :], ALU.subtract))
            wait(sp, h0, h1, r2)
            for pt in range(3):
                for rep in range(3):
                    row = 3 * pt + rep if what == 0 else 3 * rep + pt
                    ms = s_st[k].done(sp.dma_start(scr[:, row, :, b * BLK:(b + 1) * BLK], part[:, pt, :]), 16)
            used[n] = {"t": tt, "split": r2, "stored": ms}
            n += 1
        bank = 4 + b % 2
        wait(pe, used.get(("v", b - 2)))
        for j in range(TPB):
            mm = pe.matmul(ps[:, bank, j * D:(j + 1) * D], xnT[:, (b * TPB + j) * P:(b * TPB + j + 1) * P],
                           m["a1_wv"][:], start=True, stop=True)
        mm = c.PE.done(mm)
        wait(dve, mm)
        used[("v", b)] = c.DVE.done(dve.tensor_tensor(
            v[:, b * TPB:(b + 1) * TPB, :], ps[:, bank, :].rearrange("p (t d) -> p t d", d=D),
            m["a1_bv"][:].unsqueeze(1).broadcast_to([P, TPB, D]), ALU.add))
    vdone = used[("v", NB - 1)]
    wait(pe, vdone, tt, idb)
    wait(sp, (s_st[0], s_st[0].n), (s_st[1], s_st[1].n))
    wait(sp, ones_k)
    wait(pool, vdone)
    wait(pe, ones_v)
    wait(dve, ones_v)

    U = 2 * NTB
    s_load = [Events(nc, f"s_a1_load{k}", sp, by=32) for k in range(NG)]
    s_s1 = Events(nc, "s_a1_s1", pe)
    s_red = Events(nc, "s_a1_red", dve, credit=2)
    s_neg = Events(nc, "s_a1_neg", dve)
    s_mt = Events(nc, "s_a1_mt", pe)
    s_mc = Events(nc, "s_a1_mc", dve, credit=1)
    s_ms = Events(nc, "s_a1_ms", sp, credit=1, by=16)
    s_mrow = [Events(nc, f"s_a1_mrow{k}", sp, credit=1, by=16) for k in range(2)]
    s_s2 = Events(nc, "s_a1_s2", pe)
    s_exp = Events(nc, "s_a1_exp", act, credit=4)
    s_va = Events(nc, "s_a1_va", pool)
    s_pv = Events(nc, "s_a1_pv", pe, credit=U + 2)
    s_o = Events(nc, "s_a1_o", act, credit=1)
    q, kk, pt, o = m["a1_q"], m["a1_k"], m["a1_p"], m["a1_o"]
    mx, mr, msp, mt = m["a1_mx"], m["a1_mr"], m["a1_ms"], m["a1_mt"]
    chain = Events(nc, "s_a1_chain", dve)
    links = [0]

    def load(bsel, g, k):
        for dst, scr in ((q, scr_q), (kk, scr_k)):
            src = scr[k * HG:(k + 1) * HG].rearrange("h r d (b t) -> b (r d) h t", b=B)[bsel]
            if not isinstance(bsel, int):
                src = src.rearrange("o r h t -> (o r) h t")
            sp.dma_start(dst[0:KR, k, :, :], src).then_inc(s_load[k].sem, 16)

    def max_tile(st, k, n, t):
        qh, h, qt = t // 16, (t % 16) // 4, t % 4
        bank = 3 + 2 * (t % 2)
        s_red.wait(pe, st * 32 + (t - 2))
        if t % 16 == 0:
            s_mc.wait(pe, st * 2 + (qh - 1))
        for half in range(2):
            mm = pe.matmul(ps[:, bank + half, :], q[0:KR, k, h, (qh * 4 + qt) * P:(qh * 4 + qt + 1) * P],
                           kk[0:KR, k, h, half * BLK:(half + 1) * BLK], start=True, stop=True)
        s_s1.fire(mm)
        s_s1.wait(dve, st * 32 + t)
        s_red.fire(dve.tensor_reduce(mx[:, qh, h * 4 + qt:h * 4 + qt + 1],
                                       ps[:, bank:bank + 2, :].rearrange("p a b -> p (a b)"), X, ALU.max))

    def max_rows(st, k, qh):
        e = st * 2 + qh
        s_red.wait(dve, st * 32 + (16 * qh + 15))
        a = chain.fire(dve.tensor_scalar(msp[:, 0, :], mx[:, qh, :], -1.0, None, ALU.mult))
        chain.wait(dve, e * 3 + 0)
        chain.fire(dve.scalar_tensor_tensor(mr[:], mx[:, qh, :], -1.0, msp[:, 0, :], ALU.mult, ALU.subtract))
        chain.wait(dve, e * 3 + 1)
        chain.fire(dve.tensor_copy(msp[:, 1, :], mr[:]))
        chain.wait(dve, e * 3 + 2)
        s_neg.fire(dve.tensor_tensor(msp[:, 2, :], mr[:], msp[:, 1, :], ALU.subtract))
        s_neg.wait(pe, e)
        s_red.wait(pe, st * 32 + (16 * qh + 15), alone=True)
        tp = ps[0:48, 3, 0:64].bitcast(BF16)
        s_mt.fire(pe.transpose(tp, msp[:].rearrange("p a b -> p (a b)"), m["identb"][:]))
        s_mt.wait(dve, e)
        s_ms.wait(dve, e - 1)
        s_mc.fire(dve.tensor_copy(mt[:], tp))
        s_mc.wait(sp, e)
        s_mrow[qh].wait(sp, st - 1)
        s_ms.fire(sp.dma_start(scr_m[qh].rearrange("a h t q -> (a h t) q"), mt[:]))
        s_ms.wait(sp, e)
        s_mrow[qh].fire(sp.dma_start(q[KR:KA, k, :, qh * BLK:(qh + 1) * BLK],
                                       scr_m[qh].rearrange("a h t q -> a h (t q)")))

    def step(st, k, i, kn, bsel2, first=False):
        k2 = (k + 2) % NG
        s_pv.wait(sp, (st - 1) * U - 1)
        load(bsel2, st, k2)
        s_pv.wait(pool, st * U - 2)
        s_va.fire(pool.tensor_copy(
            va[:, :, k * HG:(k + 1) * HG, 0:HD],
            v[:, bass.ds(i * NTB, NTB), k * HG * HD:(k + 1) * HG * HD].rearrange("p t (h d) -> p t h d", d=HD)))
        s_va.wait(pe, st)
        s_load[kn].wait(pe, i + (1 if kn == 0 else 0))
        for u in range(U + 1):
            qh, kb = divmod(u, NTB)
            if u < U:
                if u == NTB:
                    max_rows(st + 1, kn, 0)
                if kb == 0:
                    s_mrow[qh].wait(pe, st)
                for h in range(HG):
                    n = u * HG + h
                    bank = n % 3
                    s_exp.wait(pe, st * (U * HG) + (n - 3 if n else n - 1))
                    s_s2.fire(pe.matmul(ps[:, bank, :], kk[0:KA, k, h, kb * P:(kb + 1) * P],
                                          q[0:KA, k, h, qh * BLK:(qh + 1) * BLK], start=True, stop=True))
                    s_s2.wait(act, st * (U * HG) + n)
                    if h == 0:
                        s_pv.wait(act, st * U + (u - 2))
                    s_exp.fire(act.activation(pt[:, (u % 2) * HG + h, :], ps[:, bank, :], ACT.Exp,
                                                scale=float(HD) ** -0.5))
                    if h % 2 == 1:
                        t = 2 * u + h // 2
                        max_tile(st + 1, kn, 0, t)
            if u >= 1:
                uu = u - 1
                qh1, kb1 = divmod(uu, NTB)
                s_exp.wait(pe, st * (U * HG) + (uu * HG + HG - 1))
                if kb1 == 0:
                    s_o.wait(pe, st * QH + (qh1 - 1))
                for h in range(HG):
                    mm = pe.matmul(ps[32 * h:32 * h + 32, 7, :], va[:, kb1, k * HG + h, :],
                                   pt[:, (uu % 2) * HG + h, :], start=kb1 == 0, stop=kb1 == NTB - 1,
                                   skip_group_check=True)
                s_pv.fire(mm)
                if kb1 == NTB - 1:
                    s_pv.wait(act, st * U + uu, alone=True)
                    s_o.fire(act.copy(o[:, bass.ds(i * (NG * QH) + (k * QH + qh1), 1), :]
                                        .rearrange("p o q -> p (o q)"), ps[:, 7, :]))
        max_rows(st + 1, kn, 1)

    load(0, 0, 0)
    load(0, 1, 1)
    s_load[0].wait(pe, 0)
    for t in range(32):
        max_tile(0, 0, 0, t)
        if t % 16 == 15:
            max_rows(0, 0, t // 16)
    with nc.Fori(0, B) as i:
        for k in range(NG):
            bsel2 = bass.ds(i, 1) if k < 2 else bass.ds(i * -1 + 1, 1)
            step(i * NG + k, k, i, (k + 1) % NG, bsel2)
    G = B * NG
    for k in range(NG):
        s_load[k].wait(sp, 2 if k < 2 else 1)
    for qh in range(2):
        s_mrow[qh].wait(sp, G)
    s_o.wait(pe, G * QH - 1)
    s_red.wait(pe, (G + 1) * 32 - 1)
    s_exp.wait(pe, G * U * HG - 1)
    s_mc.wait(pe, 2 * G + 1)
    s_red.wait(dve, (G + 1) * 32 - 1)
    at = xn
    rd = m["a1_rd"]
    done = {}
    for n in range(G * QH):
        b, g, qh = n // (NG * QH), n // QH % NG, n % QH
        bank = n % 2
        wait(pe, done.get(n - 2))
        for j in range(4):
            mm = pe.transpose(ps[:, bank, j * P:(j + 1) * P], o[:, n, j * P:(j + 1) * P], m["ident"][:])
        mm = c.PE.done(mm)
        wait(dve, mm)
        sums = ps[:, bank, :].rearrange("p (t h d) -> p t h d", t=4, d=32)
        c.dve_step(dve.reciprocal(rd[:, n % 2], sums[:, :, :, HD]))
        tile0 = b * NTB + qh * 4
        done[n] = c.DVE.done(dve.tensor_tensor(
            at[:, tile0:tile0 + 4, g * 32:(g + 1) * 32].rearrange("p t (h d) -> p t h d", d=HD),
            sums[:, :, :, 0:HD], rd[:, n % 2].unsqueeze(3).broadcast_to([P, 4, HG, HD]), ALU.mult))
    last = {}
    for b in range(NB):
        bank, bank2 = 2 + b % 2, 4 + b % 2
        wait(pe, done[G * QH - 1], last.get(("c", b - 2)), last.get(("y", b - 2)))
        for j in range(TPB):
            mm = pe.transpose(ps[:, bank, j * P:(j + 1) * P], at[:, b * TPB + j, :], m["ident"][:])
        wait(act, c.PE.done(mm))
        last[("c", b)] = cc = c.ACT.done(act.copy(xnT[:, b * BLK:(b + 1) * BLK], ps[:, bank, :]))
        wait(pe, cc)
        for j in range(TPB):
            mm = pe.matmul(ps[:, bank2, j * D:(j + 1) * D], xnT[:, (b * TPB + j) * P:(b * TPB + j + 1) * P],
                           m["a1_wo"][:], start=True, stop=True)
        wait(dve, c.PE.done(mm))
        xb = x[:, b * TPB:(b + 1) * TPB, :]
        y = c.dve_step(dve.tensor_tensor(xb, xb, ps[:, bank2, :].rearrange("p (t d) -> p t d", d=D), ALU.add))
        last[("y", b)] = y
        end = c.DVE.done(dve.tensor_tensor(xb, xb, m["a1_bo"][:].unsqueeze(1).broadcast_to([P, TPB, D]), ALU.add))
    return end


def attn1_layout(a, out):
    swap = np.arange(D).reshape(-1, 2)[:, ::-1].reshape(-1)
    for n in ("q", "k"):
        out[f"a1_w{n}"] = a[f"L1_attn_W{n}"].T
        out[f"a1_w{n}s"] = a[f"L1_attn_W{n}"][swap].T
    out["a1_wv"] = a["L1_attn_Wv"].T
    out["a1_wo"] = a["L1_attn_Wo"].T
    bq, bk = a["L1_attn_bq"], a["L1_attn_bk"]
    out["a1_bcol"] = np.stack([bq, bq[swap], bk, bk[swap]], 1)
    out["a1_bv"], out["a1_bo"] = a["L1_attn_bv"], a["L1_attn_bo"]
    f = np.float32
    inv = (f(1.0) / f(10000.0) ** (np.arange(0, HD, 2, dtype=f) / f(HD))).astype(f)
    ang = np.repeat(np.arange(L, dtype=f)[:, None] * inv[None, :], 2, axis=1).T
    sign = np.where(np.arange(HD) % 2 == 0, f(-1), f(1))[:, None]
    out["a1_cos"] = np.tile(np.cos(ang), (NH, 1)).astype(f)
    out["a1_sin"] = np.tile(np.sin(ang) * sign, (NH, 1)).astype(f)


H0, DK = 4, 32
CH = 32
NCH = L // CH
S6 = 6
PAD = 32
QT, KTOK, KBTOK, VBTOK, TT, AT = range(6)


def attn0_memory(c, w):
    for n, shape in (("w3", [D, 3, D]), ("bw", [D, D]), ("w1x", [D, D]), ("w1s", [P, D]), ("w2", [D, 24]),
                     ("b1", [D, 1]), ("ow", [D, D]), ("onorm", [D, 1]), ("fw1", [D, 1]), ("fw", [P, 44]),
                     ("heads", [P, P]), ("sel", [P, S6, 32]), ("strict", [P, CH]), ("incl", [P, CH]), ("diag", [P, CH])):
        c.load("a0_" + n, w["a0_" + n], shape)
    c.load("a0_b2", w["a0_b2"].partition_broadcast(P), [P, 24])
    c.load("a0_temp", w["a0_temp"].partition_broadcast(P), [P, H0])
    c.load("a0_eye", w["a0_eye"].partition_broadcast(P), [P, CH * CH])
    c.sb("a0_wf", [D, 3, 4, D])
    c.sb("a0_wfir", [P, 44, 32]); c.sb("a0_eps", [P, 2])
    c.sb("a0_tt", [P, 3, H0]); c.sb("a0_lo", [P, NT, 24]); c.sb("a0_m", [P, NT * H0]); c.sb("a0_zero", [P, P])


def attn0(c, w, x, lead):
    nc, ps, m = c.nc, c.psum, c.mem
    pe, dve, act, pool, sp = c.pe, c.dve, c.act, c.pool, c.sp
    PE, DVE, AC, PO = c.PE, c.DVE, c.ACT, c.POOL
    a = c.arena
    arena0 = a.top
    u1 = a.take([P, H0 * B * (PAD + L)])
    kk = u1[:, 0:3 * T].rearrange("p (s t) -> p s t", s=3)
    am = u1[:, 3 * T:4 * T].rearrange("p (b n j) -> p b n j", b=B, j=CH)
    v4 = u1.rearrange("p (g b t) -> p g b t", g=H0, b=B)
    bt = a.take([P, T])
    asub = bt.rearrange("p (b i j) -> p b i j", b=B, i=CH)
    ttf = a.take([P, B * CH * CH])
    tt = ttf.rearrange("p (b i j) -> p b i j", b=B, i=CH)
    taps = ttf[:, 0:12 * D].rearrange("p (s j d) -> p s j d", s=3, j=4)
    c.loads.done(sp.dma_start(ttf[:, 0:12 * D], w["a0_taps"].partition_broadcast(P)), 16)
    opf = a.take([P, (NCH + 1) * B * 6 * CH])
    op = opf.rearrange("p (n b o i) -> p n b o i", b=B, o=6, i=CH)
    wexp = opf[:, 0:NT * S6 * D].rearrange("p (t s f) -> p t s f", t=NT, s=S6)
    br = a.take([P, S6, T])
    sqf = a.take([P, 2 * BLK])
    sq = sqf.rearrange("p (k t) -> p k t", k=2)
    kbuf = sqf[:, 0:6 * P].rearrange("p (b s t) -> p b s t", b=2, s=3)
    xn, xf = m["xn"], m["xnT"]
    xp = xf[:, 0:B * (L + 3)].rearrange("p (b t) -> p b t", b=B)
    xnd = xn[:].rearrange("p t d -> p (t d)")
    scr_a = nc.dram_tensor("scr_a", [B, NCH, H0, CH, CH], F32, kind="Internal").ap()
    scr_t = nc.dram_tensor("scr_t", [B, NCH, H0, CH, CH], F32, kind="Internal").ap()

    c.loaded(pe, dve, act, pool)
    DVE.done(dve.memset(xp[:, :, 0:3], 0.0))
    DVE.done(dve.memset(m["a0_eps"][:, 0:1], 1e-6))
    DVE.done(dve.memset(m["a0_eps"][:, 1:2], 1e-5))
    DVE.done(dve.memset(m["a0_zero"][:], 0.0))
    wfd = DVE.done(dve.tensor_tensor(m["a0_wf"][:], m["a0_w3"][:].unsqueeze(2).broadcast_to([D, 3, 4, D]),
                                     taps, ALU.mult))
    zop = PO.done(pool.memset(op[:, NCH], 0.0))
    outs = layer_norm(c, x, xn, 1e-5, lead, xf,
                      out_at=lambda b: xp[:, b // 2, 3 + b % 2 * BLK:3 + b % 2 * BLK + BLK])
    wait(pe, *outs, wfd)
    read, vdone, qk = {}, [], []
    for n in range(NB):
        b, t0, sl = n // 2, n % 2 * BLK, slice(n * BLK, (n + 1) * BLK)
        base = 4 * (n % 2)
        wait(pe, read.get(n - 2))
        for s in range(3):
            for j in range(4):
                mm = pe.matmul(ps[:, base + s, :], m["a0_wf"][:, s, j, :], xp[:, b, t0 + j:t0 + j + BLK],
                               start=j == 0, stop=j == 3)
            mm = PE.done(mm)
            wait(act, mm)
            dst = kk[:, s, sl] if s < 2 else br[:, 5, sl]
            q = AC.done(act.activation(dst, ps[:, base + s, :], ACT.Silu))
        vdone.append(q)
        mm = PE.done(pe.matmul(ps[:, base + 3, :], m["a0_bw"][:], xp[:, b, 3 + t0:3 + t0 + BLK], start=True, stop=True))
        wait(act, mm)
        read[n] = AC.done(act.activation(bt[:, sl], ps[:, base + 3, :], ACT.Tanh, scale=0.5))
    wait(dve, read[NB - 1])
    c.dve_step(dve.tensor_scalar(bt[:], bt[:], 0.5, 0.5, ALU.mult, ALU.add))
    banks = {}
    for n in range(2 * NB):
        s, sl = n // NB, slice(n % NB * BLK, (n % NB + 1) * BLK)
        wait(act, banks.get(n - 2))
        z = AC.done(act.activation(sq[:, n % 2, :], kk[:, s, sl], ACT.Square))
        wait(pe, z)
        banks[n] = PE.done(pe.matmul(ps[:, n, :], m["a0_heads"][:], sq[:, n % 2, :], start=True, stop=True))
    wait(act, banks[2 * NB - 1])
    for n in range(2 * NB):
        z = AC.done(act.activation(ps[:, n, :], ps[:, n, :], ACT.Ln, bias=m["a0_eps"][:, 0:1]))
    wait(act, z)
    for n in range(2 * NB):
        s, b, half, sl = n // NB, n % NB // 2, n % 2, slice(n % NB * BLK, (n % NB + 1) * BLK)
        z = AC.done(act.activation(ps[:, n, :], ps[:, n, :], ACT.Exp, scale=-0.5))
        wait(dve, z)
        qk.append(DVE.done(dve.tensor_tensor(kk[:, s, sl], kk[:, s, sl], ps[:, n, :], ALU.mult)))
    wait(pool, qk[NB - 1])
    for b in range(B):
        qcopy = PO.done(pool.tensor_copy(op[:, 0:NCH, b, QT, :],
                                         kk[:, 0, b * L:(b + 1) * L].rearrange("p (n i) -> p n i", i=CH)))
    wait(dve, qk[-1])
    c.dve_step(dve.tensor_tensor(kk[:, 2, :], kk[:, 1, :], bt[:], ALU.mult))
    kb = (DVE, DVE.n)
    vb = c.dve_step(dve.tensor_tensor(xnd, br[:, 5, :], bt[:], ALU.mult))

    s_kbuf = Events(nc, "s_a0_kbuf", act)
    s_ap = Events(nc, "s_a0_ap", pe, credit=2)
    s_am = Events(nc, "s_a0_am", dve, credit=2)
    wait(act, kb)
    wait(pe, (DVE, DVE.n))
    with nc.Fori(0, NCH // 4) as i:
        for b in range(B):
            n = i * B + b
            s_ap.wait(act, n - 2, alone=True)
            s_kbuf.fire(act.copy(kbuf[:, b], kk[:, :, bass.ds(i * P + b * L, P)]))
            s_kbuf.wait(pe, n, alone=True)
            s_am.wait(pe, n - 2, alone=True)
            for cc in range(4):
                for out, lh, rh in ((0, 2, 1), (1, 1, 0)):
                    for h in range(H0):
                        hs, cs = slice(32 * h, 32 * h + 32), slice(cc * CH, (cc + 1) * CH)
                        mm = pe.matmul(ps[hs, 2 * b + out, cs], kbuf[hs, b, lh, cs], kbuf[hs, b, rh, cs],
                                       start=True, stop=True, skip_group_check=True)
            s_ap.fire(mm)
            s_ap.wait(dve, n)
            for out, mask, dst in ((0, "a0_strict", am[:, b, bass.ds(i * 4, 4), :]),
                                   (1, "a0_incl", op[:, bass.ds(i * 4, 4), b, AT, :])):
                z = dve.tensor_tensor(dst, ps[:, 2 * b + out, 0:4 * CH].rearrange("p (n j) -> p n j", j=CH),
                                      m[mask][:].unsqueeze(1).broadcast_to([P, 4, CH]), ALU.mult)
            s_am.fire(z)
    s_rel = Progress(nc, "s_a0_rel")
    s_am.wait(sp, B * NCH // 4 - 1)
    for b in range(B):
        for h in range(H0):
            z = s_rel.done(sp.dma_start(scr_a[b, :, h].rearrange("n i j -> i n j"), am[32 * h:32 * h + 32, b]), 16)
    wait(sp, z)
    for b in range(B):
        z = s_rel.done(sp.dma_start(asub[:, b].rearrange("p i j -> p (i j)"),
                                    scr_a[b].rearrange("n h i j -> (n h) (i j)")), 16)
    a_in = z
    for b in range(B):
        ts = slice(b * L, (b + 1) * L)
        for item, src in ((KTOK, kk[:, 1, ts]), (KBTOK, kk[:, 2, ts]), (VBTOK, xnd[:, ts])):
            z = DVE.done(dve.transpose(op[:, 0:NCH, b, item, :], src.rearrange("p (n i) -> p n i", i=CH)))
    tok = z
    s_v4 = Progress(nc, "s_a0_v4")
    wait(pool, a_in, qcopy, tok)
    s_ap.wait(pool, B * NCH // 4 - 1)
    zv = PO.done(pool.memset(v4[:, :, :, 0:PAD + 4], 0.0))
    wait(sp, zv, vdone[-1])
    for j in range(4):
        for g in range(H0):
            z = s_v4.done(sp.dma_start(v4[32 * j:32 * j + 32, g, :, PAD + j:PAD + L],
                                       br[32 * g:32 * g + 32, 5, :].rearrange("p (b t) -> p b t", b=B)[:, :, 0:L - j]), 16)
    v4_in = z
    eye = m["a0_eye"][:].rearrange("p (i j) -> p i j", i=CH).unsqueeze(1).broadcast_to([P, B, CH, CH])
    c.dve_step(dve.tensor_copy(tt, eye))
    wf = DVE.done(dve.tensor_tensor(
        m["a0_wfir"][:], m["a0_fw"][:].unsqueeze(2).broadcast_to([P, 44, 32]),
        m["a0_diag"][:].unsqueeze(1).broadcast_to([P, 44, 32]), ALU.mult))
    wait(dve, a_in)
    prod = xnd.rearrange("p (b i j) -> p b i j", b=B, i=CH)
    for i in range(1, CH):
        c.dve_step(dve.tensor_tensor(prod[:, :, 0:i, 0:i], asub[:, :, i, 0:i].unsqueeze(2).broadcast_to([P, B, i, i]),
                                     tt[:, :, 0:i, 0:i], ALU.mult))
        z = c.dve_step(dve.tensor_reduce(tt[:, :, 0:i, i], prod[:, :, 0:i, 0:i], X, ALU.add))
    wait(sp, z)
    for b in range(B):
        z = s_rel.done(sp.dma_start(scr_t[b].rearrange("n h c i -> (n h) (c i)"), tt[:, b].rearrange("p c i -> p (c i)")), 16)
    wait(sp, z)
    for b in range(B):
        for h in range(H0):
            z = s_rel.done(sp.dma_start(op[32 * h:32 * h + 32, 0:NCH, b, TT, :],
                                        scr_t[b, :, h].rearrange("n c i -> c n i")), 16)
    t_in = z
    wait(pe, wf, v4_in)
    wait(act, vdone[-1])
    firb = {}
    FM = ((1, 0, 1), (2, 1, 2), (3, 3, 8))
    for n in range(NB):
        b, t0, sl = n // 2, n % 2 * BLK, slice(n * BLK, (n + 1) * BLK)
        for s, g0, ng in FM:
            k = n * 3 + s - 1
            bank = 5 + k % 3
            wait(pe, firb.get(k - 3))
            for g in range(ng):
                for h in range(H0):
                    mm = pe.matmul(ps[32 * h:32 * h + 32, bank, :], m["a0_wfir"][:, (g0 + g) * H0 + h, :],
                                   v4[:, h, b, PAD + t0 - 4 * g:PAD + t0 - 4 * g + BLK],
                                   start=g == 0, stop=g == ng - 1, skip_group_check=True)
            wait(act, PE.done(mm))
            firb[k] = AC.done(act.copy(br[:, s, sl], ps[:, bank, :]))
    f1 = PO.done(pool.tensor_scalar(br[:, 0, :], br[:, 5, :], m["a0_fw1"][:, 0:1], None, ALU.mult))

    sbuf = bt[:, 0:24 * CH].rearrange("p (k b o i) -> p k b o i", k=2, b=B, o=6)
    wt, st, uh = (bt[:, (24 + 4 * k) * CH:(28 + 4 * k) * CH].rearrange("p (k b i) -> p k b i", k=2, b=B)
                  for k in range(3))
    W_, U_, S_, O_ = 0, 1, 3, 4
    s_sb = Events(nc, "s_a0_sb", act)
    s_w = Events(nc, "s_a0_w", pe)
    s_wn = Events(nc, "s_a0_wn", act)
    s_u = Events(nc, "s_a0_u", pe)
    s_uh = Events(nc, "s_a0_uh", dve)
    s_s = Events(nc, "s_a0_s", pe)
    s_sc = Events(nc, "s_a0_sc", dve, credit=1)
    s_o = Events(nc, "s_a0_o", pe, credit=2)
    s_oc = Events(nc, "s_a0_oc", act, credit=1)

    def each():
        for b in range(B):
            for h in range(H0):
                yield b, slice(32 * h, 32 * h + 32), slice(b * CH, (b + 1) * CH)

    def fetch(n, par, src):
        s_o.wait(act, n - 2, alone=True)
        s_sb.fire(act.copy(sbuf[:, par].rearrange("p b k i -> p (b k i)"), src))

    def make_w(n, par):
        s_sb.wait(pe, n, alone=True)
        for b, hs, bs in each():
            mm = pe.matmul(ps[hs, W_, bs], sbuf[hs, par, b, KBTOK, :], sbuf[hs, par, b, TT, :],
                           start=True, stop=True, skip_group_check=True)
        s_w.fire(mm)
        s_w.wait(act, n)
        s_wn.fire(act.mul(wt[:, par].rearrange("p b i -> p (b i)"), ps[:, W_, 0:B * CH], -1.0))

    def make_u(n, par):
        for b, hs, bs in each():
            pe.matmul(ps[hs, U_ + b, 0:CH], sbuf[hs, par, b, TT, :], sbuf[hs, par, b, VBTOK, :],
                      start=True, stop=False, skip_group_check=True)

    s_am.wait(act, B * NCH // 4 - 1)
    wait(act, t_in, tok, zop, firb[NB * 3 - 1])
    wait(pe, tok, firb[NB * 3 - 1])
    s_am.wait(pe, B * NCH // 4 - 1)
    z = DVE.done(dve.memset(st[:, 1], 0.0))
    wait(pe, z)
    pe.matmul(ps[:, S_, 0:B * CH], m["a0_zero"][:], m["a0_zero"][:, 0:B * CH], start=True, stop=True, skip_group_check=True)
    fetch(0, 0, op[:, 0].rearrange("p b k i -> p (b k i)"))
    make_w(0, 0)
    make_u(0, 0)
    with nc.Fori(0, NCH // 2) as i:
        for par in range(2):
            n, nxt = i * 2 + par, 1 - par
            fetch(n + 1, nxt, op[:, bass.ds(i * 2 + par + 1, 1)].rearrange("p o b k i -> p (o b k i)"))
            s_wn.wait(pe, n, alone=True)
            s_sc.wait(pe, n - 1, alone=True)
            for b, hs, bs in each():
                mm = pe.matmul(ps[hs, U_ + b, 0:CH], wt[hs, par, b, :], st[hs, nxt, b, :],
                               start=False, stop=True, skip_group_check=True)
            s_u.fire(mm)
            s_u.wait(dve, n)
            s_uh.fire(dve.tensor_copy(uh[:, par], ps[:, U_:U_ + 2, 0:CH]))
            make_w(n + 1, nxt)
            s_uh.wait(pe, n, alone=True)
            for b, hs, bs in each():
                mm = pe.matmul(ps[hs, S_, bs], sbuf[hs, par, b, KTOK, :], uh[hs, par, b, :],
                               start=False, stop=True, skip_group_check=True)
            s_s.fire(mm)
            s_s.wait(dve, n)
            s_o.wait(dve, n - 1)
            s_sc.fire(dve.tensor_copy(st[:, par].rearrange("p b i -> p (b i)"), ps[:, S_, 0:B * CH]))
            s_oc.wait(pe, n - 1, alone=True)
            for b, hs, bs in each():
                pe.matmul(ps[hs, O_, bs], st[hs, nxt, b, :], sbuf[hs, par, b, QT, :],
                          start=True, stop=False, skip_group_check=True)
                mm = pe.matmul(ps[hs, O_, bs], uh[hs, par, b, :], sbuf[hs, par, b, AT, :],
                               start=False, stop=True, skip_group_check=True)
            s_o.fire(mm)
            s_o.wait(act, n, alone=True)
            s_oc.fire(act.copy(br[:, 4, :].rearrange("p (b t) -> p b t", b=B)[:, :, bass.ds(i * (2 * CH) + par * CH, CH)],
                                 ps[:, O_, 0:B * CH].rearrange("p (b i) -> p b i", b=B)))
            make_u(n + 1, nxt)
    s_wn.wait(pe, NCH)
    s_oc.wait(dve, NCH - 1)
    s_oc.wait(act, NCH - 1)
    s_oc.wait(pe, NCH - 1)
    s_oc.wait(pool, NCH - 1)
    wait(dve, firb[NB * 3 - 1], f1)
    wait(act, f1)
    wait(pe, f1)
    a.top = arena0
    ab = a.take([P, 2, BLK])
    sqs = a.take([P, 2, BLK])
    stt_ = a.take([P, NB, BLK])
    sqb = a.take([P, 2, BLK])
    hg = a.take([P, T])
    fu = a.take([P, T])
    tmp = a.take([P, 2, BLK])
    assert a.top - arena0 <= H0 * B * (PAD + L) + 2 * T
    cpu = {}
    k = 0
    for n in range(NB):
        sl = slice(n * BLK, (n + 1) * BLK)
        bA, bB = n % 2, 2 + n % 2
        wait(pe, cpu.get(("st", n - 2)))
        for s in range(S6):
            wait(dve, cpu.get(("pe", k - 2)))
            ma = DVE.done(dve.scalar_tensor_tensor(ab[:, k % 2, :], br[:, s, sl], -1.0, br[:, s, sl],
                                                   ALU.mult, ALU.max))
            wait(act, cpu.get(("pe", k - 2)))
            mq = AC.done(act.activation(sqs[:, k % 2, :], br[:, s, sl], ACT.Square))
            wait(pe, ma, mq)
            f = dict(start=s == 0, stop=s == S6 - 1, skip_group_check=True)
            pe.matmul(ps[0:32, bA, :], m["a0_sel"][:, s, :], br[:, s, sl], **f)
            pe.matmul(ps[32:64, bA, :], m["a0_sel"][:, s, :], ab[:, k % 2, :], **f)
            pe.matmul(ps[64:96, bA, :], m["a0_sel"][:, s, :], sqs[:, k % 2, :], **f)
            pe.matmul(ps[96:128, bA, :], m["a0_sel"][:, s, :], sqs[:, k % 2, :], **f)
            cpu[("pe", k)] = PE.done(pe.matmul(ps[96:128, bB, :], m["a0_sel"][:, s, :], br[:, s, sl], **f))
            k += 1
        done = cpu[("pe", k - 1)]
        wait(act, done, cpu.get(("st", n - 2)))
        mq = AC.done(act.activation(sqb[96:128, n % 2, :], ps[96:128, bB, :], ACT.Square, scale=float(DK) ** -0.5))
        wait(dve, done, mq)
        DVE.done(dve.tensor_scalar(stt_[0:64, n, :], ps[0:64, bA, :], 1.0 / DK, None, ALU.mult))
        DVE.done(dve.tensor_copy(stt_[64:96, n, :], ps[64:96, bA, :]))
        c.dve_step(dve.tensor_tensor(stt_[96:128, n, :], ps[96:128, bA, :], sqb[96:128, n % 2, :], ALU.subtract))
        cpu[("st", n)] = DVE.done(dve.tensor_scalar(stt_[96:128, n, :], stt_[96:128, n, :], 0.0, 1.0 / (DK - 1),
                                                    ALU.max, ALU.mult))
    wait(act, cpu[("st", NB - 1)])
    rt = AC.done(act.activation(stt_[64:128, :, :], stt_[64:128, :, :], ACT.Sqrt))
    wait(pe, rt)
    for n in range(NB):
        b, t0, sl = n // 2, n % 2 * BLK, slice(n * BLK, (n + 1) * BLK)
        bank = 4 + n % 2
        wait(pe, cpu.get(("ge", n - 2)))
        pe.matmul(ps[:, bank, :], m["a0_w1x"][:], xp[:, b, 3 + t0:3 + t0 + BLK], start=True, stop=False)
        mm = PE.done(pe.matmul(ps[:, bank, :], m["a0_w1s"][:], stt_[:, n, :], start=False, stop=True))
        wait(act, mm)
        cpu[("ge", n)] = AC.done(act.activation(hg[:, sl], ps[:, bank, :], ACT.Gelu, bias=m["a0_b1"][:, 0:1]))
        wait(pe, cpu[("ge", n)])
        for j in range(TPB):
            t = n * TPB + j
            mm = pe.matmul(ps[:, 6, t * 24:(t + 1) * 24], hg[:, t * P:(t + 1) * P], m["a0_w2"][:], start=True, stop=True)
    mm = PE.done(mm)
    g0, g1, g2 = (m["a0_tt"][:, k, :] for k in range(3))
    c.dve_step(dve.scalar_tensor_tensor(g0, m["a0_temp"][:], -1.0, m["a0_temp"][:], ALU.mult, ALU.min))
    wait(act, (DVE, DVE.n))
    e = c.act_step(act.activation(g0, g0, ACT.Exp))
    e = AC.done(act.activation(g0, g0, ACT.Ln, bias=1.0))
    wait(dve, e)
    c.dve_step(dve.tensor_scalar(g1, m["a0_temp"][:], 0.0, 0.5, ALU.max, ALU.add))
    c.dve_step(dve.tensor_tensor(g1, g1, g0, ALU.add))
    c.dve_step(dve.reciprocal(g2, g1))
    lo = m["a0_lo"]
    mh = m["a0_m"]
    lo6 = lo[:].rearrange("p t (h s) -> p (t h) s", h=H0)
    wait(dve, mm)
    c.dve_step(dve.tensor_tensor(lo[:], ps[:, 6, 0:NT * 24].rearrange("p (t k) -> p t k", k=24),
                                 m["a0_b2"][:].unsqueeze(1).broadcast_to([P, NT, 24]), ALU.add))
    lo4 = lo[:].rearrange("p t (h s) -> p t h s", h=H0)
    c.dve_step(dve.tensor_tensor(lo4, lo4, g2.unsqueeze(1).unsqueeze(3).broadcast_to([P, NT, H0, S6]), ALU.mult))
    c.dve_step(dve.tensor_reduce(mh[:], lo6, X, ALU.max))
    z = c.dve_step(dve.tensor_tensor(lo6, lo6, mh[:].unsqueeze(2).broadcast_to([P, NT * H0, S6]), ALU.subtract))
    wait(act, z)
    e = AC.done(act.activation(lo[:], lo[:], ACT.Exp))
    wait(dve, e)
    c.dve_step(dve.tensor_reduce(mh[:], lo6, X, ALU.add))
    c.dve_step(dve.reciprocal(mh[:], mh[:]))
    wts = c.dve_step(dve.tensor_tensor(lo6, lo6, mh[:].unsqueeze(2).broadcast_to([P, NT * H0, S6]), ALU.mult))
    wait(act, wts)
    spread = [AC.done(act.copy(wexp[:, t].rearrange("p s (h d) -> p s h d", h=H0),
                               lo4[:, t].rearrange("p h s -> p s h").unsqueeze(3).broadcast_to([P, S6, H0, DK])))
              for t in range(NT)]
    k = 0
    for n in range(NB):
        sl = slice(n * BLK, (n + 1) * BLK)
        for s in range(S6):
            bank = k % 6
            wait(pe, spread[n * TPB + TPB - 1], cpu.get(("mul", k - 6)))
            for j in range(TPB):
                mm = pe.transpose(ps[:, bank, j * P:(j + 1) * P], wexp[:, n * TPB + j, s, :], m["ident"][:])
            wait(dve, PE.done(mm))
            if s == 0:
                cpu[("mul", k)] = c.dve_step(dve.tensor_tensor(fu[:, sl], br[:, s, sl], ps[:, bank, :], ALU.mult))
            else:
                cpu[("mul", k)] = c.dve_step(dve.tensor_tensor(tmp[:, k % 2, :], br[:, s, sl], ps[:, bank, :], ALU.mult))
                z = c.dve_step(dve.tensor_tensor(fu[:, sl], fu[:, sl], tmp[:, k % 2, :], ALU.add))
            k += 1
        cpu[("fu", n)] = z
    for n in range(NB):
        sl = slice(n * BLK, (n + 1) * BLK)
        wait(act, cpu[("fu", n)], cpu.get(("ms", n - 2)))
        z = AC.done(act.activation(sqs[:, n % 2, :], fu[:, sl], ACT.Square))
        bank = (6, 7, 0, 1)[n]
        wait(pe, z, cpu[("fu", NB - 1)] if n > 1 else None)
        cpu[("ms", n)] = PE.done(pe.matmul(ps[:, bank, :], m["a0_heads"][:], sqs[:, n % 2, :], start=True, stop=True))
    wait(act, cpu[("ms", NB - 1)])
    for n in range(NB):
        bank = (6, 7, 0, 1)[n]
        z = AC.done(act.activation(ps[:, bank, :], ps[:, bank, :], ACT.Ln, bias=m["a0_eps"][:, 1:2], scale=1.0 / DK))
    wait(act, z)
    for n in range(NB):
        sl = slice(n * BLK, (n + 1) * BLK)
        bank = (6, 7, 0, 1)[n]
        z = AC.done(act.activation(ps[:, bank, :], ps[:, bank, :], ACT.Exp, scale=-0.5))
        wait(dve, z)
        z = DVE.done(dve.scalar_tensor_tensor(fu[:, sl], fu[:, sl], m["a0_onorm"][:, 0:1], ps[:, bank, :],
                                              ALU.mult, ALU.mult))
        bank = 2 + n % 4
        wait(pe, z)
        for j in range(TPB):
            mm = pe.matmul(ps[:, bank, j * D:(j + 1) * D], fu[:, (n * TPB + j) * P:(n * TPB + j + 1) * P],
                           m["a0_ow"][:], start=True, stop=True)
        wait(dve, PE.done(mm))
        xb = x[:, n * TPB:(n + 1) * TPB, :]
        end = DVE.done(dve.tensor_tensor(xb, xb, ps[:, bank, :].rearrange("p (t d) -> p t d", d=D), ALU.add))
    return end


def attn0_layout(a, out):
    f = np.float32
    g = lambda n: a["L0_attn_" + n]
    out["a0_w3"] = np.stack([g("q_w"), g("k_w"), g("v_w")], 1)
    out["a0_taps"] = np.stack([g(n)[:, 0, :].T for n in ("qc_w", "kc_w", "vc_w")], 0).reshape(-1)
    out["a0_bw"] = np.repeat(g("b_w"), DK, axis=1)
    w1 = g("mlp_w1")
    out["a0_w1x"] = w1[:D]
    stat = w1[D:].reshape(H0 * S6, 4, D)
    w1s = np.zeros((P, D), f)
    for q, k in enumerate((0, 2, 3, 1)):
        w1s[32 * q:32 * q + 24] = stat[:, k]
    out["a0_w1s"] = w1s
    out["a0_w2"], out["a0_b1"], out["a0_b2"] = g("mlp_w2"), g("mlp_b1")[:, None], g("mlp_b2")
    out["a0_temp"], out["a0_ow"] = g("gate_log_temp"), g("o_w")
    out["a0_onorm"] = np.tile(g("onorm_w"), H0)[:, None]
    out["a0_fw1"] = g("fir_w1")[:, 0, :]
    cols = []
    for n, groups in (("fir_w3", 1), ("fir_w7", 2), ("fir_w31", 8)):
        wt = g(n)[:, 0, ::-1]
        wt = np.concatenate([wt, np.zeros((D, 4 * groups - wt.shape[1]), f)], 1)
        cols.append(wt.reshape(H0, DK, groups, 4).transpose(3, 1, 2, 0).reshape(P, groups * H0))
    out["a0_fw"] = np.concatenate(cols, 1)
    head = np.arange(P) // DK
    out["a0_heads"] = (head[:, None] == head[None, :]).astype(f)
    sel = np.zeros((P, S6, 32), f)
    for s in range(S6):
        sel[np.arange(P), s, head * S6 + s] = 1
    out["a0_sel"] = sel
    r = np.arange(P)[:, None] % CH
    j = np.arange(CH)[None, :]
    out["a0_strict"] = np.where(j < r, f(-1), f(0))
    out["a0_incl"] = np.where(j >= r, f(1), f(0))
    out["a0_diag"] = (j == r).astype(f)
    out["a0_eye"] = np.eye(CH, dtype=f).reshape(-1)


def ffn1_memory(c, w):
    route_memory(c, w)
    c.load("f1_rw", w["f1_rw"], [D, 8])
    c.load("f1_w1", w["f1_w1"], [D, 8, 512])
    c.load("f1_b1", w["f1_b1"], [8, 512])
    c.load("f1_wo", w["f1_wo"], [P, 4, D])
    for n in ("bo", "gamma", "beta"):
        c.load("f1_" + n, w["f1_" + n].partition_broadcast(P), [P, D])
    c.sb("f1_xm", [P, 8, BLK]); c.sb("f1_mt", [8, T]); c.sb("f1_h", [P, 4, BLK]); c.sb("f1_y", [P, NT, D])


def ffn1(c, w, x, lead):
    nc, ps, m = c.nc, c.psum, c.mem
    pe, dve, act = c.pe, c.dve, c.act
    NE, FC = 8, 4
    xn, xnT = m["xn"], m["xnT"]
    outs = layer_norm(c, x, xn, 1e-5, lead, xnT, out_at=lambda b: xnT[:, b * BLK:(b + 1) * BLK])
    c.loaded(c.pe, c.dve, c.act, c.pool)
    wait(pe, *outs)
    lg = ps[:, 2, 0:NT * NE]
    for t in range(NT):
        mm = pe.matmul(lg[:, t * NE:(t + 1) * NE], xnT[:, t * P:(t + 1) * P], m["f1_rw"][:], start=True, stop=True)
    mask = route(c, lg, None, c.PE.done(mm), 1, m["gate"])
    wait(pe, (c.DVE, c.DVE.n))
    used = {}
    for n in range(NB):
        wait(pe, used.get(("mt", n - 1)))
        for j in range(TPB):
            t = n * TPB + j
            mm = pe.transpose(ps[0:8, 3, j * P:(j + 1) * P], mask[:, t, :], m["ident"][:])
        wait(dve, c.PE.done(mm))
        used[("mt", n)] = c.DVE.done(dve.tensor_copy(m["f1_mt"][:, n * BLK:(n + 1) * BLK], ps[0:8, 3, :]))
    y = m["f1_y"]
    k = 0
    for n in range(NB):
        sl = slice(n * BLK, (n + 1) * BLK)
        for e in range(NE):
            bank = e % 2
            wait(pe, used.get(("xm", k - 2)))
            for j in range(TPB):
                mm = pe.transpose(ps[:, bank, j * P:(j + 1) * P],
                                  mask[:, n * TPB + j, e:e + 1].broadcast_to([P, P]), m["ident"][:])
            wait(dve, c.PE.done(mm), used.get(("h", n - 1)))
            used[("xm", k)] = c.DVE.done(dve.tensor_tensor(m["f1_xm"][:, e, :], xnT[:, sl], ps[:, bank, :], ALU.mult))
            k += 1
        wait(pe, used[("xm", k - 1)])
        for f in range(FC):
            wait(pe, used.get(("g", n, f - 2)), used.get(("g", n - 1, f + 2)))
            for e in range(NE):
                pe.matmul(ps[:, 4 + f % 2, :], m["f1_w1"][:, e, f * P:(f + 1) * P], m["f1_xm"][:, e, :],
                          start=e == 0, stop=False)
            mm = c.PE.done(pe.matmul(ps[:, 4 + f % 2, :], m["f1_b1"][:, f * P:(f + 1) * P], m["f1_mt"][:, sl],
                                     start=False, stop=True))
            used[("h", n)] = mm
            wait(act, mm, used.get(("y", n - 1)))
            used[("g", n, f)] = c.ACT.done(act.activation(m["f1_h"][:, f, :], ps[:, 4 + f % 2, :], ACT.Gelu))
        wait(pe, used[("g", n, FC - 1)], used.get(("o", n - 1)))
        for j in range(TPB):
            for f in range(FC):
                mm = pe.matmul(ps[:, 6, j * P:(j + 1) * P], m["f1_h"][:, f, j * P:(j + 1) * P], m["f1_wo"][:, f, :],
                               start=f == 0, stop=f == FC - 1)
        used[("y", n)] = mm = c.PE.done(mm)
        wait(dve, mm)
        yb = y[:, n * TPB:(n + 1) * TPB, :]
        used[("o", n)] = c.dve_step(dve.tensor_tensor(yb, xn[:, n * TPB:(n + 1) * TPB, :],
                                                      ps[:, 6, :].rearrange("p (t d) -> p t d", d=D), ALU.add))
        z = c.dve_step(dve.tensor_tensor(yb, yb, m["f1_bo"][:].unsqueeze(1).broadcast_to([P, TPB, D]), ALU.add))
    layer_norm(c, y, y, 1e-12, (z,))
    wait(dve, (c.DVE, c.DVE.n))
    bc = lambda v: m[v][:].unsqueeze(1).broadcast_to([P, NT, D])
    c.dve_step(dve.tensor_tensor(y[:], y[:], bc("f1_gamma"), ALU.mult))
    c.dve_step(dve.tensor_tensor(y[:], y[:], bc("f1_beta"), ALU.add))
    return c.DVE.done(dve.tensor_tensor(x[:], x[:], y[:], ALU.add))


def ffn1_layout(a, out):
    out["f1_rw"] = a["L1_ffn_Wr"].T
    out["f1_w1"] = a["L1_ffn_W1"].transpose(1, 0, 2)
    out["f1_b1"] = a["L1_ffn_b1"]
    out["f1_wo"] = a["L1_ffn_Wo"].reshape(4, P, D).transpose(1, 0, 2)
    out["f1_bo"], out["f1_gamma"], out["f1_beta"] = a["L1_ffn_bo"], a["L1_ffn_gamma"], a["L1_ffn_beta"]


def program(nc, w, x_in, out):
    c = Core(nc)
    common_memory(c, w)
    x = c.mem["x"]
    xd = x_in.rearrange("(t p) d -> p t d", p=P)
    s_io = Progress(nc, "s_io")
    end = s_io.done(c.sp.dma_start(x[:], xd), 16)
    c.loaded(c.pe)
    for memory, stage in ((attn0_memory, attn0), (ffn0_memory, ffn0), (attn1_memory, attn1), (ffn1_memory, ffn1)):
        c.arena.reset()
        memory(c, w)
        end = stage(c, w, x, (end,))
        if stage is not ffn1:
            nc.all_engine_barrier()
    wait(c.sp, end)
    end = s_io.done(c.sp.dma_start(out.rearrange("(t p) d -> p t d", p=P), x[:]), 16)
    wait(c.sp, end)


def kernel(**inputs):
    import concourse.bacc as bacc
    from concourse.bass_utils import run_bass_kernel_spmd

    nc = bacc.Bacc("TRN2", target_bir_lowering=False, num_devices=1)
    arrays = layout(inputs)
    arrays["x"] = np.ascontiguousarray(inputs["L0_attn_hidden_states"]).reshape(T, D)
    aps = {k: nc.dram_tensor("in_" + k, v.shape, mybir.dt.from_np(v.dtype), kind="ExternalInput").ap()
           for k, v in arrays.items()}
    out = nc.dram_tensor("out", (T, D), F32, kind="ExternalOutput").ap()
    program(nc, aps, aps["x"], out)
    r = run_bass_kernel_spmd(nc, [{"in_" + k: v for k, v in arrays.items()}], core_ids=[0])
    return r.results[0]["out"].reshape(B, L, D)
```

```python
import numpy as np
import concourse.bass as bass
import concourse.mybir as mybir
from concourse.alu_op_type import AluOpType as ALU

F32 = mybir.dt.float32
BF16 = mybir.dt.bfloat16
ACT = mybir.ActivationFunctionType
X = mybir.AxisListType.X

P = 128
B, L, D = 2, 1024, 128
T = B * L
NT = T // P
NTB = L // P
BLK = 512
NB = T // BLK
TPB = BLK // P


class Progress:

    def __init__(self, nc, name):
        self.sem = nc.alloc_semaphore(name)
        self.n = 0

    def done(self, instruction, by=1):
        instruction.then_inc(self.sem, by)
        self.n += by
        return (self, self.n)


class Events:

    def __init__(self, nc, name, engine, credit=0, by=1):
        self.sem, self.credit, self.by = nc.alloc_semaphore(name), credit, by
        if credit:
            engine.sem_inc(self.sem, credit * by)

    def fire(self, instruction):
        return instruction.then_inc(self.sem, self.by)

    def wait(self, engine, k, alone=False):
        engine.wait_ge(self.sem, (k + (1 + self.credit)) * self.by)
        if alone:
            engine.sem_inc(self.unread, 1)


def wait(engine, *marks):
    for mark in marks:
        if mark is not None:
            engine.wait_ge(mark[0].sem, mark[1])


class Arena:

    def __init__(self, nc, words):
        self.t, self.words, self.top = nc.alloc_sbuf_tensor("arena", [P, words], F32), words, 0

    def reset(self):
        self.top = 0

    def take(self, shape, dtype=F32):
        n = int(np.prod(shape[1:]))
        words = (n + 1) // 2 if dtype == BF16 else n
        ap = self.t[0:shape[0], self.top:self.top + words]
        self.top += words
        assert self.top <= self.words, (self.top, self.words)
        if dtype != F32:
            ap = ap.bitcast(dtype)
        names = "abcde"[:len(shape) - 1]
        if len(names) > 1:
            ap = ap.rearrange("p (" + " ".join(names) + ") -> p " + " ".join(names), **dict(zip(names, shape[1:])))
        return ap


class Core:

    def keep(self, name, shape, dtype=F32):
        self.mem[name] = self.nc.alloc_sbuf_tensor(name, shape, dtype)

    def sb(self, name, shape, dtype=F32):
        self.mem[name] = self.arena.take(shape, dtype)
        return self.mem[name]

    def load(self, name, source, shape, dtype=F32):
        self.loads.done(self.sp.dma_start(self.sb(name, shape, dtype)[:], source), 16)

    def loaded(self, *engines):
        for engine in engines:
            engine.wait_ge(self.loads.sem, self.loads.n)

    def __init__(self, nc):
        self.mem = {}
        Events.unread = nc.alloc_semaphore("s_unread")
        self.loads = Progress(nc, "s_loads")
        self.nc = nc
        self.pe, self.dve, self.act, self.pool, self.sp = nc.tensor, nc.vector, nc.scalar, nc.gpsimd, nc.sync
        self.PE, self.DVE, self.ACT, self.POOL = (Progress(nc, "s_" + n) for n in ("pe", "dve", "act", "pool"))
        self.psum = nc.alloc_psum_tensor("psum", [P, 8, BLK], F32)

    def dve_step(self, instruction):
        m = self.DVE.done(instruction)
        wait(self.dve, m)
        return m

    def act_step(self, instruction):
        m = self.ACT.done(instruction)
        wait(self.act, m)
        return m


def layer_norm(c, x, xn, eps, lead, xnT=None, banks=(6, 7), out_at=None):
    bn, mv, rs, ident = c.mem["bn"], c.mem["mv"], c.mem["rs"], c.mem["ident"]
    wait(c.dve, *lead)
    for t in range(NT):
        last = c.DVE.done(c.dve.bn_stats(bn[:, t, :], x[:, t, :]))
    wait(c.dve, last)
    for t in range(NT):
        last = c.DVE.done(c.dve.bn_aggr(mv[:, t, :], bn[:, t, :]))
    wait(c.dve, last)
    ve = c.DVE.done(c.dve.tensor_scalar(rs[:], mv[:, :, 1], eps, None, ALU.add))
    wait(c.act, ve)
    root = c.ACT.done(c.act.activation(rs[:], rs[:], ACT.Sqrt))
    wait(c.dve, root)
    c.dve_step(c.dve.reciprocal(rs[:], rs[:]))
    marks = []
    for t in range(NT):
        m = c.DVE.done(c.dve.tensor_scalar(xn[:, t, :], x[:, t, :], mv[:, t, 0:1], rs[:, t:t + 1],
                                           ALU.subtract, ALU.mult))
        marks.append(m)
    if xnT is None:
        return marks
    outs = []
    for b in range(NB):
        bank = banks[b % len(banks)]
        wait(c.pe, marks[TPB * b + TPB - 1], outs[b - len(banks)] if b >= len(banks) else None)
        for j in range(TPB):
            m = c.pe.transpose(c.psum[:, bank, j * P:(j + 1) * P], xn[:, TPB * b + j, :], ident[:])
        m = c.PE.done(m)
        wait(c.act, m)
        outs.append(c.ACT.done(c.act.copy(out_at(b), c.psum[:, bank, :])))
    return outs


NE, F = 8, 512
FC = F // P
SLOTS = 4


def tiles_of(top):
    most = T * top // P + NE - 1
    return (most + SLOTS - 1) // SLOTS * SLOTS


def route(c, lg, bias, ready, top):
    s, dve, pe = c.mem, c.dve, c.pe
    lo, cmp, eq, rank, first, sel = s["lo"], s["cmp"], s["eq"], s["rank"], s["first"], s["sel"]
    wait(dve, ready)
    lgv = lg.rearrange("p (t e) -> p t e", e=NE)
    if bias is not None:
        c.dve_step(dve.tensor_tensor(lo[:], lgv, bias[:].unsqueeze(1).broadcast_to([P, NT, NE]), ALU.add))
    else:
        c.dve_step(dve.tensor_copy(lo[:], lgv))
    mine = lo[:].unsqueeze(3).broadcast_to([P, NT, NE, NE])
    other = lo[:].unsqueeze(2).broadcast_to([P, NT, NE, NE])
    c.DVE.done(dve.tensor_tensor(cmp[:], other, mine, ALU.is_gt))
    c.dve_step(dve.tensor_tensor(eq[:], other, mine, ALU.is_equal))
    lower = s["lower"][:].unsqueeze(1).broadcast_to([P, NT, NE * NE])
    eqf = eq[:].rearrange("p t a b -> p t (a b)")
    c.dve_step(dve.tensor_tensor(eqf, eqf, lower, ALU.mult))
    c.dve_step(dve.tensor_tensor(cmp[:], cmp[:], eq[:], ALU.add))
    c.dve_step(dve.tensor_reduce(rank[:], cmp[:], X, ALU.add))
    chosen = c.DVE.done(dve.tensor_scalar(sel[:], rank[:], float(top), None, ALU.is_lt))
    wait(pe, chosen, c.filled)
    wait(dve, c.filled)
    before, total = c.psum[:, 3, 0:NT * NE], c.psum[:, 4, 0:NT * NE]
    self_ = sel[:].rearrange("p t e -> p (t e)")
    pe.matmul(before, s["earlier"][:], self_, start=True, stop=True)
    counted = c.PE.done(pe.matmul(total, s["ones"][:], self_, start=True, stop=True))
    masks = [first]
    c.DVE.done(dve.tensor_scalar(first[:], rank[:], 0.0, None, ALU.is_equal))
    if top == 2:
        second, l1, l2, g1, g2, pick = (s[n] for n in ("second", "l1", "l2", "g1", "g2", "pick"))
        masks.append(second)
        c.dve_step(dve.tensor_scalar(second[:], rank[:], 1.0, None, ALU.is_equal))
        c.DVE.done(dve.tensor_tensor(pick[:], second[:], lo[:], ALU.mult))
        c.dve_step(dve.tensor_reduce(l1[:], lo[:], X, ALU.max))
        c.dve_step(dve.tensor_reduce(l2[:], pick[:], X, ALU.add))
        d = c.DVE.done(dve.tensor_tensor(l2[:], l2[:], l1[:], ALU.subtract))
        wait(c.act, d)
        gated = c.ACT.done(c.act.activation(l2[:], l2[:], ACT.Exp))
    wait(dve, counted)
    a, b = s["scan0"], s["scan1"]
    c.dve_step(dve.tensor_copy(a[:, NT + 1:2 * NT + 1, :], total.rearrange("p (t e) -> p t e", e=NE)))
    step = 1
    while step <= NT:
        c.dve_step(dve.tensor_tensor(b[:, NT:2 * NT + 1, :], a[:, NT:2 * NT + 1, :],
                                     a[:, NT - step:2 * NT + 1 - step, :], ALU.add))
        a, b, step = b, a, 2 * step
    count = a[:, 2 * NT, :].unsqueeze(2).broadcast_to([P, NE, NT])
    more, tiles, begin, end = s["more"], s["tiles"], s["begin"], s["end"]
    c.dve_step(dve.tensor_tensor(more[:], count, s["mult"][:].unsqueeze(1).broadcast_to([P, NE, NT]), ALU.is_gt))
    c.dve_step(dve.tensor_reduce(tiles[:], more[:], X, ALU.add))
    below = s["below"]
    c.dve_step(dve.tensor_tensor(below[:], s["lower"][:].rearrange("p (a b) -> p a b", b=NE),
                                 tiles[:].unsqueeze(1).broadcast_to([P, NE, NE]), ALU.mult))
    c.dve_step(dve.tensor_reduce(begin[:], below[:], X, ALU.add))
    c.DVE.done(dve.tensor_tensor(end[:], begin[:], tiles[:], ALU.add))
    c.dve_step(dve.tensor_scalar(begin[:], begin[:], float(P), None, ALU.mult))
    row, pick2 = s["row"], s["pick2"]
    c.dve_step(dve.tensor_tensor(row[:], a[:, NT:2 * NT, :], begin[:].unsqueeze(1).broadcast_to([P, NT, NE]), ALU.add))
    c.dve_step(dve.tensor_tensor(row[:], row[:], before.rearrange("p (t e) -> p t e", e=NE), ALU.add))
    for k, mask in enumerate(masks):
        c.DVE.done(dve.tensor_tensor(pick2[:, k], row[:], mask[:], ALU.mult))
    wait(dve, (c.DVE, c.DVE.n))
    rowf, slot = s["rowf"], s["slot"]
    c.dve_step(dve.tensor_reduce(rowf[:], pick2[:], X, ALU.add))
    placed = c.DVE.done(dve.tensor_copy(slot[:], rowf[:]))
    n = tiles_of(top)
    after, owner, expert = s["after"], s["owner"], s["expert"]
    c.dve_step(dve.tensor_tensor(after[:], s["index"][:].unsqueeze(2).broadcast_to([1, n, NE]),
                                 end[0:1, :].unsqueeze(1).broadcast_to([1, n, NE]), ALU.is_ge))
    c.dve_step(dve.tensor_reduce(owner[:], after[:], X, ALU.add))
    owned = c.DVE.done(dve.tensor_scalar(expert[:], owner[:], float(NE - 1), None, ALU.min))
    if top == 2:
        wait(dve, gated)
        c.dve_step(dve.tensor_scalar(g1[:], l2[:], 1.0, None, ALU.add))
        c.dve_step(dve.reciprocal(g1[:], g1[:]))
        c.dve_step(dve.tensor_tensor(g2[:], g1[:], l2[:], ALU.mult))
    return placed, owned


def scatter_rows(c, name, top, placed, rows, sorted_dram, zeroed):
    done = Progress(c.nc, name)
    wait(c.pool, placed, zeroed)
    for t in range(NT):
        for k in range(top):
            mark = done.done(c.pool.indirect_dma_start(
                sorted_dram, bass.IndirectOffsetOnAxis(ap=c.mem["slot"][:, k, t:t + 1], axis=0), rows[:, t, :], None), 16)
    return mark


def gather_rows(c, name, top, stored, sorted_dram, rows):
    for mark in stored:
        wait(c.pool, mark)
    marks = []
    for n in range(NB):
        done = Progress(c.nc, f"{name}{n}")
        for t in range(n * TPB, (n + 1) * TPB):
            for k in range(top):
                mark = done.done(c.pool.indirect_dma_start(
                    rows[:, k, t, :], None, sorted_dram,
                    bass.IndirectOffsetOnAxis(ap=c.mem["slot"][:, k, t:t + 1], axis=0)), 16)
        marks.append(mark)
    return marks


def expert_tiles(c, name, top, scattered, owned, weighted, src, dst, gated):
    ps, m = c.psum, c.mem
    pe, dve, act, sp = c.pe, c.dve, c.act, c.sp
    xs, xt, sg, h, ht, y = (m[n] for n in ("e_x", "e_xt", "e_sg", "e_h", "e_ht", "e_y"))
    wup, wdown, ident, expert = m["e_up"], m["e_down"], m["ident"], m["expert"]
    ev = lambda what, engine, credit=0, by=1: Events(c.nc, f"{name}_{what}", engine, credit, by)
    landed = [ev(f"landed{k}", sp, by=16) for k in range(SLOTS)]
    stored = [ev(f"stored{k}", sp, credit=1, by=16) for k in range(SLOTS)]
    turned = ev("turned", pe)
    copied = ev("copied", dve)
    first = ev("first", pe)
    last = ev("last", pe) if gated else first
    acted = ev("acted", act)
    hidden = ev("hidden", dve)
    rows = hidden if gated else acted
    hturned = ev("hturned", pe)
    hcopied = ev("hcopied", act)
    down = ev("down", pe)
    ready = ev("ready", dve, credit=2)
    n = tiles_of(top)
    wait(sp, scattered)
    wait(pe, owned, weighted)
    wait(dve, owned, weighted)
    wait(act, owned)
    for k in range(SLOTS):
        landed[k].fire(sp.dma_start(xs[:, k, :], src[k * P:(k + 1) * P, :]))

    def expert_of(engine, t):
        return engine.value_load(expert[0:1, bass.ds(t, 1)], min_val=0, max_val=NE - 1)

    def step(turn, k):
        s = turn * SLOTS + k
        peeled = isinstance(turn, int)
        there = lambda lag: not peeled or 0 <= s - lag < n
        tile = lambda lag: (s - lag, (k - lag) % 2, (k - lag) % SLOTS, turn + (k - lag) // SLOTS)
        if there(1):
            t, p, _, _ = tile(1)
            e = expert_of(pe, t)
            copied.wait(pe, t, alone=True)
            first.fire(pe.matmul(ps[:, p, :], xt[:, p, :], wup[:, bass.ds(e, 1), 0:F].rearrange("p a f -> p (a f)"),
                                 start=True, stop=True))
            if gated:
                first.wait(act, t)
                acted.fire(act.activation(sg[:, p, :], ps[:, p, :], ACT.Silu))
        if there(3):
            t, p, k3, turn3 = tile(3)
            e3 = expert_of(pe, t)
            yp = ps[:, 5 + 2 * p, 0:P]
            ready.wait(pe, t - 2)
            hcopied.wait(pe, t, alone=True)
            for f in range(FC):
                mm = pe.matmul(yp, ht[:, f * P:(f + 1) * P],
                               wdown[:, bass.ds(e3, 1) if gated else slice(0, 1), f * P:(f + 1) * P].rearrange("p a f -> p (a f)"),
                               start=f == 0, stop=f == FC - 1)
            down.fire(mm)
            down.wait(dve, t)
            stored[k3].wait(dve, turn3 - 1)
            ready.fire(dve.tensor_copy(y[:, k3, :], yp))
            ready.wait(sp, t)
            stored[k3].fire(sp.dma_start(dst[bass.ds(t * P, P), :], y[:, k3, :]))
        if there(2):
            t, p, _, _ = tile(2)
            rows.wait(pe, t)
            for f in range(FC):
                mm = pe.transpose(ps[:, 4, f * P:(f + 1) * P], h[:, p, f * P:(f + 1) * P], ident[:])
            hturned.fire(mm)
            hturned.wait(act, t)
            hcopied.fire(act.copy(ht[:], ps[:, 4, :]))
        if there(0):
            p = k % 2
            landed[k].wait(pe, turn)
            turned.fire(pe.transpose(ps[:, 6, 0:P], xs[:, k, :], ident[:]))
            turned.wait(dve, s)
            copied.fire(dve.tensor_copy(xt[:, p, :], ps[:, 6, 0:P]))
            if not peeled or s + SLOTS < n:
                turned.wait(sp, s)
                landed[k].fire(sp.dma_start(xs[:, k, :], src[bass.ds((s + SLOTS) * P, P), :]))
        if there(1):
            t, p, _, _ = tile(1)
            if gated:
                last.fire(pe.matmul(ps[:, 2 + p, :], xt[:, p, :],
                                    wup[:, bass.ds(e, 1), F:2 * F].rearrange("p a f -> p (a f)"), start=True, stop=True))
                last.wait(dve, t)
                acted.wait(dve, t)
                hidden.fire(dve.tensor_tensor(h[:, p, :], sg[:, p, :], ps[:, 2 + p, :], ALU.mult))
            else:
                eb = expert_of(dve, t)
                first.wait(dve, t, alone=True)
                hidden.fire(dve.tensor_tensor(sg[:, p, :], ps[:, p, :],
                                              m["e_bias"][:, bass.ds(eb, 1), :].rearrange("p a f -> p (a f)"), ALU.add))
                hidden.wait(act, t)
                acted.fire(act.activation(h[:, p, :], sg[:, p, :], ACT.Gelu))

    turns = n // SLOTS
    for k in range(SLOTS):
        step(0, k)
    with c.nc.Fori(1, turns - 1) as i:
        for k in range(SLOTS):
            step(i, k)
    for k in range(SLOTS + 3):
        step(turns - 1 + k // SLOTS, k % SLOTS)
    return [(e, (turns + 1) * 16) for e in stored]


def sorted_memory(c, w, top, up):
    n = tiles_of(top)
    for name, shape in (("lower", [P, NE * NE]), ("mult", [P, NT])):
        c.load(name, w[name].partition_broadcast(P), shape)
    c.load("earlier", w["earlier"], [P, P])
    c.load("index", w["index"][0:n].unsqueeze(0), [1, n])
    for name, shape in (("lo", [P, NT, NE]), ("cmp", [P, NT, NE, NE]), ("eq", [P, NT, NE, NE]), ("rank", [P, NT, NE]),
                        ("first", [P, NT, NE]), ("second", [P, NT, NE]), ("sel", [P, NT, NE]), ("pick", [P, NT, NE]),
                        ("l1", [P, NT]), ("l2", [P, NT]), ("g1", [P, NT]), ("g2", [P, NT]), ("ones", [P, P]),
                        ("scan0", [P, 2 * NT + 1, NE]), ("scan1", [P, 2 * NT + 1, NE]), ("more", [P, NE, NT]),
                        ("tiles", [P, NE]), ("begin", [P, NE]), ("end", [P, NE]), ("below", [P, NE, NE]),
                        ("row", [P, NT, NE]), ("pick2", [P, top, NT, NE]), ("rowf", [P, top, NT]),
                        ("after", [1, n, NE]), ("owner", [1, n]), ("e_x", [P, SLOTS, D]), ("e_xt", [P, 2, P]),
                        ("e_sg", [P, 2, F]), ("e_h", [P, 2, F]), ("e_ht", [P, F]), ("e_y", [P, SLOTS, D]),
                        ("e_back", [P, top, NT, D]), ("e_up", [P, NE, up])):
        c.sb(name, shape)
    c.sb("slot", [P, top, NT], mybir.dt.int32)
    c.sb("expert", [1, n], mybir.dt.int32)
    c.POOL.done(c.pool.memset(c.mem["ones"][:], 1.0))
    for name in ("scan0", "scan1"):
        c.POOL.done(c.pool.memset(c.mem[name][:], 0.0))
    c.filled = (c.POOL, c.POOL.n)


def ffn0_memory(c, w):
    sorted_memory(c, w, 2, 2 * F)
    c.load("f0_rw", w["f0_rw"], [D, NE])
    c.load("f0_rb", w["f0_rb"].partition_broadcast(P), [P, NE])
    c.sb("e_down", [P, NE, F])


def ffn0(c, w, x, lead):
    m = c.mem
    xn, xnT, back = m["xn"], m["xnT"], m["e_back"]
    weights = Progress(c.nc, "s_f0_weights")
    for name in ("up", "down"):
        weighted = weights.done(c.sp.dma_start(m["e_" + name][:], w["f0_" + name]), 16)
    outs = layer_norm(c, x, xn, 1e-5, lead, xnT, out_at=lambda b: xnT[:, b * BLK:(b + 1) * BLK])
    c.loaded(c.pe, c.dve)
    wait(c.pe, *outs)
    lg = c.psum[:, 2, 0:NT * NE]
    for t in range(NT):
        mm = c.pe.matmul(lg[:, t * NE:(t + 1) * NE], xnT[:, t * P:(t + 1) * P], m["f0_rw"][:], start=True, stop=True)
    placed, owned = route(c, lg, m["f0_rb"], c.PE.done(mm), 2)
    scattered = scatter_rows(c, "s_f0_scattered", 2, placed, xn, c.sorted_x, c.zeroed)
    stores = expert_tiles(c, "s_f0", 2, scattered, owned, weighted, c.sorted_x, c.sorted_y, True)
    marks = gather_rows(c, "s_f0_back", 2, stores, c.sorted_y, back)
    for n, mark in enumerate(marks):
        wait(c.dve, mark)
        for k, gate in enumerate((m["g1"], m["g2"])):
            for t in range(n * TPB, (n + 1) * TPB):
                end = c.DVE.done(c.dve.scalar_tensor_tensor(x[:, t, :], back[:, k, t, :], gate[:, t:t + 1], x[:, t, :],
                                                            ALU.mult, ALU.add))
            wait(c.dve, end)
    return end


def common_memory(c, w):
    for n, shape in (("x", [P, NT, D]), ("xn", [P, NT, D]), ("xnT", [P, T + 8]), ("bn", [P, NT, 6]),
                     ("mv", [P, NT, 2]), ("rs", [P, NT]), ("ident", [P, P])):
        c.keep(n, shape)
    c.loads.done(c.sp.dma_start(c.mem["ident"][:], w["ident"]), 16)
    c.arena = Arena(c.nc, 45000)
    n = tiles_of(2)
    c.sorted_x = c.nc.dram_tensor("sorted_x", (n * P, D), F32).ap()
    c.sorted_y = c.nc.dram_tensor("sorted_y", (n * P, D), F32).ap()
    c.keep("zero", [P, D])
    zero = c.POOL.done(c.pool.memset(c.mem["zero"][:], 0.0))
    wait(c.act, zero)
    c.sorted_y1 = c.nc.dram_tensor("sorted_y1", (tiles_of(1) * P, D), F32).ap()
    c.sorted_x1 = c.nc.dram_tensor("sorted_x1", (tiles_of(1) * P, D), F32).ap()
    zeros = Progress(c.nc, "s_zeros1")
    c.zeroed1 = zeros.done(c.act.dma_start(c.sorted_x1.rearrange("(k p) d -> p k d", p=P),
                                           c.mem["zero"][:].unsqueeze(1).broadcast_to([P, tiles_of(1), D])), 16)
    zeros = Progress(c.nc, "s_zeros")
    c.zeroed = zeros.done(c.act.dma_start(c.sorted_x.rearrange("(k p) d -> p k d", p=P),
                                          c.mem["zero"][:].unsqueeze(1).broadcast_to([P, n, D])), 16)


def layout(inputs):
    a = {k: np.asarray(v) for k, v in inputs.items()}
    out = {"ident": np.eye(P, dtype=np.float32)}
    out["lower"] = np.tril(np.ones((NE, NE), np.float32), -1).reshape(-1)
    out["earlier"] = np.triu(np.ones((P, P), np.float32), 1)
    out["mult"] = np.arange(NT, dtype=np.float32) * P
    out["index"] = np.arange(tiles_of(2), dtype=np.float32)
    gw = a["L0_ffn_gate_w"].transpose(2, 0, 1)
    uw = a["L0_ffn_up_w"].transpose(2, 0, 1)
    out["f0_up"] = np.concatenate([gw, uw], axis=2)
    out["f0_down"] = a["L0_ffn_down_w"].transpose(0, 2, 1).reshape(NE, FC, P, D).transpose(2, 0, 1, 3).reshape(P, NE, F)
    out["f0_rw"] = a["L0_ffn_router_w"].T
    out["f0_rb"] = a["L0_ffn_router_b"]
    attn1_layout(a, out)
    attn0_layout(a, out)
    ffn1_layout(a, out)
    return {k: np.ascontiguousarray(v) for k, v in out.items()}


NH, HD = 16, 8
NG = 4
HG = NH // NG
KR = 9 * HD
KA = KR + 3
QH = L // BLK


def attn1_memory(c, w):
    for n in ("wq", "wqs", "wk", "wks", "wv", "wo"):
        c.load("a1_" + n, w["a1_" + n], [D, D])
    c.load("a1_bcol", w["a1_bcol"], [D, 4])
    c.load("a1_bv", w["a1_bv"].partition_broadcast(P), [P, D])
    c.load("a1_bo", w["a1_bo"].partition_broadcast(P), [P, D])
    c.load("a1_cos", w["a1_cos"], [D, L]); c.load("a1_sin", w["a1_sin"], [D, L])
    c.sb("identb", [P, P], BF16)
    c.sb("a1_t", [P, 2, 2, BLK])
    c.sb("a1_part", [P, 2, 3, BLK], BF16)
    c.sb("a1_v", [P, NT, D])
    c.sb("a1_q", [P, NG, HG, L], BF16); c.sb("a1_k", [P, NG, HG, L], BF16)
    c.sb("a1_va", [P, NTB, NH, 32])
    c.sb("a1_p", [P, 2 * HG, BLK])
    c.sb("a1_o", [P, B * NG * QH, BLK])
    c.sb("a1_mx", [P, 2, HG * 4]); c.sb("a1_mr", [P, HG * 4]); c.sb("a1_ms", [P, 3, HG * 4], BF16)
    c.sb("a1_mt", [3 * HG * 4, P], BF16)
    c.sb("a1_rd", [P, 2, 4, HG])


def attn1(c, w, x, lead):
    nc, ps, m = c.nc, c.psum, c.mem
    pe, dve, act, pool, sp = c.pe, c.dve, c.act, c.pool, c.sp
    xn, xnT = m["xn"], m["xnT"]
    scr_q = nc.dram_tensor("scr_q", [NH, 9, HD, T], BF16, kind="Internal").ap()
    scr_k = nc.dram_tensor("scr_k", [NH, 9, HD, T], BF16, kind="Internal").ap()
    scr_m = nc.dram_tensor("scr_m", [2, 3, HG, 4, P], BF16, kind="Internal").ap()
    outs = layer_norm(c, x, xn, 1e-5, lead, xnT, out_at=lambda b: xnT[:, b * BLK:(b + 1) * BLK])
    c.loaded(c.pe, c.dve, c.act, c.pool)
    va, v = m["a1_va"], m["a1_v"]
    c.POOL.done(pool.memset(va[:], 0.0))
    wait(pool, (c.POOL, c.POOL.n))
    ones_v = c.POOL.done(pool.memset(va[:, :, :, HD:HD + 1], 1.0))
    ones_k = c.DVE.done(dve.memset(m["a1_k"][64:96, :, :, :], 1.0))
    idb = c.DVE.done(dve.tensor_copy(m["identb"][:], m["ident"][:]))
    stored = {}
    s_st = [Progress(nc, f"s_a1_st{k}") for k in range(2)]
    used = {}
    n = 0
    for b in range(NB):
        xs = xnT[:, b * BLK:(b + 1) * BLK]
        lpos = (b * BLK) % L
        wait(pe, outs[b])
        for what, (w1, w2, b1, scr) in enumerate((("a1_wq", "a1_wqs", 0, scr_q), ("a1_wk", "a1_wks", 2, scr_k))):
            k = n % 2
            bank = 2 * k
            wait(pe, used.get(n - 2, {}).get("t"))
            pe.matmul(ps[:, bank, :], m[w1][:], xs, start=True, stop=True)
            mp = c.PE.done(pe.matmul(ps[:, bank + 1, :], m[w2][:], xs, start=True, stop=True))
            t, part = m["a1_t"][:, k], m["a1_part"][:, k]
            wait(dve, mp, used.get(n - 2, {}).get("split"))
            c.DVE.done(dve.scalar_tensor_tensor(t[:, 0, :], ps[:, bank, :], m["a1_bcol"][:, b1:b1 + 1],
                                                m["a1_cos"][:, lpos:lpos + BLK], ALU.add, ALU.mult))
            tt = c.dve_step(dve.scalar_tensor_tensor(t[:, 1, :], ps[:, bank + 1, :], m["a1_bcol"][:, b1 + 1:b1 + 2],
                                                     m["a1_sin"][:, lpos:lpos + BLK], ALU.add, ALU.mult))
            r0 = c.DVE.done(dve.tensor_tensor(t[:, 0, :], t[:, 0, :], t[:, 1, :], ALU.add))
            wait(act, r0, used.get(n - 2, {}).get("stored"))
            h0 = c.ACT.done(act.copy(part[:, 0, :], t[:, 0, :]))
            wait(pool, h0)
            r1 = c.POOL.done(pool.tensor_tensor(t[:, 1, :], t[:, 0, :], part[:, 0, :], ALU.subtract))
            wait(act, r1)
            h1 = c.ACT.done(act.copy(part[:, 1, :], t[:, 1, :]))
            wait(pool, h1)
            r2 = c.POOL.done(pool.tensor_tensor(part[:, 2, :], t[:, 1, :], part[:, 1, :], ALU.subtract))
            wait(sp, h0, h1, r2)
            for pt in range(3):
                for rep in range(3):
                    row = 3 * pt + rep if what == 0 else 3 * rep + pt
                    ms = s_st[k].done(sp.dma_start(scr[:, row, :, b * BLK:(b + 1) * BLK], part[:, pt, :]), 16)
            used[n] = {"t": tt, "split": r2, "stored": ms}
            n += 1
        bank = 4 + b % 2
        wait(pe, used.get(("v", b - 2)))
        for j in range(TPB):
            mm = pe.matmul(ps[:, bank, j * D:(j + 1) * D], xnT[:, (b * TPB + j) * P:(b * TPB + j + 1) * P],
                           m["a1_wv"][:], start=True, stop=True)
        mm = c.PE.done(mm)
        wait(dve, mm)
        used[("v", b)] = c.DVE.done(dve.tensor_tensor(
            v[:, b * TPB:(b + 1) * TPB, :], ps[:, bank, :].rearrange("p (t d) -> p t d", d=D),
            m["a1_bv"][:].unsqueeze(1).broadcast_to([P, TPB, D]), ALU.add))
    vdone = used[("v", NB - 1)]
    wait(pe, vdone, tt, idb)
    wait(sp, (s_st[0], s_st[0].n), (s_st[1], s_st[1].n))
    wait(sp, ones_k)
    wait(pool, vdone)
    wait(pe, ones_v)
    wait(dve, ones_v)

    U = 2 * NTB
    s_load = [Events(nc, f"s_a1_load{k}", sp, by=32) for k in range(NG)]
    s_s1 = Events(nc, "s_a1_s1", pe)
    s_red = Events(nc, "s_a1_red", dve, credit=2)
    s_neg = Events(nc, "s_a1_neg", dve)
    s_mt = Events(nc, "s_a1_mt", pe)
    s_mc = Events(nc, "s_a1_mc", dve, credit=1)
    s_ms = Events(nc, "s_a1_ms", sp, credit=1, by=16)
    s_mrow = [Events(nc, f"s_a1_mrow{k}", sp, credit=1, by=16) for k in range(2)]
    s_s2 = Events(nc, "s_a1_s2", pe)
    s_exp = Events(nc, "s_a1_exp", act, credit=4)
    s_va = Events(nc, "s_a1_va", pool)
    s_pv = Events(nc, "s_a1_pv", pe, credit=U + 2)
    s_o = Events(nc, "s_a1_o", act, credit=1)
    q, kk, pt, o = m["a1_q"], m["a1_k"], m["a1_p"], m["a1_o"]
    mx, mr, msp, mt = m["a1_mx"], m["a1_mr"], m["a1_ms"], m["a1_mt"]
    chain = Events(nc, "s_a1_chain", dve)
    links = [0]

    def load(bsel, g, k):
        for dst, scr in ((q, scr_q), (kk, scr_k)):
            src = scr[k * HG:(k + 1) * HG].rearrange("h r d (b t) -> b (r d) h t", b=B)[bsel]
            if not isinstance(bsel, int):
                src = src.rearrange("o r h t -> (o r) h t")
            sp.dma_start(dst[0:KR, k, :, :], src).then_inc(s_load[k].sem, 16)

    def max_tile(st, k, n, t):
        qh, h, qt = t // 16, (t % 16) // 4, t % 4
        bank = 3 + 2 * (t % 2)
        s_red.wait(pe, st * 32 + (t - 2))
        if t % 16 == 0:
            s_mc.wait(pe, st * 2 + (qh - 1))
        for half in range(2):
            mm = pe.matmul(ps[:, bank + half, :], q[0:KR, k, h, (qh * 4 + qt) * P:(qh * 4 + qt + 1) * P],
                           kk[0:KR, k, h, half * BLK:(half + 1) * BLK], start=True, stop=True)
        s_s1.fire(mm)
        s_s1.wait(dve, st * 32 + t)
        s_red.fire(dve.tensor_reduce(mx[:, qh, h * 4 + qt:h * 4 + qt + 1],
                                       ps[:, bank:bank + 2, :].rearrange("p a b -> p (a b)"), X, ALU.max))

    def max_rows(st, k, qh):
        e = st * 2 + qh
        s_red.wait(dve, st * 32 + (16 * qh + 15))
        a = chain.fire(dve.tensor_scalar(msp[:, 0, :], mx[:, qh, :], -1.0, None, ALU.mult))
        chain.wait(dve, e * 3 + 0)
        chain.fire(dve.scalar_tensor_tensor(mr[:], mx[:, qh, :], -1.0, msp[:, 0, :], ALU.mult, ALU.subtract))
        chain.wait(dve, e * 3 + 1)
        chain.fire(dve.tensor_copy(msp[:, 1, :], mr[:]))
        chain.wait(dve, e * 3 + 2)
        s_neg.fire(dve.tensor_tensor(msp[:, 2, :], mr[:], msp[:, 1, :], ALU.subtract))
        s_neg.wait(pe, e)
        s_red.wait(pe, st * 32 + (16 * qh + 15), alone=True)
        tp = ps[0:48, 3, 0:64].bitcast(BF16)
        s_mt.fire(pe.transpose(tp, msp[:].rearrange("p a b -> p (a b)"), m["identb"][:]))
        s_mt.wait(dve, e)
        s_ms.wait(dve, e - 1)
        s_mc.fire(dve.tensor_copy(mt[:], tp))
        s_mc.wait(sp, e)
        s_mrow[qh].wait(sp, st - 1)
        s_ms.fire(sp.dma_start(scr_m[qh].rearrange("a h t q -> (a h t) q"), mt[:]))
        s_ms.wait(sp, e)
        s_mrow[qh].fire(sp.dma_start(q[KR:KA, k, :, qh * BLK:(qh + 1) * BLK],
                                       scr_m[qh].rearrange("a h t q -> a h (t q)")))

    def step(st, k, i, kn, bsel2, first=False):
        k2 = (k + 2) % NG
        s_pv.wait(sp, (st - 1) * U - 1)
        load(bsel2, st, k2)
        s_pv.wait(pool, st * U - 2)
        s_va.fire(pool.tensor_copy(
            va[:, :, k * HG:(k + 1) * HG, 0:HD],
            v[:, bass.ds(i * NTB, NTB), k * HG * HD:(k + 1) * HG * HD].rearrange("p t (h d) -> p t h d", d=HD)))
        s_va.wait(pe, st)
        s_load[kn].wait(pe, i + (1 if kn == 0 else 0))
        for u in range(U + 1):
            qh, kb = divmod(u, NTB)
            if u < U:
                if u == NTB:
                    max_rows(st + 1, kn, 0)
                if kb == 0:
                    s_mrow[qh].wait(pe, st)
                for h in range(HG):
                    n = u * HG + h
                    bank = n % 3
                    s_exp.wait(pe, st * (U * HG) + (n - 3 if n else n - 1))
                    s_s2.fire(pe.matmul(ps[:, bank, :], kk[0:KA, k, h, kb * P:(kb + 1) * P],
                                          q[0:KA, k, h, qh * BLK:(qh + 1) * BLK], start=True, stop=True))
                    s_s2.wait(act, st * (U * HG) + n)
                    if h == 0:
                        s_pv.wait(act, st * U + (u - 2))
                    s_exp.fire(act.activation(pt[:, (u % 2) * HG + h, :], ps[:, bank, :], ACT.Exp,
                                                scale=float(HD) ** -0.5))
                    if h % 2 == 1:
                        t = 2 * u + h // 2
                        max_tile(st + 1, kn, 0, t)
            if u >= 1:
                uu = u - 1
                qh1, kb1 = divmod(uu, NTB)
                s_exp.wait(pe, st * (U * HG) + (uu * HG + HG - 1))
                if kb1 == 0:
                    s_o.wait(pe, st * QH + (qh1 - 1))
                for h in range(HG):
                    mm = pe.matmul(ps[32 * h:32 * h + 32, 7, :], va[:, kb1, k * HG + h, :],
                                   pt[:, (uu % 2) * HG + h, :], start=kb1 == 0, stop=kb1 == NTB - 1,
                                   skip_group_check=True)
                s_pv.fire(mm)
                if kb1 == NTB - 1:
                    s_pv.wait(act, st * U + uu, alone=True)
                    s_o.fire(act.copy(o[:, bass.ds(i * (NG * QH) + (k * QH + qh1), 1), :]
                                        .rearrange("p o q -> p (o q)"), ps[:, 7, :]))
        max_rows(st + 1, kn, 1)

    load(0, 0, 0)
    load(0, 1, 1)
    s_load[0].wait(pe, 0)
    for t in range(32):
        max_tile(0, 0, 0, t)
        if t % 16 == 15:
            max_rows(0, 0, t // 16)
    with nc.Fori(0, B) as i:
        for k in range(NG):
            bsel2 = bass.ds(i, 1) if k < 2 else bass.ds(i * -1 + 1, 1)
            step(i * NG + k, k, i, (k + 1) % NG, bsel2)
    G = B * NG
    for k in range(NG):
        s_load[k].wait(sp, 2 if k < 2 else 1)
    for qh in range(2):
        s_mrow[qh].wait(sp, G)
    s_o.wait(pe, G * QH - 1)
    s_red.wait(pe, (G + 1) * 32 - 1)
    s_exp.wait(pe, G * U * HG - 1)
    s_mc.wait(pe, 2 * G + 1)
    s_red.wait(dve, (G + 1) * 32 - 1)
    at = xn
    rd = m["a1_rd"]
    done = {}
    for n in range(G * QH):
        b, g, qh = n // (NG * QH), n // QH % NG, n % QH
        bank = n % 2
        wait(pe, done.get(n - 2))
        for j in range(4):
            mm = pe.transpose(ps[:, bank, j * P:(j + 1) * P], o[:, n, j * P:(j + 1) * P], m["ident"][:])
        mm = c.PE.done(mm)
        wait(dve, mm)
        sums = ps[:, bank, :].rearrange("p (t h d) -> p t h d", t=4, d=32)
        c.dve_step(dve.reciprocal(rd[:, n % 2], sums[:, :, :, HD]))
        tile0 = b * NTB + qh * 4
        done[n] = c.DVE.done(dve.tensor_tensor(
            at[:, tile0:tile0 + 4, g * 32:(g + 1) * 32].rearrange("p t (h d) -> p t h d", d=HD),
            sums[:, :, :, 0:HD], rd[:, n % 2].unsqueeze(3).broadcast_to([P, 4, HG, HD]), ALU.mult))
    last = {}
    for b in range(NB):
        bank, bank2 = 2 + b % 2, 4 + b % 2
        wait(pe, done[G * QH - 1], last.get(("c", b - 2)), last.get(("y", b - 2)))
        for j in range(TPB):
            mm = pe.transpose(ps[:, bank, j * P:(j + 1) * P], at[:, b * TPB + j, :], m["ident"][:])
        wait(act, c.PE.done(mm))
        last[("c", b)] = cc = c.ACT.done(act.copy(xnT[:, b * BLK:(b + 1) * BLK], ps[:, bank, :]))
        wait(pe, cc)
        for j in range(TPB):
            mm = pe.matmul(ps[:, bank2, j * D:(j + 1) * D], xnT[:, (b * TPB + j) * P:(b * TPB + j + 1) * P],
                           m["a1_wo"][:], start=True, stop=True)
        wait(dve, c.PE.done(mm))
        xb = x[:, b * TPB:(b + 1) * TPB, :]
        y = c.dve_step(dve.tensor_tensor(xb, xb, ps[:, bank2, :].rearrange("p (t d) -> p t d", d=D), ALU.add))
        last[("y", b)] = y
        end = c.DVE.done(dve.tensor_tensor(xb, xb, m["a1_bo"][:].unsqueeze(1).broadcast_to([P, TPB, D]), ALU.add))
    return end


def attn1_layout(a, out):
    swap = np.arange(D).reshape(-1, 2)[:, ::-1].reshape(-1)
    for n in ("q", "k"):
        out[f"a1_w{n}"] = a[f"L1_attn_W{n}"].T
        out[f"a1_w{n}s"] = a[f"L1_attn_W{n}"][swap].T
    out["a1_wv"] = a["L1_attn_Wv"].T
    out["a1_wo"] = a["L1_attn_Wo"].T
    bq, bk = a["L1_attn_bq"], a["L1_attn_bk"]
    out["a1_bcol"] = np.stack([bq, bq[swap], bk, bk[swap]], 1)
    out["a1_bv"], out["a1_bo"] = a["L1_attn_bv"], a["L1_attn_bo"]
    f = np.float32
    inv = (f(1.0) / f(10000.0) ** (np.arange(0, HD, 2, dtype=f) / f(HD))).astype(f)
    ang = np.repeat(np.arange(L, dtype=f)[:, None] * inv[None, :], 2, axis=1).T
    sign = np.where(np.arange(HD) % 2 == 0, f(-1), f(1))[:, None]
    out["a1_cos"] = np.tile(np.cos(ang), (NH, 1)).astype(f)
    out["a1_sin"] = np.tile(np.sin(ang) * sign, (NH, 1)).astype(f)


H0, DK = 4, 32
CH = 32
NCH = L // CH
S6 = 6
PAD = 32
QT, KTOK, KBTOK, VBTOK, TT, AT = range(6)


def attn0_memory(c, w):
    for n, shape in (("w3", [D, 3, D]), ("bw", [D, D]), ("w1x", [D, D]), ("w1s", [P, D]), ("w2", [D, 24]),
                     ("b1", [D, 1]), ("ow", [D, D]), ("onorm", [D, 1]), ("fw1", [D, 1]), ("fw", [P, 44]),
                     ("heads", [P, P]), ("sel", [P, S6, 32]), ("strict", [P, CH]), ("incl", [P, CH]), ("diag", [P, CH])):
        c.load("a0_" + n, w["a0_" + n], shape)
    c.load("a0_b2", w["a0_b2"].partition_broadcast(P), [P, 24])
    c.load("a0_temp", w["a0_temp"].partition_broadcast(P), [P, H0])
    c.load("a0_eye", w["a0_eye"].partition_broadcast(P), [P, CH * CH])
    c.sb("a0_wf", [D, 3, 4, D])
    c.sb("a0_wfir", [P, 44, 32]); c.sb("a0_eps", [P, 2])
    c.sb("a0_tt", [P, 3, H0]); c.sb("a0_lo", [P, NT, 24]); c.sb("a0_m", [P, NT * H0]); c.sb("a0_zero", [P, P])


def attn0(c, w, x, lead):
    nc, ps, m = c.nc, c.psum, c.mem
    pe, dve, act, pool, sp = c.pe, c.dve, c.act, c.pool, c.sp
    PE, DVE, AC, PO = c.PE, c.DVE, c.ACT, c.POOL
    a = c.arena
    arena0 = a.top
    u1 = a.take([P, H0 * B * (PAD + L)])
    kk = u1[:, 0:3 * T].rearrange("p (s t) -> p s t", s=3)
    am = u1[:, 3 * T:4 * T].rearrange("p (b n j) -> p b n j", b=B, j=CH)
    v4 = u1.rearrange("p (g b t) -> p g b t", g=H0, b=B)
    bt = a.take([P, T])
    asub = bt.rearrange("p (b i j) -> p b i j", b=B, i=CH)
    ttf = a.take([P, B * CH * CH])
    tt = ttf.rearrange("p (b i j) -> p b i j", b=B, i=CH)
    taps = ttf[:, 0:12 * D].rearrange("p (s j d) -> p s j d", s=3, j=4)
    c.loads.done(sp.dma_start(ttf[:, 0:12 * D], w["a0_taps"].partition_broadcast(P)), 16)
    opf = a.take([P, (NCH + 1) * B * 6 * CH])
    op = opf.rearrange("p (n b o i) -> p n b o i", b=B, o=6, i=CH)
    wexp = opf[:, 0:NT * S6 * D].rearrange("p (t s f) -> p t s f", t=NT, s=S6)
    br = a.take([P, S6, T])
    sqf = a.take([P, 2 * BLK])
    sq = sqf.rearrange("p (k t) -> p k t", k=2)
    kbuf = sqf[:, 0:6 * P].rearrange("p (b s t) -> p b s t", b=2, s=3)
    xn, xf = m["xn"], m["xnT"]
    xp = xf[:, 0:B * (L + 3)].rearrange("p (b t) -> p b t", b=B)
    xnd = xn[:].rearrange("p t d -> p (t d)")
    scr_a = nc.dram_tensor("scr_a", [B, NCH, H0, CH, CH], F32, kind="Internal").ap()
    scr_t = nc.dram_tensor("scr_t", [B, NCH, H0, CH, CH], F32, kind="Internal").ap()

    c.loaded(pe, dve, act, pool)
    DVE.done(dve.memset(xp[:, :, 0:3], 0.0))
    DVE.done(dve.memset(m["a0_eps"][:, 0:1], 1e-6))
    DVE.done(dve.memset(m["a0_eps"][:, 1:2], 1e-5))
    DVE.done(dve.memset(m["a0_zero"][:], 0.0))
    wfd = DVE.done(dve.tensor_tensor(m["a0_wf"][:], m["a0_w3"][:].unsqueeze(2).broadcast_to([D, 3, 4, D]),
                                     taps, ALU.mult))
    zop = PO.done(pool.memset(op[:, NCH], 0.0))
    outs = layer_norm(c, x, xn, 1e-5, lead, xf,
                      out_at=lambda b: xp[:, b // 2, 3 + b % 2 * BLK:3 + b % 2 * BLK + BLK])
    wait(pe, *outs, wfd)
    read, vdone, qk = {}, [], []
    for n in range(NB):
        b, t0, sl = n // 2, n % 2 * BLK, slice(n * BLK, (n + 1) * BLK)
        base = 4 * (n % 2)
        wait(pe, read.get(n - 2))
        for s in range(3):
            for j in range(4):
                mm = pe.matmul(ps[:, base + s, :], m["a0_wf"][:, s, j, :], xp[:, b, t0 + j:t0 + j + BLK],
                               start=j == 0, stop=j == 3)
            mm = PE.done(mm)
            wait(act, mm)
            dst = kk[:, s, sl] if s < 2 else br[:, 5, sl]
            q = AC.done(act.activation(dst, ps[:, base + s, :], ACT.Silu))
        vdone.append(q)
        mm = PE.done(pe.matmul(ps[:, base + 3, :], m["a0_bw"][:], xp[:, b, 3 + t0:3 + t0 + BLK], start=True, stop=True))
        wait(act, mm)
        read[n] = AC.done(act.activation(bt[:, sl], ps[:, base + 3, :], ACT.Tanh, scale=0.5))
    wait(dve, read[NB - 1])
    c.dve_step(dve.tensor_scalar(bt[:], bt[:], 0.5, 0.5, ALU.mult, ALU.add))
    banks = {}
    for n in range(2 * NB):
        s, sl = n // NB, slice(n % NB * BLK, (n % NB + 1) * BLK)
        wait(act, banks.get(n - 2))
        z = AC.done(act.activation(sq[:, n % 2, :], kk[:, s, sl], ACT.Square))
        wait(pe, z)
        banks[n] = PE.done(pe.matmul(ps[:, n, :], m["a0_heads"][:], sq[:, n % 2, :], start=True, stop=True))
    wait(act, banks[2 * NB - 1])
    for n in range(2 * NB):
        z = AC.done(act.activation(ps[:, n, :], ps[:, n, :], ACT.Ln, bias=m["a0_eps"][:, 0:1]))
    wait(act, z)
    for n in range(2 * NB):
        s, b, half, sl = n // NB, n % NB // 2, n % 2, slice(n % NB * BLK, (n % NB + 1) * BLK)
        z = AC.done(act.activation(ps[:, n, :], ps[:, n, :], ACT.Exp, scale=-0.5))
        wait(dve, z)
        qk.append(DVE.done(dve.tensor_tensor(kk[:, s, sl], kk[:, s, sl], ps[:, n, :], ALU.mult)))
    wait(pool, qk[NB - 1])
    for b in range(B):
        qcopy = PO.done(pool.tensor_copy(op[:, 0:NCH, b, QT, :],
                                         kk[:, 0, b * L:(b + 1) * L].rearrange("p (n i) -> p n i", i=CH)))
    wait(dve, qk[-1])
    c.dve_step(dve.tensor_tensor(kk[:, 2, :], kk[:, 1, :], bt[:], ALU.mult))
    kb = (DVE, DVE.n)
    vb = c.dve_step(dve.tensor_tensor(xnd, br[:, 5, :], bt[:], ALU.mult))

    s_kbuf = Events(nc, "s_a0_kbuf", act)
    s_ap = Events(nc, "s_a0_ap", pe, credit=2)
    s_am = Events(nc, "s_a0_am", dve, credit=2)
    wait(act, kb)
    wait(pe, (DVE, DVE.n))
    with nc.Fori(0, NCH // 4) as i:
        for b in range(B):
            n = i * B + b
            s_ap.wait(act, n - 2, alone=True)
            s_kbuf.fire(act.copy(kbuf[:, b], kk[:, :, bass.ds(i * P + b * L, P)]))
            s_kbuf.wait(pe, n, alone=True)
            s_am.wait(pe, n - 2, alone=True)
            for cc in range(4):
                for out, lh, rh in ((0, 2, 1), (1, 1, 0)):
                    for h in range(H0):
                        hs, cs = slice(32 * h, 32 * h + 32), slice(cc * CH, (cc + 1) * CH)
                        mm = pe.matmul(ps[hs, 2 * b + out, cs], kbuf[hs, b, lh, cs], kbuf[hs, b, rh, cs],
                                       start=True, stop=True, skip_group_check=True)
            s_ap.fire(mm)
            s_ap.wait(dve, n)
            for out, mask, dst in ((0, "a0_strict", am[:, b, bass.ds(i * 4, 4), :]),
                                   (1, "a0_incl", op[:, bass.ds(i * 4, 4), b, AT, :])):
                z = dve.tensor_tensor(dst, ps[:, 2 * b + out, 0:4 * CH].rearrange("p (n j) -> p n j", j=CH),
                                      m[mask][:].unsqueeze(1).broadcast_to([P, 4, CH]), ALU.mult)
            s_am.fire(z)
    s_rel = Progress(nc, "s_a0_rel")
    s_am.wait(sp, B * NCH // 4 - 1)
    for b in range(B):
        for h in range(H0):
            z = s_rel.done(sp.dma_start(scr_a[b, :, h].rearrange("n i j -> i n j"), am[32 * h:32 * h + 32, b]), 16)
    wait(sp, z)
    for b in range(B):
        z = s_rel.done(sp.dma_start(asub[:, b].rearrange("p i j -> p (i j)"),
                                    scr_a[b].rearrange("n h i j -> (n h) (i j)")), 16)
    a_in = z
    for b in range(B):
        ts = slice(b * L, (b + 1) * L)
        for item, src in ((KTOK, kk[:, 1, ts]), (KBTOK, kk[:, 2, ts]), (VBTOK, xnd[:, ts])):
            z = DVE.done(dve.transpose(op[:, 0:NCH, b, item, :], src.rearrange("p (n i) -> p n i", i=CH)))
    tok = z
    s_v4 = Progress(nc, "s_a0_v4")
    wait(pool, a_in, qcopy, tok)
    s_ap.wait(pool, B * NCH // 4 - 1)
    zv = PO.done(pool.memset(v4[:, :, :, 0:PAD + 4], 0.0))
    wait(sp, zv, vdone[-1])
    for j in range(4):
        for g in range(H0):
            z = s_v4.done(sp.dma_start(v4[32 * j:32 * j + 32, g, :, PAD + j:PAD + L],
                                       br[32 * g:32 * g + 32, 5, :].rearrange("p (b t) -> p b t", b=B)[:, :, 0:L - j]), 16)
    v4_in = z
    eye = m["a0_eye"][:].rearrange("p (i j) -> p i j", i=CH).unsqueeze(1).broadcast_to([P, B, CH, CH])
    c.dve_step(dve.tensor_copy(tt, eye))
    wf = DVE.done(dve.tensor_tensor(
        m["a0_wfir"][:], m["a0_fw"][:].unsqueeze(2).broadcast_to([P, 44, 32]),
        m["a0_diag"][:].unsqueeze(1).broadcast_to([P, 44, 32]), ALU.mult))
    wait(dve, a_in)
    prod = xnd.rearrange("p (b i j) -> p b i j", b=B, i=CH)
    for i in range(1, CH):
        c.dve_step(dve.tensor_tensor(prod[:, :, 0:i, 0:i], asub[:, :, i, 0:i].unsqueeze(2).broadcast_to([P, B, i, i]),
                                     tt[:, :, 0:i, 0:i], ALU.mult))
        z = c.dve_step(dve.tensor_reduce(tt[:, :, 0:i, i], prod[:, :, 0:i, 0:i], X, ALU.add))
    wait(sp, z)
    for b in range(B):
        z = s_rel.done(sp.dma_start(scr_t[b].rearrange("n h c i -> (n h) (c i)"), tt[:, b].rearrange("p c i -> p (c i)")), 16)
    wait(sp, z)
    for b in range(B):
        for h in range(H0):
            z = s_rel.done(sp.dma_start(op[32 * h:32 * h + 32, 0:NCH, b, TT, :],
                                        scr_t[b, :, h].rearrange("n c i -> c n i")), 16)
    t_in = z
    wait(pe, wf, v4_in)
    wait(act, vdone[-1])
    firb = {}
    FM = ((1, 0, 1), (2, 1, 2), (3, 3, 8))
    for n in range(NB):
        b, t0, sl = n // 2, n % 2 * BLK, slice(n * BLK, (n + 1) * BLK)
        for s, g0, ng in FM:
            k = n * 3 + s - 1
            bank = 5 + k % 3
            wait(pe, firb.get(k - 3))
            for g in range(ng):
                for h in range(H0):
                    mm = pe.matmul(ps[32 * h:32 * h + 32, bank, :], m["a0_wfir"][:, (g0 + g) * H0 + h, :],
                                   v4[:, h, b, PAD + t0 - 4 * g:PAD + t0 - 4 * g + BLK],
                                   start=g == 0, stop=g == ng - 1, skip_group_check=True)
            wait(act, PE.done(mm))
            firb[k] = AC.done(act.copy(br[:, s, sl], ps[:, bank, :]))
    f1 = PO.done(pool.tensor_scalar(br[:, 0, :], br[:, 5, :], m["a0_fw1"][:, 0:1], None, ALU.mult))

    sbuf = bt[:, 0:24 * CH].rearrange("p (k b o i) -> p k b o i", k=2, b=B, o=6)
    wt, st, uh = (bt[:, (24 + 4 * k) * CH:(28 + 4 * k) * CH].rearrange("p (k b i) -> p k b i", k=2, b=B)
                  for k in range(3))
    W_, U_, S_, O_ = 0, 1, 3, 4
    s_sb = Events(nc, "s_a0_sb", act)
    s_w = Events(nc, "s_a0_w", pe)
    s_wn = Events(nc, "s_a0_wn", act)
    s_u = Events(nc, "s_a0_u", pe)
    s_uh = Events(nc, "s_a0_uh", dve)
    s_s = Events(nc, "s_a0_s", pe)
    s_sc = Events(nc, "s_a0_sc", dve, credit=1)
    s_o = Events(nc, "s_a0_o", pe, credit=2)
    s_oc = Events(nc, "s_a0_oc", act, credit=1)

    def each():
        for b in range(B):
            for h in range(H0):
                yield b, slice(32 * h, 32 * h + 32), slice(b * CH, (b + 1) * CH)

    def fetch(n, par, src):
        s_o.wait(act, n - 2, alone=True)
        s_sb.fire(act.copy(sbuf[:, par].rearrange("p b k i -> p (b k i)"), src))

    def make_w(n, par):
        s_sb.wait(pe, n, alone=True)
        for b, hs, bs in each():
            mm = pe.matmul(ps[hs, W_, bs], sbuf[hs, par, b, KBTOK, :], sbuf[hs, par, b, TT, :],
                           start=True, stop=True, skip_group_check=True)
        s_w.fire(mm)
        s_w.wait(act, n)
        s_wn.fire(act.mul(wt[:, par].rearrange("p b i -> p (b i)"), ps[:, W_, 0:B * CH], -1.0))

    def make_u(n, par):
        for b, hs, bs in each():
            pe.matmul(ps[hs, U_ + b, 0:CH], sbuf[hs, par, b, TT, :], sbuf[hs, par, b, VBTOK, :],
                      start=True, stop=False, skip_group_check=True)

    s_am.wait(act, B * NCH // 4 - 1)
    wait(act, t_in, tok, zop, firb[NB * 3 - 1])
    wait(pe, tok, firb[NB * 3 - 1])
    s_am.wait(pe, B * NCH // 4 - 1)
    z = DVE.done(dve.memset(st[:, 1], 0.0))
    wait(pe, z)
    pe.matmul(ps[:, S_, 0:B * CH], m["a0_zero"][:], m["a0_zero"][:, 0:B * CH], start=True, stop=True, skip_group_check=True)
    fetch(0, 0, op[:, 0].rearrange("p b k i -> p (b k i)"))
    make_w(0, 0)
    make_u(0, 0)
    with nc.Fori(0, NCH // 2) as i:
        for par in range(2):
            n, nxt = i * 2 + par, 1 - par
            fetch(n + 1, nxt, op[:, bass.ds(i * 2 + par + 1, 1)].rearrange("p o b k i -> p (o b k i)"))
            s_wn.wait(pe, n, alone=True)
            s_sc.wait(pe, n - 1, alone=True)
            for b, hs, bs in each():
                mm = pe.matmul(ps[hs, U_ + b, 0:CH], wt[hs, par, b, :], st[hs, nxt, b, :],
                               start=False, stop=True, skip_group_check=True)
            s_u.fire(mm)
            s_u.wait(dve, n)
            s_uh.fire(dve.tensor_copy(uh[:, par], ps[:, U_:U_ + 2, 0:CH]))
            make_w(n + 1, nxt)
            s_uh.wait(pe, n, alone=True)
            for b, hs, bs in each():
                mm = pe.matmul(ps[hs, S_, bs], sbuf[hs, par, b, KTOK, :], uh[hs, par, b, :],
                               start=False, stop=True, skip_group_check=True)
            s_s.fire(mm)
            s_s.wait(dve, n)
            s_o.wait(dve, n - 1)
            s_sc.fire(dve.tensor_copy(st[:, par].rearrange("p b i -> p (b i)"), ps[:, S_, 0:B * CH]))
            s_oc.wait(pe, n - 1, alone=True)
            for b, hs, bs in each():
                pe.matmul(ps[hs, O_, bs], st[hs, nxt, b, :], sbuf[hs, par, b, QT, :],
                          start=True, stop=False, skip_group_check=True)
                mm = pe.matmul(ps[hs, O_, bs], uh[hs, par, b, :], sbuf[hs, par, b, AT, :],
                               start=False, stop=True, skip_group_check=True)
            s_o.fire(mm)
            s_o.wait(act, n, alone=True)
            s_oc.fire(act.copy(br[:, 4, :].rearrange("p (b t) -> p b t", b=B)[:, :, bass.ds(i * (2 * CH) + par * CH, CH)],
                                 ps[:, O_, 0:B * CH].rearrange("p (b i) -> p b i", b=B)))
            make_u(n + 1, nxt)
    s_wn.wait(pe, NCH)
    s_oc.wait(dve, NCH - 1)
    s_oc.wait(act, NCH - 1)
    s_oc.wait(pe, NCH - 1)
    s_oc.wait(pool, NCH - 1)
    wait(dve, firb[NB * 3 - 1], f1)
    wait(act, f1)
    wait(pe, f1)
    a.top = arena0
    ab = a.take([P, 2, BLK])
    sqs = a.take([P, 2, BLK])
    stt_ = a.take([P, NB, BLK])
    sqb = a.take([P, 2, BLK])
    hg = a.take([P, T])
    fu = a.take([P, T])
    tmp = a.take([P, 2, BLK])
    assert a.top - arena0 <= H0 * B * (PAD + L) + 2 * T
    cpu = {}
    k = 0
    for n in range(NB):
        sl = slice(n * BLK, (n + 1) * BLK)
        bA, bB = n % 2, 2 + n % 2
        wait(pe, cpu.get(("st", n - 2)))
        for s in range(S6):
            wait(dve, cpu.get(("pe", k - 2)))
            ma = DVE.done(dve.scalar_tensor_tensor(ab[:, k % 2, :], br[:, s, sl], -1.0, br[:, s, sl],
                                                   ALU.mult, ALU.max))
            wait(act, cpu.get(("pe", k - 2)))
            mq = AC.done(act.activation(sqs[:, k % 2, :], br[:, s, sl], ACT.Square))
            wait(pe, ma, mq)
            f = dict(start=s == 0, stop=s == S6 - 1, skip_group_check=True)
            pe.matmul(ps[0:32, bA, :], m["a0_sel"][:, s, :], br[:, s, sl], **f)
            pe.matmul(ps[32:64, bA, :], m["a0_sel"][:, s, :], ab[:, k % 2, :], **f)
            pe.matmul(ps[64:96, bA, :], m["a0_sel"][:, s, :], sqs[:, k % 2, :], **f)
            pe.matmul(ps[96:128, bA, :], m["a0_sel"][:, s, :], sqs[:, k % 2, :], **f)
            cpu[("pe", k)] = PE.done(pe.matmul(ps[96:128, bB, :], m["a0_sel"][:, s, :], br[:, s, sl], **f))
            k += 1
        done = cpu[("pe", k - 1)]
        wait(act, done, cpu.get(("st", n - 2)))
        mq = AC.done(act.activation(sqb[96:128, n % 2, :], ps[96:128, bB, :], ACT.Square, scale=float(DK) ** -0.5))
        wait(dve, done, mq)
        DVE.done(dve.tensor_scalar(stt_[0:64, n, :], ps[0:64, bA, :], 1.0 / DK, None, ALU.mult))
        DVE.done(dve.tensor_copy(stt_[64:96, n, :], ps[64:96, bA, :]))
        c.dve_step(dve.tensor_tensor(stt_[96:128, n, :], ps[96:128, bA, :], sqb[96:128, n % 2, :], ALU.subtract))
        cpu[("st", n)] = DVE.done(dve.tensor_scalar(stt_[96:128, n, :], stt_[96:128, n, :], 0.0, 1.0 / (DK - 1),
                                                    ALU.max, ALU.mult))
    wait(act, cpu[("st", NB - 1)])
    rt = AC.done(act.activation(stt_[64:128, :, :], stt_[64:128, :, :], ACT.Sqrt))
    wait(pe, rt)
    for n in range(NB):
        b, t0, sl = n // 2, n % 2 * BLK, slice(n * BLK, (n + 1) * BLK)
        bank = 4 + n % 2
        wait(pe, cpu.get(("ge", n - 2)))
        pe.matmul(ps[:, bank, :], m["a0_w1x"][:], xp[:, b, 3 + t0:3 + t0 + BLK], start=True, stop=False)
        mm = PE.done(pe.matmul(ps[:, bank, :], m["a0_w1s"][:], stt_[:, n, :], start=False, stop=True))
        wait(act, mm)
        cpu[("ge", n)] = AC.done(act.activation(hg[:, sl], ps[:, bank, :], ACT.Gelu, bias=m["a0_b1"][:, 0:1]))
        wait(pe, cpu[("ge", n)])
        for j in range(TPB):
            t = n * TPB + j
            mm = pe.matmul(ps[:, 6, t * 24:(t + 1) * 24], hg[:, t * P:(t + 1) * P], m["a0_w2"][:], start=True, stop=True)
    mm = PE.done(mm)
    g0, g1, g2 = (m["a0_tt"][:, k, :] for k in range(3))
    c.dve_step(dve.scalar_tensor_tensor(g0, m["a0_temp"][:], -1.0, m["a0_temp"][:], ALU.mult, ALU.min))
    wait(act, (DVE, DVE.n))
    e = c.act_step(act.activation(g0, g0, ACT.Exp))
    e = AC.done(act.activation(g0, g0, ACT.Ln, bias=1.0))
    wait(dve, e)
    c.dve_step(dve.tensor_scalar(g1, m["a0_temp"][:], 0.0, 0.5, ALU.max, ALU.add))
    c.dve_step(dve.tensor_tensor(g1, g1, g0, ALU.add))
    c.dve_step(dve.reciprocal(g2, g1))
    lo = m["a0_lo"]
    mh = m["a0_m"]
    lo6 = lo[:].rearrange("p t (h s) -> p (t h) s", h=H0)
    wait(dve, mm)
    c.dve_step(dve.tensor_tensor(lo[:], ps[:, 6, 0:NT * 24].rearrange("p (t k) -> p t k", k=24),
                                 m["a0_b2"][:].unsqueeze(1).broadcast_to([P, NT, 24]), ALU.add))
    lo4 = lo[:].rearrange("p t (h s) -> p t h s", h=H0)
    c.dve_step(dve.tensor_tensor(lo4, lo4, g2.unsqueeze(1).unsqueeze(3).broadcast_to([P, NT, H0, S6]), ALU.mult))
    c.dve_step(dve.tensor_reduce(mh[:], lo6, X, ALU.max))
    z = c.dve_step(dve.tensor_tensor(lo6, lo6, mh[:].unsqueeze(2).broadcast_to([P, NT * H0, S6]), ALU.subtract))
    wait(act, z)
    e = AC.done(act.activation(lo[:], lo[:], ACT.Exp))
    wait(dve, e)
    c.dve_step(dve.tensor_reduce(mh[:], lo6, X, ALU.add))
    c.dve_step(dve.reciprocal(mh[:], mh[:]))
    wts = c.dve_step(dve.tensor_tensor(lo6, lo6, mh[:].unsqueeze(2).broadcast_to([P, NT * H0, S6]), ALU.mult))
    wait(act, wts)
    spread = [AC.done(act.copy(wexp[:, t].rearrange("p s (h d) -> p s h d", h=H0),
                               lo4[:, t].rearrange("p h s -> p s h").unsqueeze(3).broadcast_to([P, S6, H0, DK])))
              for t in range(NT)]
    k = 0
    for n in range(NB):
        sl = slice(n * BLK, (n + 1) * BLK)
        for s in range(S6):
            bank = k % 6
            wait(pe, spread[n * TPB + TPB - 1], cpu.get(("mul", k - 6)))
            for j in range(TPB):
                mm = pe.transpose(ps[:, bank, j * P:(j + 1) * P], wexp[:, n * TPB + j, s, :], m["ident"][:])
            wait(dve, PE.done(mm))
            if s == 0:
                cpu[("mul", k)] = c.dve_step(dve.tensor_tensor(fu[:, sl], br[:, s, sl], ps[:, bank, :], ALU.mult))
            else:
                cpu[("mul", k)] = c.dve_step(dve.tensor_tensor(tmp[:, k % 2, :], br[:, s, sl], ps[:, bank, :], ALU.mult))
                z = c.dve_step(dve.tensor_tensor(fu[:, sl], fu[:, sl], tmp[:, k % 2, :], ALU.add))
            k += 1
        cpu[("fu", n)] = z
    for n in range(NB):
        sl = slice(n * BLK, (n + 1) * BLK)
        wait(act, cpu[("fu", n)], cpu.get(("ms", n - 2)))
        z = AC.done(act.activation(sqs[:, n % 2, :], fu[:, sl], ACT.Square))
        bank = (6, 7, 0, 1)[n]
        wait(pe, z, cpu[("fu", NB - 1)] if n > 1 else None)
        cpu[("ms", n)] = PE.done(pe.matmul(ps[:, bank, :], m["a0_heads"][:], sqs[:, n % 2, :], start=True, stop=True))
    wait(act, cpu[("ms", NB - 1)])
    for n in range(NB):
        bank = (6, 7, 0, 1)[n]
        z = AC.done(act.activation(ps[:, bank, :], ps[:, bank, :], ACT.Ln, bias=m["a0_eps"][:, 1:2], scale=1.0 / DK))
    wait(act, z)
    for n in range(NB):
        sl = slice(n * BLK, (n + 1) * BLK)
        bank = (6, 7, 0, 1)[n]
        z = AC.done(act.activation(ps[:, bank, :], ps[:, bank, :], ACT.Exp, scale=-0.5))
        wait(dve, z)
        z = DVE.done(dve.scalar_tensor_tensor(fu[:, sl], fu[:, sl], m["a0_onorm"][:, 0:1], ps[:, bank, :],
                                              ALU.mult, ALU.mult))
        bank = 2 + n % 4
        wait(pe, z)
        for j in range(TPB):
            mm = pe.matmul(ps[:, bank, j * D:(j + 1) * D], fu[:, (n * TPB + j) * P:(n * TPB + j + 1) * P],
                           m["a0_ow"][:], start=True, stop=True)
        wait(dve, PE.done(mm))
        xb = x[:, n * TPB:(n + 1) * TPB, :]
        end = DVE.done(dve.tensor_tensor(xb, xb, ps[:, bank, :].rearrange("p (t d) -> p t d", d=D), ALU.add))
    return end


def attn0_layout(a, out):
    f = np.float32
    g = lambda n: a["L0_attn_" + n]
    out["a0_w3"] = np.stack([g("q_w"), g("k_w"), g("v_w")], 1)
    out["a0_taps"] = np.stack([g(n)[:, 0, :].T for n in ("qc_w", "kc_w", "vc_w")], 0).reshape(-1)
    out["a0_bw"] = np.repeat(g("b_w"), DK, axis=1)
    w1 = g("mlp_w1")
    out["a0_w1x"] = w1[:D]
    stat = w1[D:].reshape(H0 * S6, 4, D)
    w1s = np.zeros((P, D), f)
    for q, k in enumerate((0, 2, 3, 1)):
        w1s[32 * q:32 * q + 24] = stat[:, k]
    out["a0_w1s"] = w1s
    out["a0_w2"], out["a0_b1"], out["a0_b2"] = g("mlp_w2"), g("mlp_b1")[:, None], g("mlp_b2")
    out["a0_temp"], out["a0_ow"] = g("gate_log_temp"), g("o_w")
    out["a0_onorm"] = np.tile(g("onorm_w"), H0)[:, None]
    out["a0_fw1"] = g("fir_w1")[:, 0, :]
    cols = []
    for n, groups in (("fir_w3", 1), ("fir_w7", 2), ("fir_w31", 8)):
        wt = g(n)[:, 0, ::-1]
        wt = np.concatenate([wt, np.zeros((D, 4 * groups - wt.shape[1]), f)], 1)
        cols.append(wt.reshape(H0, DK, groups, 4).transpose(3, 1, 2, 0).reshape(P, groups * H0))
    out["a0_fw"] = np.concatenate(cols, 1)
    head = np.arange(P) // DK
    out["a0_heads"] = (head[:, None] == head[None, :]).astype(f)
    sel = np.zeros((P, S6, 32), f)
    for s in range(S6):
        sel[np.arange(P), s, head * S6 + s] = 1
    out["a0_sel"] = sel
    r = np.arange(P)[:, None] % CH
    j = np.arange(CH)[None, :]
    out["a0_strict"] = np.where(j < r, f(-1), f(0))
    out["a0_incl"] = np.where(j >= r, f(1), f(0))
    out["a0_diag"] = (j == r).astype(f)
    out["a0_eye"] = np.eye(CH, dtype=f).reshape(-1)


def ffn1_memory(c, w):
    sorted_memory(c, w, 1, F)
    c.load("f1_rw", w["f1_rw"], [D, NE])
    for n in ("bo", "gamma", "beta"):
        c.load("f1_" + n, w["f1_" + n].partition_broadcast(P), [P, D])
    c.sb("e_down", [P, 1, F])
    c.sb("e_bias", [P, NE, F])


def ffn1(c, w, x, lead):
    m, dve = c.mem, c.dve
    xn, xnT, back = m["xn"], m["xnT"], m["e_back"]
    weights = Progress(c.nc, "s_f1_weights")
    for name in ("up", "down", "bias"):
        source = w["f1_" + name]
        weighted = weights.done(c.sp.dma_start(m["e_" + name][:], source.partition_broadcast(P) if name == "bias" else source), 16)
    outs = layer_norm(c, x, xn, 1e-5, lead, xnT, out_at=lambda b: xnT[:, b * BLK:(b + 1) * BLK])
    c.loaded(c.pe, c.dve)
    wait(c.pe, *outs)
    lg = c.psum[:, 2, 0:NT * NE]
    for t in range(NT):
        mm = c.pe.matmul(lg[:, t * NE:(t + 1) * NE], xnT[:, t * P:(t + 1) * P], m["f1_rw"][:], start=True, stop=True)
    placed, owned = route(c, lg, None, c.PE.done(mm), 1)
    scattered = scatter_rows(c, "s_f1_scattered", 1, placed, xn, c.sorted_x1, c.zeroed1)
    bc = lambda v, k: m[v][:].unsqueeze(1).broadcast_to([P, k, D])
    wait(dve, scattered)
    c.dve_step(dve.tensor_tensor(xn[:], xn[:], bc("f1_bo", NT), ALU.add))
    stores = expert_tiles(c, "s_f1", 1, scattered, owned, weighted, c.sorted_x1, c.sorted_y1, False)
    marks = gather_rows(c, "s_f1_back", 1, stores, c.sorted_y1, back)
    y, bn, mv, rs = xn, m["bn"], m["mv"], m["rs"]
    for n, mark in enumerate(marks):
        wait(dve, mark)
        yb = y[:, n * TPB:(n + 1) * TPB, :]
        c.dve_step(dve.tensor_tensor(yb, yb, back[:, 0, n * TPB:(n + 1) * TPB, :], ALU.add))
        for t in range(n * TPB, (n + 1) * TPB):
            z = c.DVE.done(dve.bn_stats(bn[:, t, :], y[:, t, :]))
        wait(dve, z)
        for t in range(n * TPB, (n + 1) * TPB):
            z = c.DVE.done(dve.bn_aggr(mv[:, t, :], bn[:, t, :]))
    wait(dve, z)
    z = c.DVE.done(dve.tensor_scalar(rs[:], mv[:, :, 1], 1e-12, None, ALU.add))
    wait(c.act, z)
    z = c.ACT.done(c.act.activation(rs[:], rs[:], ACT.Sqrt))
    wait(dve, z)
    c.dve_step(dve.reciprocal(rs[:], rs[:]))
    for t in range(NT):
        z = c.DVE.done(dve.tensor_scalar(y[:, t, :], y[:, t, :], mv[:, t, 0:1], rs[:, t:t + 1], ALU.subtract, ALU.mult))
    wait(dve, z)
    c.dve_step(dve.tensor_tensor(y[:], y[:], bc("f1_gamma", NT), ALU.mult))
    c.dve_step(dve.tensor_tensor(x[:], x[:], bc("f1_beta", NT), ALU.add))
    return c.DVE.done(dve.tensor_tensor(x[:], x[:], y[:], ALU.add))


def ffn1_layout(a, out):
    out["f1_rw"] = a["L1_ffn_Wr"].T
    out["f1_up"] = a["L1_ffn_W1"].transpose(1, 0, 2)
    out["f1_bias"] = a["L1_ffn_b1"]
    out["f1_down"] = a["L1_ffn_Wo"].reshape(FC, P, D).transpose(1, 0, 2).reshape(P, 1, F)
    out["f1_bo"], out["f1_gamma"], out["f1_beta"] = a["L1_ffn_bo"], a["L1_ffn_gamma"], a["L1_ffn_beta"]


def program(nc, w, x_in, out):
    c = Core(nc)
    common_memory(c, w)
    x = c.mem["x"]
    xd = x_in.rearrange("(t p) d -> p t d", p=P)
    s_io = Progress(nc, "s_io")
    end = s_io.done(c.sp.dma_start(x[:], xd), 16)
    c.loaded(c.pe)
    for memory, stage in ((attn0_memory, attn0), (ffn0_memory, ffn0), (attn1_memory, attn1), (ffn1_memory, ffn1)):
        c.arena.reset()
        memory(c, w)
        end = stage(c, w, x, (end,))
        if stage is not ffn1:
            nc.all_engine_barrier()
    wait(c.sp, end)
    end = s_io.done(c.sp.dma_start(out.rearrange("(t p) d -> p t d", p=P), x[:]), 16)
    wait(c.sp, end)


def kernel(**inputs):
    import concourse.bacc as bacc
    from concourse.bass_utils import run_bass_kernel_spmd

    nc = bacc.Bacc("TRN2", target_bir_lowering=False, num_devices=1)
    arrays = layout(inputs)
    arrays["x"] = np.ascontiguousarray(inputs["L0_attn_hidden_states"]).reshape(T, D)
    aps = {k: nc.dram_tensor("in_" + k, v.shape, mybir.dt.from_np(v.dtype), kind="ExternalInput").ap()
           for k, v in arrays.items()}
    out = nc.dram_tensor("out", (T, D), F32, kind="ExternalOutput").ap()
    program(nc, aps, aps["x"], out)
    r = run_bass_kernel_spmd(nc, [{"in_" + k: v for k, v in arrays.items()}], core_ids=[0])
    return r.results[0]["out"].reshape(B, L, D)
```

```python
import numpy as np
import concourse.bass as bass
import concourse.mybir as mybir
from concourse.alu_op_type import AluOpType as ALU

F32 = mybir.dt.float32
BF16 = mybir.dt.bfloat16
ACT = mybir.ActivationFunctionType
X = mybir.AxisListType.X

P = 128
B, L, D = 2, 1024, 128
T = B * L
NT = T // P
NTB = L // P
BLK = 512
NB = T // BLK
TPB = BLK // P


class Progress:

    def __init__(self, nc, name):
        self.sem = nc.alloc_semaphore(name)
        self.n = 0

    def done(self, instruction, by=1):
        instruction.then_inc(self.sem, by)
        self.n += by
        return (self, self.n)


class Events:

    def __init__(self, nc, name, engine, credit=0, by=1):
        self.sem, self.credit, self.by = nc.alloc_semaphore(name), credit, by
        if credit:
            engine.sem_inc(self.sem, credit * by)

    def fire(self, instruction):
        return instruction.then_inc(self.sem, self.by)

    def wait(self, engine, k, alone=False):
        engine.wait_ge(self.sem, (k + (1 + self.credit)) * self.by)
        if alone:
            engine.sem_inc(self.unread, 1)


def wait(engine, *marks):
    for mark in marks:
        if mark is not None:
            engine.wait_ge(mark[0].sem, mark[1])


class Arena:

    def __init__(self, nc, words):
        self.t, self.words, self.top = nc.alloc_sbuf_tensor("arena", [P, words], F32), words, 0

    def reset(self):
        self.top = 0

    def take(self, shape, dtype=F32):
        n = int(np.prod(shape[1:]))
        words = (n + 1) // 2 if dtype == BF16 else n
        ap = self.t[0:shape[0], self.top:self.top + words]
        self.top += words
        assert self.top <= self.words, (self.top, self.words)
        if dtype != F32:
            ap = ap.bitcast(dtype)
        names = "abcde"[:len(shape) - 1]
        if len(names) > 1:
            ap = ap.rearrange("p (" + " ".join(names) + ") -> p " + " ".join(names), **dict(zip(names, shape[1:])))
        return ap


class Core:

    def keep(self, name, shape, dtype=F32):
        self.mem[name] = self.nc.alloc_sbuf_tensor(name, shape, dtype)

    def sb(self, name, shape, dtype=F32):
        self.mem[name] = self.arena.take(shape, dtype)
        return self.mem[name]

    def load(self, name, source, shape, dtype=F32):
        self.loads.done(self.sp.dma_start(self.sb(name, shape, dtype)[:], source), 16)

    def loaded(self, *engines):
        for engine in engines:
            engine.wait_ge(self.loads.sem, self.loads.n)

    def __init__(self, nc):
        self.mem = {}
        Events.unread = nc.alloc_semaphore("s_unread")
        self.loads = Progress(nc, "s_loads")
        self.nc = nc
        self.pe, self.dve, self.act, self.pool, self.sp = nc.tensor, nc.vector, nc.scalar, nc.gpsimd, nc.sync
        self.PE, self.DVE, self.ACT, self.POOL = (Progress(nc, "s_" + n) for n in ("pe", "dve", "act", "pool"))
        self.psum = nc.alloc_psum_tensor("psum", [P, 8, BLK], F32)

    def dve_step(self, instruction):
        m = self.DVE.done(instruction)
        wait(self.dve, m)
        return m

    def act_step(self, instruction):
        m = self.ACT.done(instruction)
        wait(self.act, m)
        return m


def layer_norm(c, x, xn, eps, lead, xnT=None, banks=(6, 7), out_at=None):
    bn, mv, rs, ident = c.mem["bn"], c.mem["mv"], c.mem["rs"], c.mem["ident"]
    for t in range(NT):
        if t % TPB == 0:
            wait(c.dve, lead[t // TPB % len(lead)])
        last = c.DVE.done(c.dve.bn_stats(bn[:, t, :], x[:, t, :]))
    wait(c.dve, last)
    for t in range(NT):
        last = c.DVE.done(c.dve.bn_aggr(mv[:, t, :], bn[:, t, :]))
    wait(c.dve, last)
    ve = c.DVE.done(c.dve.tensor_scalar(rs[:], mv[:, :, 1], eps, None, ALU.add))
    wait(c.act, ve)
    root = c.ACT.done(c.act.activation(rs[:], rs[:], ACT.Sqrt))
    wait(c.dve, root)
    c.dve_step(c.dve.reciprocal(rs[:], rs[:]))
    marks = []
    for t in range(NT):
        m = c.DVE.done(c.dve.tensor_scalar(xn[:, t, :], x[:, t, :], mv[:, t, 0:1], rs[:, t:t + 1],
                                           ALU.subtract, ALU.mult))
        marks.append(m)
    if xnT is None:
        return marks
    outs = []
    for b in range(NB):
        bank = banks[b % len(banks)]
        wait(c.pe, marks[TPB * b + TPB - 1], outs[b - len(banks)] if b >= len(banks) else None)
        for j in range(TPB):
            m = c.pe.transpose(c.psum[:, bank, j * P:(j + 1) * P], xn[:, TPB * b + j, :], ident[:])
        m = c.PE.done(m)
        wait(c.act, m)
        outs.append(c.ACT.done(c.act.copy(out_at(b), c.psum[:, bank, :])))
    return outs


NE, F = 8, 512
FC = F // P
SLOTS = 4


def tiles_of(top):
    most = T * top // P + NE - 1
    return (most + SLOTS - 1) // SLOTS * SLOTS


def logits(c, weights, xnT, outs):
    lt, lg = c.mem["lt"], c.psum[:, 2, 0:NT * NE]
    copied = []
    for b, bank in enumerate((0, 1, 3, 4)):
        wait(c.pe, outs[b])
        mm = c.PE.done(c.pe.matmul(c.psum[0:NE, bank, :], weights, xnT[:, b * BLK:(b + 1) * BLK], start=True, stop=True))
        wait(c.dve, mm)
        copied.append(c.DVE.done(c.dve.tensor_copy(lt[:, b, :], c.psum[0:NE, bank, :])))
    for t in range(NT):
        if t % TPB == 0:
            wait(c.pe, copied[t // TPB])
        mm = c.pe.transpose(lg[:, t * NE:(t + 1) * NE], lt[:, t // TPB, t % TPB * P:(t % TPB + 1) * P], c.mem["ident"][0:NE, 0:NE])
    return lg, c.PE.done(mm)


def route(c, lg, bias, ready, top):
    s, dve, pe = c.mem, c.dve, c.pe
    c.DVE.done(dve.tensor_copy(s["lanes_b"][:], s["lanes"][:]))
    c.DVE.done(dve.tensor_copy(s["lower_b"][:], s["lower"][:]))
    c.DVE.done(dve.tensor_copy(s["tiles_b"][:], s["tile_index"][:]))
    for k in range(top):
        c.DVE.done(dve.tensor_copy(s["values"][:, 0:2, k * NT:(k + 1) * NT], s["number"][:]))
    lo, cmp, eq, rank, first, sel = s["lo"], s["cmp"], s["eq"], s["rank"], s["first"], s["sel"]
    wait(dve, ready)
    lgv = lg.rearrange("p (t e) -> p t e", e=NE)
    if bias is not None:
        c.dve_step(dve.tensor_tensor(lo[:], lgv, bias[:].unsqueeze(1).broadcast_to([P, NT, NE]), ALU.add))
    else:
        c.dve_step(dve.tensor_copy(lo[:], lgv))
    mine = lo[:].unsqueeze(3).broadcast_to([P, NT, NE, NE])
    other = lo[:].unsqueeze(2).broadcast_to([P, NT, NE, NE])
    c.DVE.done(dve.tensor_tensor(cmp[:], other, mine, ALU.is_gt))
    c.dve_step(dve.tensor_tensor(eq[:], other, mine, ALU.is_equal))
    lower = s["lower_b"][:].unsqueeze(1).broadcast_to([P, NT, NE * NE])
    eqf = eq[:].rearrange("p t a b -> p t (a b)")
    c.dve_step(dve.tensor_tensor(eqf, eqf, lower, ALU.mult))
    c.dve_step(dve.tensor_tensor(cmp[:], cmp[:], eq[:], ALU.add))
    c.dve_step(dve.tensor_reduce(rank[:], cmp[:], X, ALU.add))
    chosen = c.DVE.done(dve.tensor_scalar(sel[:], rank[:], float(top), None, ALU.is_lt))
    wait(pe, chosen, c.filled)
    wait(dve, c.filled)
    before, total = c.psum[:, 3, 0:NT * NE], c.psum[:, 4, 0:NT * NE]
    self_ = sel[:].rearrange("p t e -> p (t e)")
    pe.matmul(before, s["earlier"][:], self_, start=True, stop=True)
    counted = c.PE.done(pe.matmul(total, s["ones"][:], self_, start=True, stop=True))
    masks = [first]
    c.DVE.done(dve.tensor_scalar(first[:], rank[:], 0.0, None, ALU.is_equal))
    if top == 2:
        second, l1, l2, g1, g2, pick = (s[n] for n in ("second", "l1", "l2", "g1", "g2", "pick"))
        masks.append(second)
        c.dve_step(dve.tensor_scalar(second[:], rank[:], 1.0, None, ALU.is_equal))
        c.DVE.done(dve.tensor_tensor(pick[:], second[:], lo[:], ALU.mult))
        c.dve_step(dve.tensor_reduce(l1[:], lo[:], X, ALU.max))
        c.dve_step(dve.tensor_reduce(l2[:], pick[:], X, ALU.add))
        d = c.DVE.done(dve.tensor_tensor(l2[:], l2[:], l1[:], ALU.subtract))
        wait(c.act, d)
        gated = c.ACT.done(c.act.activation(l2[:], l2[:], ACT.Exp))
    wait(dve, counted)
    a, b = s["scan0"], s["scan1"]
    c.dve_step(dve.tensor_copy(a[:, NT + 1:2 * NT + 1, :], total.rearrange("p (t e) -> p t e", e=NE)))
    step = 1
    while step <= NT:
        c.dve_step(dve.tensor_tensor(b[:, NT:2 * NT + 1, :], a[:, NT:2 * NT + 1, :],
                                     a[:, NT - step:2 * NT + 1 - step, :], ALU.add))
        a, b, step = b, a, 2 * step
    count = a[:, 2 * NT, :].unsqueeze(2).broadcast_to([P, NE, NT])
    more, tiles, begin, end = s["more"], s["tiles"], s["begin"], s["end"]
    c.dve_step(dve.tensor_tensor(more[:], count, s["mult"][:].unsqueeze(1).broadcast_to([P, NE, NT]), ALU.is_gt))
    c.dve_step(dve.tensor_reduce(tiles[:], more[:], X, ALU.add))
    below = s["below"]
    c.dve_step(dve.tensor_tensor(below[:], s["lower"][:].rearrange("p (a b) -> p a b", b=NE),
                                 tiles[:].unsqueeze(1).broadcast_to([P, NE, NE]), ALU.mult))
    c.dve_step(dve.tensor_reduce(begin[:], below[:], X, ALU.add))
    c.DVE.done(dve.tensor_tensor(end[:], begin[:], tiles[:], ALU.add))
    c.dve_step(dve.tensor_scalar(begin[:], begin[:], float(P), None, ALU.mult))
    row, pick2 = s["row"], s["pick2"]
    c.dve_step(dve.tensor_tensor(row[:], a[:, NT:2 * NT, :], begin[:].unsqueeze(1).broadcast_to([P, NT, NE]), ALU.add))
    c.dve_step(dve.tensor_tensor(row[:], row[:], before.rearrange("p (t e) -> p t e", e=NE), ALU.add))
    for k, mask in enumerate(masks):
        c.DVE.done(dve.tensor_tensor(pick2[:, k], row[:], mask[:], ALU.mult))
    wait(dve, (c.DVE, c.DVE.n))
    rowf = s["rowf"]
    c.dve_step(dve.tensor_reduce(rowf[:], pick2[:], X, ALU.add))
    whole = s["whole"]
    c.dve_step(dve.tensor_copy(whole[:, 0], rowf[:]))
    c.DVE.done(dve.tensor_scalar(whole[:, 1], whole[:, 0], 7, None, ALU.logical_shift_right))
    c.dve_step(dve.tensor_scalar(whole[:, 0], whole[:, 0], P - 1, None, ALU.bitwise_and))
    c.DVE.done(dve.tensor_copy(s["tile_b"][:], whole[:, 1]))
    c.dve_step(dve.tensor_copy(s["lane_b"][:], whole[:, 0]))
    n, TC = tiles_of(top), top * NT
    flat = lambda v: v.rearrange("p k t -> p (k t)")
    values = s["values"]
    if top == 2:
        wait(dve, gated)
        g, rest = s["g"], s["rest"]
        part = lambda c0: values[:, c0, :].rearrange("p (k t) -> p k t", k=top)
        c.dve_step(dve.tensor_scalar(g1[:], l2[:], 1.0, None, ALU.add))
        c.dve_step(dve.reciprocal(g[:, 0, :], g1[:]))
        c.dve_step(dve.tensor_tensor(g[:, 1, :], g[:, 0, :], l2[:], ALU.mult))
        c.dve_step(dve.tensor_copy(part(2), g[:]))
        c.dve_step(dve.tensor_tensor(rest[:, 0], g[:], part(2), ALU.subtract))
        c.dve_step(dve.tensor_copy(part(3), rest[:, 0]))
        c.dve_step(dve.tensor_tensor(part(4), rest[:, 0], part(3), ALU.subtract))
    C = values.shape[1]
    at_lane, at_tile, carry = s["at_lane"], s["at_tile"], s["carry"]
    found = c.psum[:, 5, 0:C * n]
    step = 2 * TPB
    for q in range(0, TC, step):
        r = slice(q, q + step)
        c.DVE.done(dve.tensor_tensor(at_lane[:, r, :], flat(s["lane_b"])[:, r].unsqueeze(2).broadcast_to([P, step, P]),
                                     s["lanes_b"][:].unsqueeze(1).broadcast_to([P, step, P]), ALU.is_equal))
        c.dve_step(dve.tensor_tensor(at_tile[:, r, :], flat(s["tile_b"])[:, r].unsqueeze(2).broadcast_to([P, step, n]),
                                     s["tiles_b"][:].unsqueeze(1).broadcast_to([P, step, n]), ALU.is_equal))
        m = c.DVE.done(dve.tensor_tensor(carry[:, r], at_tile[:, r, :].unsqueeze(2).broadcast_to([P, step, C, n]),
                                         values[:, :, r].rearrange("p c k -> p k c").unsqueeze(3).broadcast_to([P, step, C, n]),
                                         ALU.mult))
        wait(pe, m)
        for k in range(q, q + step):
            m = pe.matmul(found, at_lane[:, k, :], carry[:, k].rearrange("p c n -> p (c n)"), start=k == 0, stop=k == TC - 1)
    m = c.PE.done(m)
    after, owner, expert = s["after"], s["owner"], s["expert"]
    c.dve_step(dve.tensor_tensor(after[:], s["index"][:].unsqueeze(2).broadcast_to([1, n, NE]),
                                 end[0:1, :].unsqueeze(1).broadcast_to([1, n, NE]), ALU.is_ge))
    c.dve_step(dve.tensor_reduce(owner[:], after[:], X, ALU.add))
    owned = c.DVE.done(dve.tensor_scalar(expert[:], owner[:], float(NE - 1), None, ALU.min))
    wait(dve, m)
    tok, spare, fv = s["tok"], s["to_spare"], s["found"]
    c.dve_step(dve.tensor_copy(fv[:].rearrange("p c n -> p (c n)"), found))
    if top == 2:
        c.DVE.done(dve.tensor_tensor(fv[:, 2, :], fv[:, 2, :], fv[:, 3, :], ALU.add))
    c.dve_step(dve.tensor_tensor(tok[:], fv[:, 0, :], fv[:, 1, :], ALU.add))
    if top == 2:
        c.DVE.done(dve.tensor_tensor(s["gate"][:], fv[:, 2, :], fv[:, 4, :], ALU.add))
    c.DVE.done(dve.tensor_scalar(s["source"][:], tok[:], -1.0, 0.0, ALU.add, ALU.max))
    c.dve_step(dve.scalar_tensor_tensor(spare[:], tok[:], 0.0, s["spare"][:], ALU.is_equal, ALU.mult))
    placed = c.DVE.done(dve.scalar_tensor_tensor(s["target"][:], tok[:], -1.0, spare[:], ALU.add, ALU.add))
    return placed, owned


def expert_tiles(c, name, top, placed, owned, weighted, cleared, src, dst, gated):
    ps, m = c.psum, c.mem
    pe, dve, act, pool = c.pe, c.dve, c.act, c.pool
    xs, xt, sg, h, ht, y = (m[n] for n in ("e_x", "e_xt", "e_sg", "e_h", "e_ht", "e_y"))
    wup, wdown, ident, expert = m["e_up"], m["e_down"], m["ident"], m["expert"]
    ev = lambda what, engine, credit=0, by=1: Events(c.nc, f"{name}_{what}", engine, credit, by)
    landed = [ev(f"landed{k}", pool, by=16) for k in range(SLOTS)]
    stored = [ev(f"stored{k}", pool, by=16) for k in range(SLOTS)]
    turned = ev("turned", pe)
    copied = ev("copied", dve)
    first = ev("first", pe)
    last = ev("last", pe) if gated else first
    acted = ev("acted", act)
    hidden = ev("hidden", dve)
    rows = hidden if gated else acted
    hturned = ev("hturned", pe)
    hcopied = ev("hcopied", act)
    down = ev("down", pe)
    ready = ev("ready", dve, credit=2)
    fetched = ev("fetched", dve)
    aimed = ev("aimed", dve)
    n = tiles_of(top)
    wait(pool, placed, *cleared)
    wait(pe, owned, weighted)
    wait(dve, owned, weighted, placed)
    wait(act, owned)

    def gather(t, k):
        here = m["e_from"][:, k:k + 1]
        fetched.fire(dve.tensor_copy(here, m["source"][:, bass.ds(t, 1)]))
        fetched.wait(pool, t, alone=True)
        landed[k].fire(pool.indirect_dma_start(xs[:, k, :], None, src, bass.IndirectOffsetOnAxis(ap=here, axis=0)))

    for k in range(SLOTS):
        gather(k, k)

    def expert_of(engine, t):
        return engine.value_load(expert[0:1, bass.ds(t, 1)], min_val=0, max_val=NE - 1)

    def step(turn, k):
        s = turn * SLOTS + k
        peeled = isinstance(turn, int)
        there = lambda lag: not peeled or 0 <= s - lag < n
        tile = lambda lag: (s - lag, (k - lag) % 2, (k - lag) % SLOTS, turn + (k - lag) // SLOTS)
        one = lambda ap: ap.rearrange("p a f -> p (a f)")

        def turn_x():
            landed[k].wait(pe, turn)
            turned.fire(pe.transpose(ps[:, 6, 0:P], xs[:, k, :], ident[:]))
            turned.wait(dve, s)
            copied.fire(dve.tensor_copy(xt[:, k % 2, :], ps[:, 6, 0:P]))
            if not peeled or s + SLOTS < n:
                gather(s + SLOTS, k)

        def multiply_up():
            t, p, _, _ = tile(1)
            e = expert_of(pe, t)
            copied.wait(pe, t, alone=True)
            first.fire(pe.matmul(ps[:, p, :], xt[:, p, :], one(wup[:, bass.ds(e, 1), 0:F]), start=True, stop=True))
            if gated:
                first.wait(act, t)
                acted.fire(act.activation(sg[:, p, :], ps[:, p, :], ACT.Silu))
                return e
            eb = expert_of(dve, t)
            first.wait(dve, t, alone=True)
            hidden.fire(dve.tensor_tensor(sg[:, p, :], ps[:, p, :], one(m["e_bias"][:, bass.ds(eb, 1), :]), ALU.add))
            hidden.wait(act, t)
            acted.fire(act.activation(h[:, p, :], sg[:, p, :], ACT.Gelu))

        def multiply_up_again(e):
            t, p, _, _ = tile(1)
            last.fire(pe.matmul(ps[:, 2 + p, :], xt[:, p, :], one(wup[:, bass.ds(e, 1), F:2 * F]), start=True, stop=True))
            last.wait(dve, t)
            acted.wait(dve, t)
            hidden.fire(dve.tensor_tensor(h[:, p, :], sg[:, p, :], ps[:, 2 + p, :], ALU.mult))

        def turn_hidden():
            t, p, _, _ = tile(2)
            rows.wait(pe, t)
            for f in range(FC):
                mm = pe.transpose(ps[:, 4, f * P:(f + 1) * P], h[:, p, f * P:(f + 1) * P], ident[:])
            hturned.fire(mm)
            hturned.wait(act, t)
            hcopied.fire(act.copy(ht[:], ps[:, 4, :]))

        def multiply_down():
            t, p, k3, turn3 = tile(3)
            e = bass.ds(expert_of(pe, t), 1) if gated else slice(0, 1)
            yp = ps[:, 5 + 2 * p, 0:P]
            ready.wait(pe, t - 2)
            hcopied.wait(pe, t, alone=True)
            for f in range(FC):
                mm = pe.matmul(yp, ht[:, f * P:(f + 1) * P], one(wdown[:, e, f * P:(f + 1) * P]), start=f == 0, stop=f == FC - 1)
            down.fire(mm)
            if not (peeled and turn3 == 0):
                stored[k3].wait(dve, turn3 - 1, alone=True)
            place = m["e_to"][:, k3:k3 + 1]
            aimed.fire(dve.tensor_copy(place, m["target"][:, bass.ds(t, 1)]))
            down.wait(dve, t)
            if gated:
                ready.fire(dve.tensor_scalar(y[:, k3, :], yp, m["gate"][:, bass.ds(t, 1)], None, ALU.mult))
                if not (peeled and turn3 == k3 == 0):
                    stored[(k3 - 1) % SLOTS].wait(pool, turn3 - 1 if k3 == 0 else turn3)
            else:
                ready.fire(dve.tensor_copy(y[:, k3, :], yp))
            aimed.wait(pool, t, alone=True)
            ready.wait(pool, t, alone=True)
            index = bass.IndirectOffsetOnAxis(ap=place, axis=0)
            add = dict(compute_op=ALU.add) if gated else {}
            stored[k3].fire(pool.indirect_dma_start(dst, index, y[:, k3, :], None, **add))

        e = multiply_up() if there(1) else None
        if not gated and there(0):
            turn_x()
        if there(3):
            multiply_down()
        if there(2):
            turn_hidden()
        if gated and there(0):
            turn_x()
        if gated and there(1):
            multiply_up_again(e)

    turns = n // SLOTS
    for k in range(2 * SLOTS):
        step(k // SLOTS, k % SLOTS)
    with c.nc.Fori(2, turns - 1) as i:
        for k in range(SLOTS):
            step(i, k)
    for k in range(SLOTS + 3):
        step(turns - 1 + k // SLOTS, k % SLOTS)
    return [(e, turns * 16) for e in stored]


def sorted_memory(c, w, top, up):
    n = tiles_of(top)
    for name, shape in (("lower", [P, NE * NE]), ("mult", [P, NT]), ("lanes", [P, P])):
        c.load(name, w[name].partition_broadcast(P), shape)
    c.load("tile_index", w["index"][0:n].partition_broadcast(P), [P, n])
    c.load("number", w["number"], [P, 2, NT])
    c.load("spare", w[f"spare{top}"], [P, n])
    c.load("earlier", w["earlier"], [P, P])
    c.load("index", w["index"][0:n].unsqueeze(0), [1, n])
    for name, shape in (("lo", [P, NT, NE]), ("rank", [P, NT, NE]),
                        ("first", [P, NT, NE]), ("second", [P, NT, NE]), ("sel", [P, NT, NE]), ("pick", [P, NT, NE]),
                        ("l1", [P, NT]), ("l2", [P, NT]), ("g1", [P, NT]), ("g2", [P, NT]), ("ones", [P, P]),
                        ("scan0", [P, 2 * NT + 1, NE]), ("scan1", [P, 2 * NT + 1, NE]), ("more", [P, NE, NT]),
                        ("tiles", [P, NE]), ("begin", [P, NE]), ("end", [P, NE]), ("below", [P, NE, NE]),
                        ("row", [P, NT, NE]), ("pick2", [P, top, NT, NE]), ("rowf", [P, top, NT]),
                        ("after", [1, n, NE]), ("owner", [1, n]), ("e_x", [P, SLOTS, D]), ("e_xt", [P, 2, P]),
                        ("e_sg", [P, 2, F]), ("e_h", [P, 2, F]), ("e_ht", [P, F]), ("e_y", [P, SLOTS, D]),
                        ("e_back", [P, NT, D]), ("g", [P, top, NT]),
                        ("tok", [P, n]), ("to_spare", [P, n]), ("gate", [P, n]), ("e_up", [P, NE, up])):
        c.sb(name, shape)
    c.sb("lt", [NE, NB, BLK])
    C = 5 if top == 2 else 2
    for name, shape in (("cmp", [P, NT, NE, NE]), ("eq", [P, NT, NE, NE]), ("lower_b", [P, NE * NE]), ("at_lane", [P, top * NT, P]),
                        ("at_tile", [P, top * NT, n]), ("carry", [P, top * NT, C, n]),
                        ("values", [P, C, top * NT]), ("lanes_b", [P, P]), ("tiles_b", [P, n]), ("lane_b", [P, top, NT]),
                        ("tile_b", [P, top, NT])):
        c.sb(name, shape, BF16)
    for name, shape in (("rest", [P, 2, top, NT]), ("found", [P, C, n])):
        c.sb(name, shape)
    c.sb("source", [P, n], mybir.dt.int32)
    c.sb("target", [P, n], mybir.dt.int32)
    c.sb("whole", [P, 2, top, NT], mybir.dt.int32)
    c.sb("e_from", [P, SLOTS], mybir.dt.int32)
    c.sb("e_to", [P, SLOTS], mybir.dt.int32)
    c.sb("expert", [1, n], mybir.dt.int32)
    c.POOL.done(c.pool.memset(c.mem["ones"][:], 1.0))
    for name in ("scan0", "scan1"):
        c.POOL.done(c.pool.memset(c.mem[name][:], 0.0))
    c.filled = (c.POOL, c.POOL.n)


def ffn0_memory(c, w):
    sorted_memory(c, w, 2, 2 * F)
    c.load("f0_rw", w["f0_rw"], [D, NE])
    c.load("f0_rb", w["f0_rb"].partition_broadcast(P), [P, NE])
    c.sb("e_down", [P, NE, F])


def ffn0(c, w, x, lead):
    m = c.mem
    xn, xnT, back = m["xn"], m["xnT"], m["e_back"]
    weights = Progress(c.nc, "s_f0_weights")
    for name in ("up", "down"):
        weighted = weights.done(c.sp.dma_start(m["e_" + name][:], w["f0_" + name]), 16)
    outs = layer_norm(c, x, xn, 1e-5, lead, xnT, out_at=lambda b: xnT[:, b * BLK:(b + 1) * BLK])
    normed = c.DVE.n
    c.loaded(c.pe, c.dve)
    lg, ready = logits(c, m["f0_rw"][:], xnT, outs)
    wait(c.sp, (c.DVE, normed))
    copied = Progress(c.nc, "s_f0_rows").done(c.sp.dma_start(c.rows_x[0].rearrange("(t p) d -> p t d", p=P), xn[:]), 16)
    placed, owned = route(c, lg, m["f0_rb"], ready, 2)
    stores = expert_tiles(c, "s_f0", 2, placed, owned, weighted, (c.zeroed, copied), c.rows_x[0], c.rows_y[0], True)
    for n, mark in enumerate(results(c, "s_f0_back", stores, c.rows_y[0], back)):
        wait(c.dve, mark)
        xb = x[:, n * TPB:(n + 1) * TPB, :]
        end = c.DVE.done(c.dve.tensor_tensor(xb, xb, back[:, n * TPB:(n + 1) * TPB, :], ALU.add))
    return end


def results(c, name, stored, rows, back):
    wait(c.sp, *stored)
    marks = []
    for n in range(NB):
        at = slice(n * TPB, (n + 1) * TPB)
        marks.append(Progress(c.nc, f"{name}{n}").done(
            c.sp.dma_start(back[:, at, :], rows[n * BLK:(n + 1) * BLK].rearrange("(t p) d -> p t d", p=P)), 16))
    return marks


def common_memory(c, w):
    for n, shape in (("x", [P, NT, D]), ("xn", [P, NT, D]), ("xnT", [P, T + 8]), ("bn", [P, NT, 6]),
                     ("mv", [P, NT, 2]), ("rs", [P, NT]), ("ident", [P, P])):
        c.keep(n, shape)
    c.loads.done(c.sp.dma_start(c.mem["ident"][:], w["ident"]), 16)
    c.arena = Arena(c.nc, 46200)
    c.rows_x = [c.nc.dram_tensor(f"rows_x{k}", (T, D), F32).ap() for k in range(2)]
    c.rows_y = [c.nc.dram_tensor(f"rows_y{k}", (T + n, D), F32).ap() for k, n in enumerate((P, tiles_of(1) * P))]
    c.keep("zero", [P, D])
    zero = c.POOL.done(c.pool.memset(c.mem["zero"][:], 0.0))
    wait(c.act, zero)
    zeros = Progress(c.nc, "s_zeros")
    c.zeroed = zeros.done(c.act.dma_start(c.rows_y[0].rearrange("(k p) d -> p k d", p=P),
                                          c.mem["zero"][:].unsqueeze(1).broadcast_to([P, NT + 1, D])), 16)


def layout(inputs):
    a = {k: np.asarray(v) for k, v in inputs.items()}
    out = {"ident": np.eye(P, dtype=np.float32)}
    out["lower"] = np.tril(np.ones((NE, NE), np.float32), -1).reshape(-1)
    out["earlier"] = np.triu(np.ones((P, P), np.float32), 1)
    out["mult"] = np.arange(NT, dtype=np.float32) * P
    out["lanes"] = np.arange(P, dtype=np.float32)
    lanes = np.arange(P, dtype=np.float32)[:, None]
    out["number"] = np.stack([np.repeat(lanes + 1, NT, axis=1), np.repeat(out["mult"][None], P, axis=0)], 1)
    out["spare2"] = np.repeat(lanes + T + 1, tiles_of(2), axis=1)
    out["spare1"] = lanes + T + 1 + np.arange(tiles_of(1), dtype=np.float32) * P
    out["index"] = np.arange(tiles_of(2), dtype=np.float32)
    gw = a["L0_ffn_gate_w"].transpose(2, 0, 1)
    uw = a["L0_ffn_up_w"].transpose(2, 0, 1)
    out["f0_up"] = np.concatenate([gw, uw], axis=2)
    out["f0_down"] = a["L0_ffn_down_w"].transpose(0, 2, 1).reshape(NE, FC, P, D).transpose(2, 0, 1, 3).reshape(P, NE, F)
    out["f0_rw"] = a["L0_ffn_router_w"].T
    out["f0_rb"] = a["L0_ffn_router_b"]
    attn1_layout(a, out)
    attn0_layout(a, out)
    ffn1_layout(a, out)
    return {k: np.ascontiguousarray(v) for k, v in out.items()}


NH, HD = 16, 8
NG = 4
HG = NH // NG
KR = 9 * HD
KA = KR + 3
QH = L // BLK


def attn1_memory(c, w):
    for n in ("wq", "wqs", "wk", "wks", "wv", "wo"):
        c.load("a1_" + n, w["a1_" + n], [D, D])
    c.load("a1_bcol", w["a1_bcol"], [D, 4])
    c.load("a1_bv", w["a1_bv"].partition_broadcast(P), [P, D])
    c.load("a1_bo", w["a1_bo"].partition_broadcast(P), [P, D])
    c.load("a1_cos", w["a1_cos"], [D, L]); c.load("a1_sin", w["a1_sin"], [D, L])
    c.sb("a1_t", [P, 2, 2, BLK])
    c.sb("a1_part", [P, 2, 3, BLK], BF16)
    c.sb("a1_v", [P, NT, D])
    c.sb("a1_q", [P, NG, HG, L], BF16); c.sb("a1_k", [P, NG, HG, L], BF16)
    c.sb("a1_va", [P, NTB, NH, 32])
    c.sb("a1_p", [P, 2 * HG, BLK])
    c.sb("a1_o", [P, B * NG * QH, BLK])
    c.sb("a1_mx", [P, 2, HG * 4]); c.sb("a1_mr", [P, HG * 4]); c.sb("a1_ms", [P, 3, 32], BF16)
    c.sb("a1_mt", [P, 3, 32], BF16)
    c.sb("a1_rd", [P, 2, NTB, HG])


def attn1(c, w, x, lead):
    nc, ps, m = c.nc, c.psum, c.mem
    pe, dve, act, pool, sp = c.pe, c.dve, c.act, c.pool, c.sp
    xn, xnT = m["xn"], m["xnT"]
    scr_q = nc.dram_tensor("scr_q", [NH, HD, 9, T], BF16, kind="Internal").ap()
    scr_k = nc.dram_tensor("scr_k", [NH, HD, 9, T], BF16, kind="Internal").ap()
    scr_m = nc.dram_tensor("scr_m", [2, 3, HG * 4, 4, 32], BF16, kind="Internal").ap()
    outs = layer_norm(c, x, xn, 1e-5, lead, xnT, (4, 5), out_at=lambda b: xnT[:, b * BLK:(b + 1) * BLK])
    c.loaded(c.pe, c.dve, c.act, c.pool)
    va, v = m["a1_va"], m["a1_v"]
    c.POOL.done(pool.memset(va[:], 0.0))
    wait(pool, (c.POOL, c.POOL.n))
    ones_v = c.POOL.done(pool.memset(va[:, :, :, HD:HD + 1], 1.0))
    two = float(np.frombuffer(np.array([0x3F803F80], np.uint32).tobytes(), np.float32)[0])
    kwords = m["a1_k"][64:96].rearrange("p g h t -> p (g h t)").bitcast(F32)
    wait(pool, ones_v)
    ones_k = c.POOL.done(pool.memset(kwords, two))
    wait(pool, ones_k)
    idle = c.POOL.done(pool.memset(m["a1_ms"][:], 0.0))
    s_st = [Progress(nc, f"s_a1_st{k}") for k in range(2 * B)]
    used = {}

    def project(n):
        b, what = divmod(n, 2)
        w1, w2, b1, scr = (("a1_wq", "a1_wqs", 0, scr_q), ("a1_wk", "a1_wks", 2, scr_k))[what]
        lpos, sems = (b * BLK) % L, s_st[2 * (b // 2) + what]
        bank, bank2 = ((0, 1), (2, 7))[what]
        before = used.get(n - 2, {})
        wait(pe, outs[b], before.get("t"), used.get(("v", b - 1)))
        xs = xnT[:, b * BLK:(b + 1) * BLK]
        pe.matmul(ps[:, bank, :], m[w1][:], xs, start=True, stop=True)
        mp = c.PE.done(pe.matmul(ps[:, bank2, :], m[w2][:], xs, start=True, stop=True))
        t, part = m["a1_t"][:, what], m["a1_part"][:, what]
        wait(dve, mp, before.get("split"))
        c.DVE.done(dve.scalar_tensor_tensor(t[:, 0, :], ps[:, bank, :], m["a1_bcol"][:, b1:b1 + 1],
                                            m["a1_cos"][:, lpos:lpos + BLK], ALU.add, ALU.mult))
        tt = c.dve_step(dve.scalar_tensor_tensor(t[:, 1, :], ps[:, bank2, :], m["a1_bcol"][:, b1 + 1:b1 + 2],
                                                 m["a1_sin"][:, lpos:lpos + BLK], ALU.add, ALU.mult))
        r0 = c.DVE.done(dve.tensor_tensor(t[:, 0, :], t[:, 0, :], t[:, 1, :], ALU.add))
        wait(act, r0, before.get("stored"))
        h0 = c.ACT.done(act.copy(part[:, 0, :], t[:, 0, :]))
        wait(pool, h0)
        r1 = c.POOL.done(pool.tensor_tensor(t[:, 1, :], t[:, 0, :], part[:, 0, :], ALU.subtract))
        wait(act, r1)
        h1 = c.ACT.done(act.copy(part[:, 1, :], t[:, 1, :]))
        wait(pool, h1)
        r2 = c.POOL.done(pool.tensor_tensor(part[:, 2, :], t[:, 1, :], part[:, 1, :], ALU.subtract))
        for pt in range(3):
            to = scr.rearrange("h d r t -> (h d) r t")[:, :, b * BLK:(b + 1) * BLK]
            to = to[:, 3 * pt:3 * pt + 3, :] if what == 0 else to[:, bass.ds(pt, 3, 3), :]
            wait(sp, (h0, h1, r2)[pt])
            ms = sems.done(sp.dma_start(to, part[:, pt, :].unsqueeze(1).broadcast_to([P, 3, BLK])), 16)
        used[n] = {"t": tt, "split": r2, "stored": ms}

    def project_v(b):
        wait(pe, used[2 * b]["t"])
        for j in range(TPB):
            mm = pe.matmul(ps[:, 0, j * D:(j + 1) * D], xnT[:, (b * TPB + j) * P:(b * TPB + j + 1) * P],
                           m["a1_wv"][:], start=True, stop=True)
        mm = c.PE.done(mm)
        wait(dve, mm)
        used[("v", b)] = c.DVE.done(dve.tensor_tensor(
            v[:, b * TPB:(b + 1) * TPB, :], ps[:, 0, :].rearrange("p (t d) -> p t d", d=D),
            m["a1_bv"][:].unsqueeze(1).broadcast_to([P, TPB, D]), ALU.add))

    for b in range(QH):
        project(2 * b)
        project(2 * b + 1)
        project_v(b)
    wait(sp, (s_st[0], s_st[0].n), (s_st[1], s_st[1].n))
    wait(sp, ones_k)
    wait(pe, ones_v, *outs)
    wait(dve, ones_v, idle)

    U = 2 * NTB
    s_load = [Events(nc, f"s_a1_load{k}", sp, by=32) for k in range(NG)]
    s_s1 = Events(nc, "s_a1_s1", pe)
    s_red = Events(nc, "s_a1_red", dve, credit=2)
    s_mc = Events(nc, "s_a1_mc", dve)
    s_ms = Events(nc, "s_a1_ms", sp, credit=1, by=64)
    s_mrow = [Events(nc, f"s_a1_mrow{k}", sp, credit=1, by=16) for k in range(2)]
    s_s2 = Events(nc, "s_a1_s2", pe)
    s_exp = Events(nc, "s_a1_exp", act, credit=4)
    s_va = Events(nc, "s_a1_va", pool)
    s_pv = Events(nc, "s_a1_pv", pe, credit=U + 2)
    s_o = Events(nc, "s_a1_o", act, credit=1)
    q, kk, pt, o = m["a1_q"], m["a1_k"], m["a1_p"], m["a1_o"]
    mx, mr, msp, mt = m["a1_mx"], m["a1_mr"], m["a1_ms"], m["a1_mt"]
    chain = Events(nc, "s_a1_chain", dve)
    links = [0]

    def load(bsel, g, k):
        for dst, scr in ((q, scr_q), (kk, scr_k)):
            src = scr[k * HG:(k + 1) * HG].rearrange("h d r (b t) -> b (d r) h t", b=B)[bsel]
            if not isinstance(bsel, int):
                src = src.rearrange("o r h t -> (o r) h t")
            sp.dma_start(dst[0:KR, k, :, :], src).then_inc(s_load[k].sem, 16)

    def max_tile(st, k, n, t):
        qh, h, qt = t // 16, (t % 16) // 4, t % 4
        bank = 3 + 2 * (t % 2)
        s_red.wait(pe, st * 32 + (t - 2))
        for half in range(2):
            mm = pe.matmul(ps[:, bank + half, :], q[0:KR, k, h, (qh * 4 + qt) * P:(qh * 4 + qt + 1) * P],
                           kk[0:KR, k, h, half * BLK:(half + 1) * BLK], start=True, stop=True)
        s_s1.fire(mm)
        s_s1.wait(dve, st * 32 + t)
        s_red.fire(dve.tensor_reduce(mx[:, qh, h * 4 + qt:h * 4 + qt + 1],
                                       ps[:, bank:bank + 2, :].rearrange("p a b -> p (a b)"), X, ALU.max))

    def max_rows(st, k, qh):
        e = st * 2 + qh
        s_red.wait(dve, st * 32 + (16 * qh + 15))
        n = HG * 4
        chain.fire(dve.tensor_scalar(msp[:, 0, 0:n], mx[:, qh, :], -1.0, None, ALU.mult))
        chain.wait(dve, e * 4 + 0)
        chain.fire(dve.scalar_tensor_tensor(mr[:], mx[:, qh, :], -1.0, msp[:, 0, 0:n], ALU.mult, ALU.subtract))
        chain.wait(dve, e * 4 + 1)
        chain.fire(dve.tensor_copy(msp[:, 1, 0:n], mr[:]))
        chain.wait(dve, e * 4 + 2)
        chain.fire(dve.tensor_tensor(msp[:, 2, 0:n], mr[:], msp[:, 1, 0:n], ALU.subtract))
        chain.wait(dve, e * 4 + 3)
        s_ms.wait(dve, e - 1)
        s_mc.fire(dve.transpose(mt[:].rearrange("p a b -> p (a b)"), msp[:].rearrange("p a b -> p (a b)")))
        s_mc.wait(sp, e)
        s_mrow[qh].wait(sp, st - 1)
        for r in range(4):
            sp.dma_start(scr_m[qh, :, :, r, :].rearrange("a i j -> i a j"), mt[32 * r:32 * r + n]).then_inc(s_ms.sem, 16)
        s_ms.wait(sp, e)
        s_mrow[qh].fire(sp.dma_start(q[KR:KA, k, :, qh * BLK:(qh + 1) * BLK],
                                     scr_m[qh].rearrange("a (h t) r j -> a h (t r j)", h=HG)))

    def step(st, k, i, kn, bsel2, first=False):
        k2 = (k + 2) % NG
        s_pv.wait(sp, (st - 1) * U - 1)
        load(bsel2, st, k2)
        s_pv.wait(pool, st * U - 2)
        s_va.fire(pool.tensor_copy(
            va[:, :, k * HG:(k + 1) * HG, 0:HD],
            v[:, bass.ds(i * NTB, NTB), k * HG * HD:(k + 1) * HG * HD].rearrange("p t (h d) -> p t h d", d=HD)))
        s_va.wait(pe, st)
        s_load[kn].wait(pe, i + (1 if kn == 0 else 0))
        for u in range(U + 1):
            qh, kb = divmod(u, NTB)
            if u < U:
                if u == NTB:
                    max_rows(st + 1, kn, 0)
                if kb == 0:
                    s_mrow[qh].wait(pe, st)
                for h in range(HG):
                    n = u * HG + h
                    bank = n % 3
                    s_exp.wait(pe, st * (U * HG) + (n - 3 if n else n - 1))
                    s_s2.fire(pe.matmul(ps[:, bank, :], kk[0:KA, k, h, kb * P:(kb + 1) * P],
                                          q[0:KA, k, h, qh * BLK:(qh + 1) * BLK], start=True, stop=True))
                    s_s2.wait(act, st * (U * HG) + n)
                    if h == 0:
                        s_pv.wait(act, st * U + (u - 2))
                    s_exp.fire(act.activation(pt[:, (u % 2) * HG + h, :], ps[:, bank, :], ACT.Exp,
                                                scale=float(HD) ** -0.5))
                    if h % 2 == 1:
                        t = 2 * u + h // 2
                        max_tile(st + 1, kn, 0, t)
            if u >= 1:
                uu = u - 1
                qh1, kb1 = divmod(uu, NTB)
                s_exp.wait(pe, st * (U * HG) + (uu * HG + HG - 1))
                if kb1 == 0:
                    s_o.wait(pe, st * QH + (qh1 - 1))
                for h in range(HG):
                    mm = pe.matmul(ps[32 * h:32 * h + 32, 7, :], va[:, kb1, k * HG + h, :],
                                   pt[:, (uu % 2) * HG + h, :], start=kb1 == 0, stop=kb1 == NTB - 1,
                                   skip_group_check=True)
                s_pv.fire(mm)
                if kb1 == NTB - 1:
                    s_pv.wait(act, st * U + uu, alone=True)
                    s_o.fire(act.copy(o[:, bass.ds(i * (NG * QH) + (k * QH + qh1), 1), :]
                                        .rearrange("p o q -> p (o q)"), ps[:, 7, :]))
        max_rows(st + 1, kn, 1)

    load(0, 0, 0)
    load(0, 1, 1)
    others = [lambda b=b, f=f: f(b) for b in range(QH, NB)
              for f in (lambda b: project(2 * b), lambda b: project(2 * b + 1), project_v)]
    for more in others[:4]:
        more()
    s_load[0].wait(pe, 0)
    for t in range(32):
        if t in (4, 8):
            others[3 + t // 4]()
        max_tile(0, 0, 0, t)
        if t % 16 == 15:
            max_rows(0, 0, t // 16)
    wait(pe, used[("v", NB - 1)], used[2 * NB - 1]["t"])
    wait(pool, used[("v", NB - 1)])
    biased = c.POOL.done(pool.tensor_tensor(x[:], x[:], m["a1_bo"][:].unsqueeze(1).broadcast_to([P, NT, D]), ALU.add))
    wait(sp, (s_st[2], s_st[2].n), (s_st[3], s_st[3].n))
    with nc.Fori(0, B) as i:
        for k in range(NG):
            bsel2 = bass.ds(i, 1) if k < 2 else bass.ds(i * -1 + 1, 1)
            step(i * NG + k, k, i, (k + 1) % NG, bsel2)
    G = B * NG
    for k in range(NG):
        s_load[k].wait(sp, 2 if k < 2 else 1)
    for qh in range(2):
        s_mrow[qh].wait(sp, G)
    s_o.wait(pe, G * QH - 1)
    s_red.wait(pe, (G + 1) * 32 - 1)
    s_exp.wait(pe, G * U * HG - 1)
    s_red.wait(dve, (G + 1) * 32 - 1)
    at = xn
    rd = m["a1_rd"]
    done = {}
    for n in range(G):
        b, g, k = n // NG, n % NG, n % 2
        wait(pe, done.get(n - 2))
        for j in range(NTB):
            mm = pe.transpose(ps[:, 2 * k + j // TPB, j % TPB * P:(j % TPB + 1) * P],
                              o[:, n * QH + j // TPB, j % TPB * P:(j % TPB + 1) * P], m["ident"][:])
        mm = c.PE.done(mm)
        wait(dve, mm)
        sums = ps[:, 2 * k:2 * k + 2, :].rearrange("p a b -> p (a b)").rearrange("p (t h d) -> p t h d", t=NTB, d=32)
        c.dve_step(dve.reciprocal(rd[:, k], sums[:, :, :, HD]))
        done[n] = c.DVE.done(dve.tensor_tensor(
            at[:, b * NTB:(b + 1) * NTB, g * 32:(g + 1) * 32].rearrange("p t (h d) -> p t h d", d=HD),
            sums[:, :, :, 0:HD], rd[:, k].unsqueeze(3).broadcast_to([P, NTB, HG, HD]), ALU.mult))
    turned = []
    for b in range(NB):
        wait(pe, done[(b // QH + 1) * NG - 1])
        for j in range(TPB):
            mm = pe.transpose(ps[:, 4 + b, j * P:(j + 1) * P], at[:, b * TPB + j, :], m["ident"][:])
        wait(act, c.PE.done(mm))
        turned.append(c.ACT.done(act.copy(xnT[:, b * BLK:(b + 1) * BLK], ps[:, 4 + b, :])))
    wait(pe, done[G - 1])
    wait(dve, biased)
    for b in range(NB):
        wait(pe, turned[b])
        for j in range(TPB):
            mm = pe.matmul(ps[:, b, j * D:(j + 1) * D], xnT[:, (b * TPB + j) * P:(b * TPB + j + 1) * P],
                           m["a1_wo"][:], start=True, stop=True)
        wait(dve, c.PE.done(mm))
        xb = x[:, b * TPB:(b + 1) * TPB, :]
        end = c.DVE.done(dve.tensor_tensor(xb, xb, ps[:, b, :].rearrange("p (t d) -> p t d", d=D), ALU.add))
    return end


def attn1_layout(a, out):
    swap = np.arange(D).reshape(-1, 2)[:, ::-1].reshape(-1)
    for n in ("q", "k"):
        out[f"a1_w{n}"] = a[f"L1_attn_W{n}"].T
        out[f"a1_w{n}s"] = a[f"L1_attn_W{n}"][swap].T
    out["a1_wv"] = a["L1_attn_Wv"].T
    out["a1_wo"] = a["L1_attn_Wo"].T
    bq, bk = a["L1_attn_bq"], a["L1_attn_bk"]
    out["a1_bcol"] = np.stack([bq, bq[swap], bk, bk[swap]], 1)
    out["a1_bv"], out["a1_bo"] = a["L1_attn_bv"], a["L1_attn_bo"]
    f = np.float32
    inv = (f(1.0) / f(10000.0) ** (np.arange(0, HD, 2, dtype=f) / f(HD))).astype(f)
    ang = np.repeat(np.arange(L, dtype=f)[:, None] * inv[None, :], 2, axis=1).T
    sign = np.where(np.arange(HD) % 2 == 0, f(-1), f(1))[:, None]
    out["a1_cos"] = np.tile(np.cos(ang), (NH, 1)).astype(f)
    out["a1_sin"] = np.tile(np.sin(ang) * sign, (NH, 1)).astype(f)


H0, DK = 4, 32
CH = 32
NCH = L // CH
S6 = 6
PAD = 32
QT, KTOK, AT, TT, VBTOK, KBTOK = range(6)


def attn0_memory(c, w):
    for n, shape in (("w3", [D, 3, D]), ("bw", [D, D]), ("w1x", [D, D]), ("w1s", [P, D]), ("w2", [D, 24]),
                     ("b1", [D, 1]), ("tapc", [D, 2, 4]), ("ow", [D, D]), ("onorm", [D, 1]), ("fw1", [D, 1]), ("fw", [P, 44]),
                     ("heads", [P, P]), ("sel", [P, S6, 32]), ("strict", [P, CH]), ("incl", [P, CH]), ("diag", [P, CH])):
        c.load("a0_" + n, w["a0_" + n], shape)
    c.load("a0_b2", w["a0_b2"].partition_broadcast(P), [P, 24])
    c.load("a0_temp", w["a0_temp"].partition_broadcast(P), [P, H0])
    c.load("a0_eye", w["a0_eye"].partition_broadcast(P), [P, CH * CH])
    c.sb("a0_wf", [D, 4, D])
    c.sb("a0_wfir", [P, 44, 32]); c.sb("a0_eps", [P, 2])
    c.sb("a0_tt", [P, 3, H0]); c.sb("a0_lo", [P, NT, 24]); c.sb("a0_m", [P, NT * H0])


def attn0(c, w, x, lead):
    nc, ps, m = c.nc, c.psum, c.mem
    pe, dve, act, pool, sp = c.pe, c.dve, c.act, c.pool, c.sp
    PE, DVE, AC, PO = c.PE, c.DVE, c.ACT, c.POOL
    a = c.arena
    arena0 = a.top
    u1 = a.take([P, H0 * B * (PAD + L)])
    v4 = u1.rearrange("p (g b t) -> p g b t", g=H0, b=B)
    bt = a.take([P, T])
    asub = bt.rearrange("p (b j i) -> p b j i", b=B, i=CH)
    ttf = a.take([P, B * CH * CH])
    tt = ttf.rearrange("p (b i j) -> p b i j", b=B, i=CH)
    taps = ttf[:, 0:4 * D].rearrange("p (j d) -> p j d", j=4)
    c.loads.done(sp.dma_start(ttf[:, 0:4 * D], w["a0_taps"].partition_broadcast(P)), 16)
    opf = a.take([P, (NCH + 1) * B * 6 * CH])
    op = opf.rearrange("p (n b o i) -> p n b o i", b=B, o=6, i=CH)
    wexp = opf[:, 0:NT * S6 * D].rearrange("p (t s f) -> p t s f", t=NT, s=S6)
    nz = 2 * B * (L + 3)
    z2 = opf[:, 0:nz].rearrange("p (s b t) -> p s b t", s=2, b=B)
    csum = opf[:, nz:nz + 4 * BLK].rearrange("p (k s t) -> p k s t", k=2, s=2)
    brf = a.take([P, S6 * T])
    br = brf.rearrange("p (s t) -> p s t", s=S6)
    kk = br[:, 0:3, :]
    am = brf[:, 3 * T:4 * T].rearrange("p (b n j) -> p b n j", b=B, j=CH)
    part = a.take([P, NB, BLK])
    sqf = a.take([P, 2 * BLK])
    sq = sqf.rearrange("p (k t) -> p k t", k=2)
    kbuf = sqf[:, 0:6 * P].rearrange("p (b s t) -> p b s t", b=2, s=3)
    xn, xf = m["xn"], m["xnT"]
    xp = xf[:, 0:B * (L + 3)].rearrange("p (b t) -> p b t", b=B)
    xnd = xn[:].rearrange("p t d -> p (t d)")
    scr_a = nc.dram_tensor("scr_a", [B, NCH, H0, CH, CH], F32, kind="Internal").ap()
    scr_t = nc.dram_tensor("scr_t", [B, NCH, H0, CH, CH], F32, kind="Internal").ap()

    DVE.done(dve.memset(xp[:, :, 0:3], 0.0))
    DVE.done(dve.memset(m["a0_eps"][:, 0:1], 1e-6))
    DVE.done(dve.memset(m["a0_eps"][:, 1:2], 1e-5))
    DVE.done(dve.memset(z2[:, :, :, 0:3], 0.0))
    zop = PO.done(pool.memset(op[:, NCH], 0.0))
    outs = layer_norm(c, x, xn, 1e-5, lead, xf,
                      out_at=lambda b: xp[:, b // 2, 3 + b % 2 * BLK:3 + b % 2 * BLK + BLK])
    c.loaded(pe, dve, act, pool)
    wfd = DVE.done(dve.tensor_tensor(m["a0_wf"][:], m["a0_w3"][:, 0, :].unsqueeze(1).broadcast_to([D, 4, D]),
                                     taps, ALU.mult))
    wait(pe, *outs, wfd)
    read, vdone, qk = {}, [], []
    for n in range(NB):
        b, t0, sl = n // 2, n % 2 * BLK, slice(n * BLK, (n + 1) * BLK)
        base = 4 * (n % 2)
        wait(pe, read.get(n - 2))
        here = xp[:, b, 3 + t0:3 + t0 + BLK]
        for s in (1, 2):
            mm = PE.done(pe.matmul(ps[:, base + s, :], m["a0_w3"][:, s, :], here, start=True, stop=True))
            wait(act, mm)
            z = AC.done(act.copy(z2[:, s - 1, b, 3 + t0:3 + t0 + BLK], ps[:, base + s, :]))
        wait(dve, z, read.get(n - 2))
        last = [None, None]
        for j in range(4):
            for s in range(2):
                tap, src, dst = m["a0_tapc"][:, s, j:j + 1], z2[:, s, b, t0 + j:t0 + j + BLK], csum[:, n % 2, s, :]
                wait(dve, last[s])
                last[s] = DVE.done(dve.tensor_scalar(dst, src, tap, None, ALU.mult) if j == 0 else
                                   dve.scalar_tensor_tensor(dst, src, tap, dst, ALU.mult, ALU.add))
        for j in range(4):
            mm = pe.matmul(ps[:, base, :], m["a0_wf"][:, j, :], xp[:, b, t0 + j:t0 + j + BLK], start=j == 0, stop=j == 3)
        mm = PE.done(mm)
        wait(act, mm)
        AC.done(act.activation(kk[:, 0, sl], ps[:, base, :], ACT.Silu))
        mm = PE.done(pe.matmul(ps[:, base + 3, :], m["a0_bw"][:], here, start=True, stop=True))
        wait(act, mm)
        AC.done(act.activation(bt[:, sl], ps[:, base + 3, :], ACT.Tanh, scale=0.5))
        wait(act, *last)
        AC.done(act.activation(kk[:, 1, sl], csum[:, n % 2, 0, :], ACT.Silu))
        read[n] = AC.done(act.activation(br[:, 5, sl], csum[:, n % 2, 1, :], ACT.Silu))
        vdone.append(read[n])
    wait(dve, read[NB - 1])
    c.dve_step(dve.tensor_scalar(bt[:], bt[:], 0.5, 0.5, ALU.mult, ALU.add))
    s_v4 = Progress(nc, "s_a0_v4")
    zv = PO.done(pool.memset(v4[:, :, :, 0:PAD + 4], 0.0))
    wait(sp, zv, vdone[-1])
    for j in range(4):
        for g in range(H0):
            v4_in = s_v4.done(sp.dma_start(v4[32 * j:32 * j + 32, g, :, PAD + j:PAD + L],
                                           br[32 * g:32 * g + 32, 5, :].rearrange("p (b t) -> p b t", b=B)[:, :, 0:L - j]), 16)
    wf = DVE.done(dve.tensor_tensor(
        m["a0_wfir"][:], m["a0_fw"][:].unsqueeze(2).broadcast_to([P, 44, 32]),
        m["a0_diag"][:].unsqueeze(1).broadcast_to([P, 44, 32]), ALU.mult))
    vb = DVE.done(dve.tensor_tensor(xnd, br[:, 5, :], bt[:], ALU.mult))
    banks = {}
    pair = lambda n: (1 - n // NB, n % NB, slice(n % NB * BLK, (n % NB + 1) * BLK))
    for n in range(2 * NB):
        s, _, sl = pair(n)
        wait(act, banks.get(n - 2))
        z = AC.done(act.activation(sq[:, n % 2, :], kk[:, s, sl], ACT.Square))
        wait(pe, z)
        banks[n] = PE.done(pe.matmul(ps[:, n, :], m["a0_heads"][:], sq[:, n % 2, :], start=True, stop=True))
    wait(act, banks[2 * NB - 1])
    for n in range(2 * NB):
        z = AC.done(act.activation(ps[:, n, :], ps[:, n, :], ACT.Ln, bias=m["a0_eps"][:, 0:1]))
    wait(act, z)
    for n in range(2 * NB):
        s, _, sl = pair(n)
        z = AC.done(act.activation(ps[:, n, :], ps[:, n, :], ACT.Exp, scale=-0.5))
        wait(dve, z)
        qk.append(DVE.done(dve.tensor_tensor(kk[:, s, sl], kk[:, s, sl], ps[:, n, :], ALU.mult)))
        if s == 1:
            wait(dve, qk[-1])
            kb = DVE.done(dve.tensor_tensor(kk[:, 2, sl], kk[:, 1, sl], bt[:, sl], ALU.mult))
    wait(pool, qk[-1], read[NB - 1])
    for b in range(B):
        qcopy = PO.done(pool.tensor_copy(op[:, 0:NCH, b, QT, :],
                                         kk[:, 0, b * L:(b + 1) * L].rearrange("p (n i) -> p n i", i=CH)))

    s_kbuf = Events(nc, "s_a0_kbuf", act)
    s_ap = Events(nc, "s_a0_ap", pe, credit=2)
    s_am = Events(nc, "s_a0_am", dve, credit=2)
    s_out = [Progress(nc, f"s_a0_out{b}") for b in range(B)]
    s_in = Progress(nc, "s_a0_in")
    wait(act, kb, qk[-1])
    wait(pe, qk[-1])
    wait(dve, kb, qk[-1], vb)
    GR = NCH // 4
    for b in range(B):
        with nc.Fori(0, GR // 2) as i:
            for par in range(2):
                n = i * 2 + (par + b * GR)
                s_ap.wait(act, n - 2, alone=True)
                s_kbuf.fire(act.copy(kbuf[:, par], kk[:, :, bass.ds(i * (2 * P) + (par * P + b * L), P)]))
                s_kbuf.wait(pe, n, alone=True)
                s_am.wait(pe, n - 2, alone=True)
                prods = ps[:, 2 * par, 0:8 * CH].rearrange("p (n o i) -> p n o i", o=2, i=CH)
                for cc in range(4):
                    for h in range(H0):
                        hs, cs = slice(32 * h, 32 * h + 32), slice(cc * CH, (cc + 1) * CH)
                        mm = pe.matmul(prods[hs, cc], kbuf[hs, par, 1, cs], kbuf[hs, par, 0:3:2, cs],
                                       start=True, stop=True, skip_group_check=True)
                s_ap.fire(mm)
                s_ap.wait(dve, n)
                for out, mask, dst in ((1, "a0_strict", am[:, b, bass.ds(i * 8 + par * 4, 4), :]),
                                       (0, "a0_incl", op[:, bass.ds(i * 8 + par * 4, 4), b, AT, :])):
                    z = dve.tensor_tensor(dst, prods[:, :, out, :],
                                          m[mask][:].unsqueeze(1).broadcast_to([P, 4, CH]), ALU.mult)
                s_am.fire(z)
        s_am.wait(sp, (b + 1) * GR - 1)
        for h in range(H0):
            a_out = s_out[b].done(sp.dma_start(scr_a[b, :, h].rearrange("n j i -> j n i"), am[32 * h:32 * h + 32, b]), 16)
        wait(sp, a_out)
        a_in = s_in.done(sp.dma_start(asub[:, b].rearrange("p j i -> p (j i)"),
                                      scr_a[b].rearrange("n h j i -> (n h) (j i)")), 16)
        ts = slice(b * L, (b + 1) * L)
        for item, src in ((KTOK, kk[:, 1, ts]), (KBTOK, kk[:, 2, ts]), (VBTOK, xnd[:, ts])):
            tok = DVE.done(dve.transpose(op[:, 0:NCH, b, item, :], src.rearrange("p (n i) -> p n i", i=CH)))
        if b == 0:
            eye = m["a0_eye"][:].rearrange("p (i j) -> p i j", i=CH).unsqueeze(1).broadcast_to([P, B, CH, CH])
            eye_read = DVE.done(dve.tensor_copy(tt, eye))
    wait(dve, a_in, eye_read, tok)
    s_rel = Progress(nc, "s_a0_rel")
    prod = xnd.rearrange("p (b i j) -> p b i j", b=B, i=CH)
    for i in range(1, CH):
        c.dve_step(dve.tensor_tensor(prod[:, :, 0:i, 0:i], asub[:, :, 0:i, i].unsqueeze(2).broadcast_to([P, B, i, i]),
                                     tt[:, :, 0:i, 0:i], ALU.mult))
        z = c.dve_step(dve.tensor_reduce(tt[:, :, 0:i, i], prod[:, :, 0:i, 0:i], X, ALU.add))
    wait(sp, z)
    for b in range(B):
        z = s_rel.done(sp.dma_start(scr_t[b].rearrange("n h c i -> (n h) (c i)"), tt[:, b].rearrange("p c i -> p (c i)")), 16)
    wait(sp, z)
    for b in range(B):
        for h in range(H0):
            z = s_rel.done(sp.dma_start(op[32 * h:32 * h + 32, 0:NCH, b, TT, :],
                                        scr_t[b, :, h].rearrange("n c i -> c n i")), 16)
    t_in = z
    s_ap.wait(pool, B * NCH // 4 - 1)
    wait(pool, tok, qcopy)
    f1 = PO.done(pool.tensor_scalar(br[:, 0, :], br[:, 5, :], m["a0_fw1"][:, 0:1], None, ALU.mult))
    wait(pe, wf, v4_in)
    s_am.wait(act, B * NCH // 4 - 1)
    wait(act, vdone[-1], qcopy, tok, a_out, eye_read)
    ab = m["a0_eye"][:].rearrange("p (k t) -> p k t", k=2)
    sqs = sq
    stat = {}

    def moments(k, s, n):
        xb = br[:, s, n * BLK:(n + 1) * BLK]
        wait(act, stat.get(k - 2))
        AC.done(act.activation(ab[:, k % 2, :], xb, ACT.Abs))
        stat["in", k] = AC.done(act.activation(sqs[:, k % 2, :], xb, ACT.Square))

    def statistics(k, s, n, start, stop):
        wait(pe, stat["in", k])
        for q, moving in enumerate((br[:, s, n * BLK:(n + 1) * BLK], ab[:, k % 2, :], sqs[:, k % 2, :], sqs[:, k % 2, :])):
            mm = pe.matmul(ps[32 * q:32 * q + 32, n, :], m["a0_sel"][:, s, :], moving,
                           start=start, stop=stop, skip_group_check=True)
        stat[k] = PE.done(mm)

    firb = {}
    FM = ((1, 0, 1), (2, 1, 2), (3, 3, 8))
    k = 0
    for n in range(NB + 1):
        b, t0, sl = n // 2, n % 2 * BLK, slice(n * BLK, (n + 1) * BLK)
        for i, (s, g0, ng) in enumerate(FM):
            units = [(k + u, s0) for u, s0 in enumerate(((5,), (1, 2), (3, 0))[i])] if n else []
            k += len(units)
            if i == 2:
                wait(act, f1)
            for k0, s0 in units:
                moments(k0, s0, n - 1)
            if n < NB:
                bank = 5 + (n * 3 + i) % 3
                wait(pe, firb.get(n * 3 + i - 3))
                for g in range(ng):
                    for h in range(H0):
                        mm = pe.matmul(ps[32 * h:32 * h + 32, bank, :], m["a0_wfir"][:, (g0 + g) * H0 + h, :],
                                       v4[:, h, b, PAD + t0 - 4 * g:PAD + t0 - 4 * g + BLK],
                                       start=g == 0, stop=g == ng - 1, skip_group_check=True)
                wait(act, PE.done(mm))
                firb[n * 3 + i] = AC.done(act.copy(br[:, s, sl], ps[:, bank, :]))
            for k0, s0 in units:
                statistics(k0, s0, n - 1, s0 == 5, s0 == 0)
        if n:
            wait(act, stat[k - 1])
            parts = AC.done(act.copy(part[:, n - 1, :], ps[:, n - 1, :]))

    g0, g1, g2 = (m["a0_tt"][:, k, :] for k in range(3))
    c.dve_step(dve.scalar_tensor_tensor(g0, m["a0_temp"][:], -1.0, m["a0_temp"][:], ALU.mult, ALU.min))
    wait(act, (DVE, DVE.n))
    e = c.act_step(act.activation(g0, g0, ACT.Exp))
    e = AC.done(act.activation(g0, g0, ACT.Ln, bias=1.0))
    wait(dve, e)
    c.dve_step(dve.tensor_scalar(g1, m["a0_temp"][:], 0.0, 0.5, ALU.max, ALU.add))
    c.dve_step(dve.tensor_tensor(g1, g1, g0, ALU.add))
    c.dve_step(dve.reciprocal(g2, g1))
    EYE, WT, OPS = 0, 1, 2
    sbuf = bt[:, 0:32 * CH].rearrange("p (k b o i) -> p k b o i", k=2, b=B, o=8)
    st, uh = (bt[:, (32 + 2 * k) * CH:(34 + 2 * k) * CH].rearrange("p (b i) -> p b i", b=B) for k in range(2))
    W_, SUO = 0, (1, 2)
    BS, BU, BO = (slice(k * CH, (k + 1) * CH) for k in range(3))
    s_sb = Events(nc, "s_a0_sb", act)
    s_w = Events(nc, "s_a0_w", pe)
    s_wn = Events(nc, "s_a0_wn", act)
    s_u = Events(nc, "s_a0_u", pe)
    s_uh = Events(nc, "s_a0_uh", dve)
    s_s = Events(nc, "s_a0_s", pe, credit=B)
    s_sc = Events(nc, "s_a0_sc", dve, credit=B)
    s_oc = Events(nc, "s_a0_oc", dve)
    heads = [slice(32 * h, 32 * h + 32) for h in range(H0)]

    def fetch(n, par, src):
        s_s.wait(act, n * B - 3, alone=True)
        s_sb.fire(act.copy(sbuf[:, par, :, OPS:8, :].rearrange("p b k i -> p b (k i)"), src))

    def make_w(n, par, b):
        if b == 0:
            s_sb.wait(pe, n, alone=True)
        for hs in heads:
            mm = pe.matmul(ps[hs, W_, b * CH:(b + 1) * CH], sbuf[hs, par, b, OPS + KBTOK, :], sbuf[hs, par, b, OPS + TT, :],
                           start=True, stop=True, skip_group_check=True)
        if b == B - 1:
            s_w.fire(mm)
            s_w.wait(act, n)
            s_wn.fire(act.mul(sbuf[:, par, :, WT, :], ps[:, W_, 0:B * CH].rearrange("p (b i) -> p b i", b=B), -1.0))

    def make_u(n, par, b):
        for hs in heads:
            pe.matmul(ps[hs, SUO[b], BU], sbuf[hs, par, b, OPS + VBTOK, :], sbuf[hs, par, b, OPS + TT, :],
                      start=True, stop=False, skip_group_check=True)

    s_am.wait(act, B * NCH // 4 - 1)
    wait(act, t_in, tok, zop)
    wait(pe, tok, parts)
    s_am.wait(pe, B * NCH // 4 - 1)
    wait(dve, parts)
    for n in range(NB):
        pe.matmul(ps[:, 4 + n, :], m["a0_w1x"][:], xp[:, n // 2, 3 + n % 2 * BLK:3 + n % 2 * BLK + BLK], start=True, stop=False)
    DVE.done(dve.memset(st[:], 0.0))
    z = DVE.done(dve.tensor_copy(sbuf[:, :, :, EYE, :].rearrange("p k b i -> p (k b) i"),
                                 m["a0_diag"][:].unsqueeze(1).broadcast_to([P, 2 * B, CH])))
    wait(pe, z)
    wait(act, z)
    s_sb.fire(act.copy(sbuf[:, 0, :, OPS:8, :].rearrange("p b k i -> p b (k i)"), op[:, 0].rearrange("p b k i -> p b (k i)")))
    for b in range(B):
        make_w(0, 0, b)
    for b in range(B):
        make_u(0, 0, b)
    with nc.Fori(0, NCH // 2) as i:
        for par in range(2):
            n, nxt = i * 2 + par, 1 - par
            fetch(n + 1, nxt, op[:, bass.ds(i * 2 + par + 1, 1)].rearrange("p o b k i -> p (o b) (k i)"))
            s_wn.wait(pe, n, alone=True)
            for b in range(B):
                s_sc.wait(pe, (n - 1) * B + b, alone=True)
                for hs in heads:
                    mm = pe.matmul(ps[hs, SUO[b], 0:3 * CH], st[hs, b, :], sbuf[hs, par, b, EYE:EYE + 3, :],
                                   start=False, stop=False, skip_group_check=True)
                s_u.fire(mm)
                s_u.wait(dve, n * B + b)
                s_uh.fire(dve.transpose(uh[:, b, :], ps[:, SUO[b], BU]))
            make_w(n + 1, nxt, 0)
            for b in range(B):
                s_uh.wait(pe, n * B + b, alone=True)
                so = ps[:, SUO[b], 0:3 * CH].rearrange("p (o i) -> p o i", o=3)[:, 0:3:2, :]
                for hs in heads:
                    mm = pe.matmul(so[hs], uh[hs, b, :], sbuf[hs, par, b, OPS + KTOK:OPS + AT + 1, :],
                                   start=False, stop=True, skip_group_check=True)
                s_s.fire(mm)
                s_s.wait(dve, n * B + b)
                s_sc.fire(dve.transpose(st[:, b, :], ps[:, SUO[b], BS]))
                s_oc.fire(dve.tensor_copy(br[:, 4, :].rearrange("p (b t) -> p b t", b=B)[:, b, bass.ds(i * (2 * CH) + par * CH, CH)],
                                          ps[:, SUO[b], BO]))
            make_w(n + 1, nxt, 1)
            for b in range(B):
                s_oc.wait(pe, n * B + b, alone=True)
                make_u(n + 1, nxt, b)
    s_wn.wait(pe, NCH)
    s_oc.wait(dve, B * NCH - 1)
    s_oc.wait(act, B * NCH - 1)
    s_oc.wait(pe, B * NCH - 1)
    s_oc.wait(pool, B * NCH - 1)
    wait(dve, parts, f1)
    a.top = arena0
    raw = a.take([P, 2, BLK])
    stt_ = a.take([P, NB, BLK])
    sqb = a.take([P, 2, BLK])
    fu = a.take([P, T])
    tmpf = a.take([P, 2 * 5 * BLK])
    tmp = tmpf.rearrange("p (k s t) -> p k s t", k=2, s=5)
    hg = tmpf[:, 0:T]
    assert a.top - arena0 <= H0 * B * (PAD + L) + 2 * T
    cpu = {}
    moments(k, 4, 0)
    for n in range(NB):
        if n + 1 < NB:
            moments(k + 1, 4, n + 1)
        statistics(k, 4, n, True, True)
        done = stat[k]
        k += 1
        wait(dve, done, cpu.get(("sq", n - 2)))
        full = raw[:, n % 2]
        z = c.dve_step(dve.tensor_tensor(full, ps[:, n, :], part[:, n, :], ALU.add))
        wait(act, z, cpu.get(("st", n - 2)))
        cpu[("sq", n)] = mq = AC.done(act.activation(sqb[96:128, n % 2, :], full[0:32], ACT.Square, scale=float(DK) ** -0.5))
        DVE.done(dve.tensor_scalar(stt_[0:64, n, :], full[0:64], 1.0 / DK, None, ALU.mult))
        DVE.done(dve.tensor_copy(stt_[64:96, n, :], full[64:96]))
        wait(dve, mq)
        c.dve_step(dve.tensor_tensor(stt_[96:128, n, :], full[96:128], sqb[96:128, n % 2, :], ALU.subtract))
        cpu[("st", n)] = DVE.done(dve.tensor_scalar(stt_[96:128, n, :], stt_[96:128, n, :], 0.0, 1.0 / (DK - 1),
                                                    ALU.max, ALU.mult))
    wait(act, cpu[("st", NB - 1)])
    rt = AC.done(act.activation(stt_[64:128, :, :], stt_[64:128, :, :], ACT.Sqrt))
    wait(pe, rt)
    for n in range(NB):
        sl, bank = slice(n * BLK, (n + 1) * BLK), 4 + n
        mm = PE.done(pe.matmul(ps[:, bank, :], m["a0_w1s"][:], stt_[:, n, :], start=False, stop=True))
        wait(act, mm)
        cpu[("ge", n)] = AC.done(act.activation(hg[:, sl], ps[:, bank, :], ACT.Gelu, bias=m["a0_b1"][:, 0:1]))
    for n in range(NB):
        wait(pe, cpu[("ge", n)])
        for t in range(n * TPB, (n + 1) * TPB):
            mm = pe.matmul(ps[:, 0, t * 24:(t + 1) * 24], hg[:, t * P:(t + 1) * P], m["a0_w2"][:], start=True, stop=True)
    mm = PE.done(mm)
    lo = m["a0_lo"]
    mh = m["a0_m"]
    lo6 = lo[:].rearrange("p t (h s) -> p (t h) s", h=H0)
    wait(dve, mm)
    c.dve_step(dve.tensor_tensor(lo[:], ps[:, 0, 0:NT * 24].rearrange("p (t k) -> p t k", k=24),
                                 m["a0_b2"][:].unsqueeze(1).broadcast_to([P, NT, 24]), ALU.add))
    lo4 = lo[:].rearrange("p t (h s) -> p t h s", h=H0)
    c.dve_step(dve.tensor_tensor(lo4, lo4, g2.unsqueeze(1).unsqueeze(3).broadcast_to([P, NT, H0, S6]), ALU.mult))
    c.dve_step(dve.tensor_reduce(mh[:], lo6, X, ALU.max))
    z = c.dve_step(dve.tensor_tensor(lo6, lo6, mh[:].unsqueeze(2).broadcast_to([P, NT * H0, S6]), ALU.subtract))
    wait(act, z)
    e = AC.done(act.activation(lo[:], lo[:], ACT.Exp))
    wait(dve, e)
    c.dve_step(dve.tensor_reduce(mh[:], lo6, X, ALU.add))
    c.dve_step(dve.reciprocal(mh[:], mh[:]))
    wts = c.dve_step(dve.tensor_tensor(lo6, lo6, mh[:].unsqueeze(2).broadcast_to([P, NT * H0, S6]), ALU.mult))
    wait(act, wts)
    spread = []
    for t in range(NT):
        to = wexp[:, t].rearrange("p s (h d) -> p s h d", h=H0)
        weights = lo4[:, t].rearrange("p h s -> p s h").unsqueeze(3).broadcast_to([P, S6, H0, DK])
        spread.append(DVE.done(dve.tensor_copy(to, weights)) if t in (1, 3) else AC.done(act.copy(to, weights)))
    k, half = 0, None

    def sum_up(n, left, right):
        sl = slice(n * BLK, (n + 1) * BLK)
        wait(dve, left, right)
        z = DVE.done(dve.tensor_tensor(fu[:, sl], fu[:, sl], tmp[:, n % 2, 1, :], ALU.add))
        wait(act, z, cpu.get(("ms", n - 2)))
        cpu[("fu2", n)] = AC.done(act.activation(sqs[:, n % 2, :], fu[:, sl], ACT.Square))

    def mean_square(n):
        wait(pe, cpu[("fu2", n)])
        cpu[("ms", n)] = PE.done(pe.matmul(ps[:, 4 + n, :], m["a0_heads"][:], sqs[:, n % 2, :], start=True, stop=True))
        wait(act, cpu[("ms", n)])
        return AC.done(act.activation(ps[:, 4 + n, :], ps[:, 4 + n, :], ACT.Ln, bias=m["a0_eps"][:, 1:2], scale=1.0 / DK))

    for n in range(NB):
        sl, t = slice(n * BLK, (n + 1) * BLK), tmp[:, n % 2]
        mul = []
        for s in range(S6):
            bank = k % 4
            wait(pe, spread[n * TPB + TPB - 2], spread[n * TPB + TPB - 1], cpu.get(("mul", k - 4)))
            for j in range(TPB):
                mm = pe.transpose(ps[:, bank, j * P:(j + 1) * P], wexp[:, n * TPB + j, s, :], m["ident"][:])
            wait(dve, PE.done(mm))
            to = fu[:, sl] if s == 0 else t[:, s - 1, :]
            mul.append(DVE.done(dve.tensor_tensor(to, br[:, s, sl], ps[:, bank, :], ALU.mult)))
            cpu[("mul", k)] = mul[-1]
            if s == 2:
                wait(dve, mul[1])
                half_v = DVE.done(dve.tensor_tensor(fu[:, sl], fu[:, sl], t[:, 0, :], ALU.add))
            if s == 3:
                wait(pool, mul[3])
                PO.done(pool.tensor_tensor(t[:, 1, :], t[:, 1, :], t[:, 2, :], ALU.add))
            if s == 1 and n > 1:
                mean_square(n - 2)
            if s == 4 and half:
                sum_up(n - 1, *half)
            k += 1
        eng, prog = (pool, PO) if n < NB - 1 else (dve, DVE)
        for s in (4, 5):
            wait(eng, mul[s], (PO, PO.n), (DVE, DVE.n) if eng is dve else None)
            prog.done(eng.tensor_tensor(t[:, 1, :], t[:, 1, :], t[:, s - 1, :], ALU.add))
        half = (half_v, (prog, prog.n))
    mean_square(NB - 2)
    sum_up(NB - 1, *half)
    z = mean_square(NB - 1)
    wait(act, z)
    scaled = []
    for n in range(NB):
        sl = slice(n * BLK, (n + 1) * BLK)
        bank = 4 + n
        z = AC.done(act.activation(ps[:, bank, :], ps[:, bank, :], ACT.Exp, scale=-0.5))
        wait(dve, z)
        scaled.append(DVE.done(dve.scalar_tensor_tensor(fu[:, sl], fu[:, sl], m["a0_onorm"][:, 0:1], ps[:, bank, :],
                                                        ALU.mult, ALU.mult)))
    for n in range(NB):
        bank = n
        wait(pe, scaled[n])
        for j in range(TPB):
            mm = pe.matmul(ps[:, bank, j * D:(j + 1) * D], fu[:, (n * TPB + j) * P:(n * TPB + j + 1) * P],
                           m["a0_ow"][:], start=True, stop=True)
        wait(dve, PE.done(mm))
        xb = x[:, n * TPB:(n + 1) * TPB, :]
        end = DVE.done(dve.tensor_tensor(xb, xb, ps[:, bank, :].rearrange("p (t d) -> p t d", d=D), ALU.add))
    return end


def attn0_layout(a, out):
    f = np.float32
    g = lambda n: a["L0_attn_" + n]
    out["a0_w3"] = np.stack([g("q_w"), g("k_w"), g("v_w")], 1)
    out["a0_taps"] = g("qc_w")[:, 0, :].T.reshape(-1)
    out["a0_tapc"] = np.stack([g("kc_w")[:, 0, :], g("vc_w")[:, 0, :]], 1)
    out["a0_bw"] = np.repeat(g("b_w"), DK, axis=1)
    w1 = g("mlp_w1")
    out["a0_w1x"] = w1[:D]
    stat = w1[D:].reshape(H0 * S6, 4, D)
    w1s = np.zeros((P, D), f)
    for q, k in enumerate((0, 2, 3, 1)):
        w1s[32 * q:32 * q + 24] = stat[:, k]
    out["a0_w1s"] = w1s
    out["a0_w2"], out["a0_b1"], out["a0_b2"] = g("mlp_w2"), g("mlp_b1")[:, None], g("mlp_b2")
    out["a0_temp"], out["a0_ow"] = g("gate_log_temp"), g("o_w")
    out["a0_onorm"] = np.tile(g("onorm_w"), H0)[:, None]
    out["a0_fw1"] = g("fir_w1")[:, 0, :]
    cols = []
    for n, groups in (("fir_w3", 1), ("fir_w7", 2), ("fir_w31", 8)):
        wt = g(n)[:, 0, ::-1]
        wt = np.concatenate([wt, np.zeros((D, 4 * groups - wt.shape[1]), f)], 1)
        cols.append(wt.reshape(H0, DK, groups, 4).transpose(3, 1, 2, 0).reshape(P, groups * H0))
    out["a0_fw"] = np.concatenate(cols, 1)
    head = np.arange(P) // DK
    out["a0_heads"] = (head[:, None] == head[None, :]).astype(f)
    sel = np.zeros((P, S6, 32), f)
    for s in range(S6):
        sel[np.arange(P), s, head * S6 + s] = 1
    out["a0_sel"] = sel
    r = np.arange(P)[:, None] % CH
    j = np.arange(CH)[None, :]
    out["a0_strict"] = np.where(j > r, f(-1), f(0))
    out["a0_incl"] = np.where(j >= r, f(1), f(0))
    out["a0_diag"] = (j == r).astype(f)
    out["a0_eye"] = np.eye(CH, dtype=f).reshape(-1)


def ffn1_memory(c, w):
    sorted_memory(c, w, 1, F)
    c.load("f1_rw", w["f1_rw"], [D, NE])
    for n in ("bo", "gamma", "beta"):
        c.load("f1_" + n, w["f1_" + n].partition_broadcast(P), [P, D])
    c.sb("e_down", [P, 1, F])
    c.sb("f1_off", [P, NT])
    c.sb("e_bias", [P, NE, F])


def ffn1(c, w, x, lead):
    m, dve = c.mem, c.dve
    xn, xnT, back = m["xn"], m["xnT"], m["e_back"]
    weights = Progress(c.nc, "s_f1_weights")
    for name in ("up", "down", "bias"):
        source = w["f1_" + name]
        weighted = weights.done(c.sp.dma_start(m["e_" + name][:], source.partition_broadcast(P) if name == "bias" else source), 16)
    outs = layer_norm(c, x, xn, 1e-5, lead, xnT, out_at=lambda b: xnT[:, b * BLK:(b + 1) * BLK])
    normed = c.DVE.n
    c.loaded(c.pe, c.dve)
    lg, ready = logits(c, m["f1_rw"][:], xnT, outs)
    wait(c.sp, (c.DVE, normed))
    copied = Progress(c.nc, "s_f1_rows").done(c.sp.dma_start(c.rows_x[1].rearrange("(t p) d -> p t d", p=P), xn[:]), 16)
    placed, owned = route(c, lg, None, ready, 1)
    bc = lambda v, k: m[v][:].unsqueeze(1).broadcast_to([P, k, D])
    wait(dve, copied)
    c.dve_step(dve.tensor_tensor(xn[:], xn[:], bc("f1_bo", NT), ALU.add))
    stores = expert_tiles(c, "s_f1", 1, placed, owned, weighted, (copied,), c.rows_x[1], c.rows_y[1], False)
    marks = results(c, "s_f1_back", stores, c.rows_y[1], back)
    y, bn, mv, rs, off = xn, m["bn"], m["mv"], m["rs"], m["f1_off"]
    c.dve_step(dve.tensor_tensor(x[:], x[:], bc("f1_beta", NT), ALU.add))
    for n, mark in enumerate(marks):
        wait(dve, mark)
        yb = y[:, n * TPB:(n + 1) * TPB, :]
        c.dve_step(dve.tensor_tensor(yb, yb, back[:, n * TPB:(n + 1) * TPB, :], ALU.add))
        for t in range(n * TPB, (n + 1) * TPB):
            z = c.DVE.done(dve.bn_stats(bn[:, t, :], y[:, t, :]))
        wait(dve, z)
        for t in range(n * TPB, (n + 1) * TPB):
            z = c.DVE.done(dve.bn_aggr(mv[:, t, :], bn[:, t, :]))
    wait(dve, z)
    z = c.DVE.done(dve.tensor_scalar(rs[:], mv[:, :, 1], 1e-12, None, ALU.add))
    wait(c.act, z)
    z = c.ACT.done(c.act.activation(rs[:], rs[:], ACT.Sqrt))
    wait(dve, z)
    c.dve_step(dve.reciprocal(rs[:], rs[:]))
    z = c.DVE.done(dve.scalar_tensor_tensor(off[:], mv[:, :, 0], -1.0, rs[:], ALU.mult, ALU.mult))
    wait(c.act, z)
    ends = []
    for t in range(NT):
        z = c.ACT.done(c.act.activation(back[:, t, :], y[:, t, :], ACT.Identity, scale=rs[:, t:t + 1], bias=off[:, t:t + 1]))
        if t % TPB == TPB - 1:
            at = slice(t - TPB + 1, t + 1)
            wait(dve, z)
            c.dve_step(dve.tensor_tensor(back[:, at, :], back[:, at, :], bc("f1_gamma", TPB), ALU.mult))
            ends.append(c.DVE.done(dve.tensor_tensor(x[:, at, :], x[:, at, :], back[:, at, :], ALU.add)))
    return ends


def ffn1_layout(a, out):
    out["f1_rw"] = a["L1_ffn_Wr"].T
    out["f1_up"] = a["L1_ffn_W1"].transpose(1, 0, 2)
    out["f1_bias"] = a["L1_ffn_b1"]
    out["f1_down"] = a["L1_ffn_Wo"].reshape(FC, P, D).transpose(1, 0, 2).reshape(P, 1, F)
    out["f1_bo"], out["f1_gamma"], out["f1_beta"] = a["L1_ffn_bo"], a["L1_ffn_gamma"], a["L1_ffn_beta"]


def program(nc, w, x_in, out):
    c = Core(nc)
    common_memory(c, w)
    x = c.mem["x"]
    block = lambda dram, n: dram.rearrange("(t p) d -> p t d", p=P)[:, n * TPB:(n + 1) * TPB, :]
    end = [Progress(nc, f"s_x{n}").done(c.sp.dma_start(x[:, n * TPB:(n + 1) * TPB, :], block(x_in, n)), 16)
           for n in range(NB)]
    c.loaded(c.pe)
    for memory, stage in ((attn0_memory, attn0), (ffn0_memory, ffn0), (attn1_memory, attn1), (ffn1_memory, ffn1)):
        c.arena.reset()
        memory(c, w)
        end = stage(c, w, x, end)
        if stage is not ffn1:
            nc.all_engine_barrier()
            end = [end]
    s_out = Progress(nc, "s_out")
    for n in range(NB):
        wait(c.sp, end[n])
        landed = s_out.done(c.sp.dma_start(block(out, n), x[:, n * TPB:(n + 1) * TPB, :]), 16)
    wait(c.sp, landed)


def kernel(**inputs):
    import concourse.bacc as bacc
    from concourse.bass_utils import run_bass_kernel_spmd

    nc = bacc.Bacc("TRN2", target_bir_lowering=False, num_devices=1)
    arrays = layout(inputs)
    arrays["x"] = np.ascontiguousarray(inputs["L0_attn_hidden_states"]).reshape(T, D)
    aps = {k: nc.dram_tensor("in_" + k, v.shape, mybir.dt.from_np(v.dtype), kind="ExternalInput").ap()
           for k, v in arrays.items()}
    out = nc.dram_tensor("out", (T, D), F32, kind="ExternalOutput").ap()
    program(nc, aps, aps["x"], out)
    r = run_bass_kernel_spmd(nc, [{"in_" + k: v for k, v in arrays.items()}], core_ids=[0])
    return r.results[0]["out"].reshape(B, L, D)
```
